# Optimizing a Trainium2 kernel written in Bass

```python
import numpy as np
import jax
import jax.numpy as jnp

def _softmax(x, axis=-1):
    return jax.nn.softmax(x, axis=axis)

def _gelu(x):
    return jax.nn.gelu(x, approximate=True)

def _silu(x):
    return jax.nn.silu(x)

def _sigmoid(x):
    return jax.nn.sigmoid(x)

def _layernorm(x, axis=-1, eps=1e-05):
    m = jnp.mean(x, axis=axis, keepdims=True)
    v = jnp.var(x, axis=axis, keepdims=True)
    return (x - m) / jnp.sqrt(v + eps)

def _scatter_add(tgt, idx, src, axis=0):
    return tgt.at[idx].add(src)

def _segment_sum(src, seg, n):
    return jax.ops.segment_sum(src, seg, n)
kernel_name = 'mk_gnn_resnorm_d2_gnn_r64_720a10'

def setup_inputs(seed: int=0):
    np.random.seed(seed)
    _w = jnp.asarray

    def _rec_inputs():
        import jax
        import jax.numpy as jnp
        _gk = jax.random.key(seed)
        x = -0.000202 + 1 * jax.random.normal(jax.random.fold_in(_gk, 1), (100000, 64), jnp.float32)
        src = jax.random.randint(jax.random.fold_in(_gk, 2), (25000,), 0, 100000, jnp.int32)
        dst = jnp.minimum((100000 * jax.random.uniform(jax.random.fold_in(_gk, 3), (25000,)) ** 2.0).astype(jnp.int32), 99999)
        _o = jnp.argsort(dst, stable=True)
        src = src[_o]
        dst = dst[_o]
        edge_attr_16 = 0.000196303 + 1.00016 * jax.random.normal(jax.random.fold_in(_gk, 12), (25000, 16), jnp.float32)
        return (x, src, dst, edge_attr_16)
    x, src, dst, edge_attr_16 = _rec_inputs()

    def _L0_gnn_setup():
        import jax, jax.numpy as jnp
        import numpy as np
        N = 100000
        E = 25000
        H = 64
        EF = 16
        EPS = 1e-05

        def _layer_norm(x, gamma, beta):
            mu = jnp.mean(x, axis=-1, keepdims=True)
            var = jnp.mean(jnp.square(x - mu), axis=-1, keepdims=True)
            return (x - mu) * jax.lax.rsqrt(var + EPS) * gamma + beta
        key = jax.random.key(seed)
        ks = jax.random.split(key, 12)
        s = 0.05
        return {'node_features': jax.random.normal(ks[0], (N, H), jnp.float32), 'edge_index': jax.random.randint(ks[1], (2, E), 0, N, dtype=jnp.int64), 'edge_features': jax.random.normal(ks[2], (E, EF), jnp.float32), 'W_m1': jax.random.normal(ks[3], (2 * H + EF, H), jnp.float32) * s, 'b_m1': jnp.zeros((H,), jnp.float32), 'W_m2': jax.random.normal(ks[4], (H, H), jnp.float32) * s, 'b_m2': jnp.zeros((H,), jnp.float32), 'W_u1': jax.random.normal(ks[5], (2 * H, H), jnp.float32) * s, 'b_u1': jnp.zeros((H,), jnp.float32), 'W_u2': jax.random.normal(ks[6], (H, H), jnp.float32) * s, 'b_u2': jnp.zeros((H,), jnp.float32), 'gamma': jnp.ones((H,), jnp.float32), 'beta': jnp.zeros((H,), jnp.float32)}
    _L0_gnn_all = _L0_gnn_setup()
    _L0_gnn_in = {k: v for k, v in _L0_gnn_all.items() if k in ('W_m1', 'b_m1', 'W_m2', 'b_m2', 'W_u1', 'b_u1', 'W_u2', 'b_u2', 'gamma', 'beta')}
    del _L0_gnn_all

    def _L1_gnn_setup():
        import jax, jax.numpy as jnp
        import numpy as np
        N_NODES = 100000
        N_EDGES = 25000
        IN_F, HID_F, OUT_F = (64, 64, 64)
        key = jax.random.key(seed)
        ks = jax.random.split(key, 9)
        return {'x': jax.random.normal(ks[0], (N_NODES, IN_F), dtype=jnp.float32), 'src': jax.random.randint(ks[1], (N_EDGES,), 0, N_NODES, dtype=jnp.int64), 'dst': jax.random.randint(ks[2], (N_EDGES,), 0, N_NODES, dtype=jnp.int64), 'W_self1': jax.random.normal(ks[3], (IN_F, HID_F), dtype=jnp.float32) * (1.0 / np.sqrt(IN_F)), 'W_neigh1': jax.random.normal(ks[4], (IN_F, HID_F), dtype=jnp.float32) * (1.0 / np.sqrt(IN_F)), 'b1': jnp.zeros((HID_F,), dtype=jnp.float32), 'W_self2': jax.random.normal(ks[5], (HID_F, OUT_F), dtype=jnp.float32) * (1.0 / np.sqrt(HID_F)), 'W_neigh2': jax.random.normal(ks[6], (HID_F, OUT_F), dtype=jnp.float32) * (1.0 / np.sqrt(HID_F)), 'b2': jnp.zeros((OUT_F,), dtype=jnp.float32)}
    _L1_gnn_all = _L1_gnn_setup()
    _L1_gnn_in = {k: v for k, v in _L1_gnn_all.items() if k in ('W_self1', 'W_neigh1', 'b1', 'W_self2', 'W_neigh2', 'b2')}
    del _L1_gnn_all
    return {'x': x, 'src': src, 'dst': dst, 'edge_attr_16': edge_attr_16, 'L0_gnn_W_m1': _L0_gnn_in['W_m1'], 'L0_gnn_b_m1': _L0_gnn_in['b_m1'], 'L0_gnn_W_m2': _L0_gnn_in['W_m2'], 'L0_gnn_b_m2': _L0_gnn_in['b_m2'], 'L0_gnn_W_u1': _L0_gnn_in['W_u1'], 'L0_gnn_b_u1': _L0_gnn_in['b_u1'], 'L0_gnn_W_u2': _L0_gnn_in['W_u2'], 'L0_gnn_b_u2': _L0_gnn_in['b_u2'], 'L0_gnn_gamma': _L0_gnn_in['gamma'], 'L0_gnn_beta': _L0_gnn_in['beta'], 'L1_gnn_W_self1': _L1_gnn_in['W_self1'], 'L1_gnn_W_neigh1': _L1_gnn_in['W_neigh1'], 'L1_gnn_b1': _L1_gnn_in['b1'], 'L1_gnn_W_self2': _L1_gnn_in['W_self2'], 'L1_gnn_W_neigh2': _L1_gnn_in['W_neigh2'], 'L1_gnn_b2': _L1_gnn_in['b2']}

def reference(x, src, dst, edge_attr_16, L0_gnn_W_m1, L0_gnn_b_m1, L0_gnn_W_m2, L0_gnn_b_m2, L0_gnn_W_u1, L0_gnn_b_u1, L0_gnn_W_u2, L0_gnn_b_u2, L0_gnn_gamma, L0_gnn_beta, L1_gnn_W_self1, L1_gnn_W_neigh1, L1_gnn_b1, L1_gnn_W_self2, L1_gnn_W_neigh2, L1_gnn_b2):
    import jax
    import jax.numpy as jnp

    def _L0_gnn_ref(node_features, edge_index, edge_features, W_m1, b_m1, W_m2, b_m2, W_u1, b_u1, W_u2, b_u2, gamma, beta):
        import jax, jax.numpy as jnp
        import numpy as np
        N = 100000
        E = 25000
        H = 64
        EF = 16
        EPS = 1e-05

        def _layer_norm(x, gamma, beta):
            mu = jnp.mean(x, axis=-1, keepdims=True)
            var = jnp.mean(jnp.square(x - mu), axis=-1, keepdims=True)
            return (x - mu) * jax.lax.rsqrt(var + EPS) * gamma + beta
        src_idx = edge_index[0]
        dst_idx = edge_index[1]
        h_src = node_features[src_idx]
        h_dst = node_features[dst_idx]
        msg_in = jnp.concatenate([h_dst, h_src, edge_features], axis=1)
        messages = jax.nn.relu(msg_in @ W_m1 + b_m1) @ W_m2 + b_m2
        aggregated = jax.ops.segment_sum(messages, dst_idx, num_segments=node_features.shape[0])
        upd_in = jnp.concatenate([node_features, aggregated], axis=1)
        updated = jax.nn.relu(upd_in @ W_u1 + b_u1) @ W_u2 + b_u2
        return _layer_norm(node_features + updated, gamma, beta)

    def _L1_gnn_ref(x, src, dst, W_self1, W_neigh1, b1, W_self2, W_neigh2, b2):
        import jax, jax.numpy as jnp
        import numpy as np
        N_NODES = 100000
        N_EDGES = 25000
        IN_F, HID_F, OUT_F = (64, 64, 64)
        N = x.shape[0]
        deg = jax.ops.segment_sum(jnp.ones(dst.shape, dtype=x.dtype), dst, num_segments=N)
        inv_deg = jnp.where(deg > 0, 1.0 / jnp.maximum(deg, 1.0), 0.0)[:, None]

        def sage_conv(h, W_s, W_n, b):
            agg = jax.ops.segment_sum(h[src], dst, num_segments=N) * inv_deg
            return h @ W_s + agg @ W_n + b
        h = jax.nn.relu(sage_conv(x, W_self1, W_neigh1, b1))
        return sage_conv(h, W_self2, W_neigh2, b2)
    edge_index = jnp.stack([src, dst])
    x = _layernorm(x + _L0_gnn_ref(x, edge_index, edge_attr_16, L0_gnn_W_m1, L0_gnn_b_m1, L0_gnn_W_m2, L0_gnn_b_m2, L0_gnn_W_u1, L0_gnn_b_u1, L0_gnn_W_u2, L0_gnn_b_u2, L0_gnn_gamma, L0_gnn_beta), axis=-1)
    x = _layernorm(x + _L1_gnn_ref(x, src, dst, L1_gnn_W_self1, L1_gnn_W_neigh1, L1_gnn_b1, L1_gnn_W_self2, L1_gnn_W_neigh2, L1_gnn_b2), axis=-1)
    return x

_drawn_inputs = setup_inputs


def setup_inputs(seed=0):
    import zlib

    import numpy as np

    out = dict(_drawn_inputs(seed))
    spreads = {'L0_gnn_b_m1': (0.0, 2.0),
     'L0_gnn_b_m2': (0.0, 2.0),
     'L0_gnn_b_u1': (0.0, 0.546),
     'L0_gnn_b_u2': (0.0, 0.1),
     'L0_gnn_gamma': (1.0, 0.2),
     'L0_gnn_beta': (0.0, 0.1),
     'L1_gnn_b1': (0.0, 0.1),
     'L1_gnn_b2': (0.0, 0.1)}
    factors = {'edge_attr_16': 8.0, 'L0_gnn_W_m1': 8.0, 'L0_gnn_W_m2': 8.0}
    for name, (base, spread) in spreads.items():
        noise = np.random.default_rng([zlib.crc32(name.encode()), seed]).standard_normal(out[name].shape)
        drawn = base * np.exp(spread * noise) if base else spread * noise
        out[name] = jnp.asarray(drawn.astype(out[name].dtype))
    for name, factor in factors.items():
        out[name] = (out[name] * factor).astype(out[name].dtype)
    return out
```

```python
from contextlib import ExitStack

import concourse.bass as bass
from concourse import mybir

P = 128
H = 64
EPS = 1e-5
BANK = 512
RING = 4
UNROLL = 4

ALU = mybir.AluOpType
ACT = mybir.ActivationFunctionType
F32 = mybir.dt.float32
BF16 = mybir.dt.bfloat16
I32 = mybir.dt.int32
AX_X = mybir.AxisListType.X


class Step:

    def __init__(self, eng, k, base, kept):
        self.eng, self.k, self.base, self.kept = eng, k, base, kept

    def back(self, n):
        return Step(self.eng, self.k, self.base - n, self.kept)

    def value(self, per_step, plus):
        add = per_step * self.base + plus
        if self.k is None:
            return max(add, 0)
        key = (per_step, add)
        if key not in self.kept:
            self.kept[key] = self.eng.snap(self.k * (per_step * UNROLL) + add)
        return self.kept[key]

    def done(self, lag=0, each=1, ring=1):
        add = each * ((self.base - lag) // ring + 1)
        if self.k is None:
            return max(add, 0)
        key = (each, ring, add)
        if key not in self.kept:
            self.kept[key] = self.eng.snap(self.k * (each * UNROLL // ring) + add)
        return self.kept[key]

    def slot(self, ring):
        return self.base % ring


def all_steps(eng, first, count, body, peel=1, last=None):
    assert (count - peel) % UNROLL == 0
    loops = (count - peel) // UNROLL - (1 if last else 0)
    for i in range(peel):
        body(Step(eng, None, first + i, {}))
    with eng.Fori(0, loops) as k:
        kept = {}
        for i in range(UNROLL):
            body(Step(eng, k, first + peel + i, kept))
    if last:
        for i in range(count - UNROLL, count - 1):
            body(Step(eng, None, first + i, {}))
        last(Step(eng, None, first + count - 1, {}))


def build_gnn(nc, x, src, dst, edge_attr, W_m1, b_m1, W_m2, b_m2, W_u1, b_u1, W_u2, b_u2, gamma, beta,
              W_self1, W_neigh1, b_1, W_self2, W_neigh2, b_2, out):
    N = x.shape[0]
    E = src.shape[0]
    EF = edge_attr.shape[1]
    TC = 4
    EC = TC * P
    NCH = -(-E // EC)
    EP = NCH * EC
    NT = EP // P
    TA = NT // 2
    DC = 8 * P
    ND = 2 * NCH
    OVER = ND * DC - N
    assert 0 <= OVER < DC and NT % 2 == 0 and TA <= P and E % 100 == 0
    NTP = NT + 2 * TC
    NOWHERE = 1 << 20
    assert N < NOWHERE

    def scratch(name, shape, dt):
        return nc.dram_tensor(name, shape, dt, kind="Internal").ap()

    dst_line = scratch("dst_line", (EP + 2,), I32)
    src_line = scratch("src_line", (EP,), I32)
    ea_rows = scratch("ea_rows", (EP, EF), F32)
    same_line = scratch("same_line", (EP,), F32)
    inv_line = scratch("inv_line", (EP,), F32)
    row_of_node = scratch("row_of_node", (N, 1), I32)
    x1_rows = scratch("x1_rows", (2 * EP, H), F32)
    h1_rows = scratch("h1_rows", (2 * EP, H), F32)

    with ExitStack() as ctx:
        def sb(name, shape, dt=F32):
            return ctx.enter_context(nc.sbuf_tensor(name, shape, dt))

        def sem(name):
            return ctx.enter_context(nc.semaphore(name))

        def sems(name, n):
            return [sem(f"{name}{i}") for i in range(n)]

        def bank(name):
            return ctx.enter_context(nc.psum_tensor(name, [P, BANK], F32))

        psF0, psF1 = bank("psF0"), bank("psF1")
        psB0, psB1 = bank("psB0"), bank("psB1")
        psM0, psM1 = bank("psM0"), bank("psM1")
        psN = [bank("psN0"), bank("psN1")]

        ident = sb("ident", [P, P])
        bd_c = sb("bd_c", [P, P])
        bd_u1 = sb("bd_u1", [P, P])
        bd_u2 = sb("bd_u2", [P, P])
        bd_s1 = sb("bd_s1", [P, P])
        bd_s2 = sb("bd_s2", [P, P])
        w_m1 = sb("w_m1", [P, H])
        w_m1e = sb("w_m1e", [TC * EF, TC, H])
        w_m2 = sb("w_m2", [H + 1, H])
        w_u1a = sb("w_u1a", [H, P])
        w_n1 = sb("w_n1", [H, P])
        w_l2 = sb("w_l2", [P, H])
        cen = sb("cen", [P, 6, H])
        cmean = sb("cmean", [P, 6])
        bm1_c = sb("bm1_c", [H, 1])
        bu1_c = sb("bu1_c", [P, 1])
        b1_c = sb("b1_c", [P, 1])
        eps_c = sb("eps_c", [P, 1])
        gam = sb("gam", [P, H])
        brow = sb("brow", [96, 4, H])
        brest = sb("brest", [96, 4, H])
        bpart = sb("bpart", [96, 4, H], BF16)
        bmid = sb("bmid", [96, 4, H], BF16)
        bias3 = sb("bias3", [96, 4, BANK], BF16)
        pick = sb("pick", [96, P], BF16)
        ones_r = sb("ones_r", [1, EC])

        raw = sb("raw", [TA, 4, 2, P], I32)
        rowf = sb("rowf", [TA, 4, 2, P])
        notlast = sb("notlast", [TA, 2, P])
        edges = sb("edges", [P, 4, NTP], I32)
        SRC, DSTG, SIDX, ENUM = range(4)
        rows2 = sb("rows2", [P, NTP], I32)
        fill = sb("fill", [P, N // 80], I32)
        zpad = sb("zpad", [P, 16], I32)

        xd = sb("xd", [P, 2, BANK])
        f_xT, f_U, f_sT = sb("f_xT", [P, BANK]), sb("f_U", [P, BANK]), sb("f_sT", [P, BANK])
        f_sq, f_y, f_yg, f_s = (sb(n, [P, BANK]) for n in ("f_sq", "f_y", "f_yg", "f_s"))
        f_x1 = sb("f_x1", [P, 2, BANK])
        f_var, f_std, f_rstd = (sb(n, [P, 2, 8]) for n in ("f_var", "f_std", "f_rstd"))
        g_xT, g_h, g_r, g_sq = (sb(n, [P, BANK]) for n in ("g_xT", "g_h", "g_r", "g_sq"))
        g_out = sb("g_out", [P, 2, BANK])
        g_var, g_std, g_rstd = (sb(n, [P, 8]) for n in ("g_var", "g_std", "g_rstd"))

        er = sb("er", [P, RING, BANK])
        ea = sb("ea", [P, 2, TC * EF])
        same = sb("same", [H, 2, EC])
        inv = sb("inv", [H, 2, EC])
        m_xT = sb("m_xT", [P, 2, BANK])
        m_eaT = sb("m_eaT", [TC * EF, P])
        m_hid = sb("m_hid", [H + 1, EC])
        m_agg = sb("m_agg", [H, 2, EC])
        m_cnt = sb("m_cnt", [1, 2, EC])
        m_inv = sb("m_inv", [1, 2, EC])
        n_U, n_sT, n_sq, n_y, n_yg, n_s = (sb(n, [P, BANK]) for n in ("n_U", "n_sT", "n_sq", "n_y", "n_yg", "n_s"))
        n_x1 = sb("n_x1", [P, 2, BANK])
        n_var, n_std, n_rstd = (sb(n, [P, 2, 8]) for n in ("n_var", "n_std", "n_rstd"))
        ix1 = sb("ix1", [P, RING, 4, TC], I32)
        ix2 = sb("ix2", [P, RING, 4, TC], I32)
        ix3 = sb("ix3", [P, RING, 2, TC], I32)
        slots = sb("slots", [P, 2, TC], I32)
        absent = sb("absent", [P, TC])
        away = sb("away", [P, TC])
        rowix = sb("rowix", [P, RING, TC], I32)
        q_T, q_mean = sb("q_T", [P, BANK]), sb("q_mean", [H, EC])
        q_h = sb("q_h", [P, 2, BANK])
        t_T = sb("t_T", [P, BANK])
        t_x1 = sb("t_x1", [P, RING, TC * H])
        t_r, t_sq = sb("t_r", [P, TC * H]), sb("t_sq", [P, TC * H])
        t_var, t_std, t_rstd = (sb(n, [P, TC]) for n in ("t_var", "t_std", "t_rstd"))
        t_out = sb("t_out", [P, RING, TC * H])

        weights_in, biases_in, lines_in, pads_in = sem("weights_in"), sem("biases_in"), sem("lines_in"), sem("pads_in")
        raw_in, same_out, fill_out = sem("raw_in"), sem("same_out"), sem("fill_out")
        pool_consts, zeroed, setup_dve = sem("pool_consts"), sem("zeroed"), sem("setup_dve")
        rowf_ready, edgesT, edges_ready = sem("rowf_ready"), sem("edgesT"), sem("edges_ready")
        pads_ready, fill_ready = sem("pads_ready"), sem("fill_ready")

        lines_cleared, pool_cleared = sem("lines_cleared"), sem("pool_cleared")

        xd_in = sems("xd_in", 2)
        f_xT_ps, f_xT_sb, f_u_ps, f_U_sb, f_r_ps, f_sq1, f_var1, f_std1, f_rstd1 = map(
            sem, "f_xT_ps f_xT_sb f_u_ps f_U_sb f_r_ps f_sq1 f_var1 f_std1 f_rstd1".split())
        f_y_sb, f_yg_sb, f_s_sb, f_sT_ps, f_sT_sb, f_sc_ps, f_sq2, f_var2, f_std2, f_rstd2, f_x1_sb = map(
            sem, "f_y_sb f_yg_sb f_s_sb f_sT_ps f_sT_sb f_sc_ps f_sq2 f_var2 f_std2 f_rstd2 f_x1_sb".split())
        g_xT_ps, g_xT_sb, g_h_ps, g_h_sb, g_o_ps, g_r_sb, g_sq_sb, g_var_sb, g_std_sb, g_rstd_sb, g_out_sb = map(
            sem, "g_xT_ps g_xT_sb g_h_ps g_h_sb g_o_ps g_r_sb g_sq_sb g_var_sb g_std_sb g_rstd_sb g_out_sb".split())
        out_stored = sems("out_stored", 2)

        er_in = sems("er_in", RING)
        ix1_ready, ends_in = sem("ix1_ready"), sems("ends_in", 2)
        rows_set = sems("rows_set", RING)
        m_T_ps, m_xT_sb, m_eaT_sb, m_hid_ps, m_hid_sb, m_msg_ps, m_agg_sb, m_cnt_sb, m_inv_sb, m_u_ps = map(
            sem, "m_T_ps m_xT_sb m_eaT_sb m_hid_ps m_hid_sb m_msg_ps m_agg_sb m_cnt_sb m_inv_sb m_u_ps".split())
        inv_stored = sems("inv_stored", 2)
        n_U_sb, n_r_ps, n_sq1, n_var1, n_std1, n_rstd1, n_y_sb, n_yg_sb, n_s_sb = map(
            sem, "n_U_sb n_r_ps n_sq1 n_var1 n_std1 n_rstd1 n_y_sb n_yg_sb n_s_sb".split())
        n_sT_ps, n_sT_sb, n_sc_ps, n_sq2, n_var2, n_std2, n_rstd2, n_x1_sb = map(
            sem, "n_sT_ps n_sT_sb n_sc_ps n_sq2 n_var2 n_std2 n_rstd2 n_x1_sb".split())
        x1_stored = sems("x1_stored", 2)

        ix2_ready, absent_sb, away_sb, rowix_ready = map(sem, "ix2_ready absent_sb away_sb rowix_ready".split())
        slots_in = sems("slots_in", 2)
        q_er_in, q_x1_in, q_line_in = sems("q_er_in", RING), sems("q_x1_in", RING), sems("q_line_in", 2)
        q_T_ps, q_T_sb, q_agg_sb, q_mean_sb, q_h_ps, q_h_sb = map(
            sem, "q_T_ps q_T_sb q_agg_sb q_mean_sb q_h_ps q_h_sb".split())
        h1_stored = sems("h1_stored", 2)

        ix3_ready = sem("ix3_ready")
        t_er_in, t_h1_in, t_line_in = sems("t_er_in", RING), sems("t_h1_in", RING), sems("t_line_in", 2)
        t_T_ps, t_T_sb, t_agg_sb, t_mean_sb, t_o_ps, t_r_sb, t_sq_sb, t_var_sb, t_std_sb, t_rstd_sb, t_out_sb = map(
            sem, "t_T_ps t_T_sb t_agg_sb t_mean_sb t_o_ps t_r_sb t_sq_sb t_var_sb t_std_sb t_rstd_sb t_out_sb".split())
        rows_scattered = sems("rows_scattered", RING)

        def tiles(ap):
            return ap.rearrange("p (t f) -> p t f", f=H)

        def halves(ap):
            return ap.rearrange("p (t h f) -> p t h f", h=2, f=H)

        def per_row(ap, n):
            return ap.unsqueeze(2).to_broadcast([P, n, H])

        def one_line(ap):
            return ap.rearrange("(a n) -> a n", a=1)

        col = lambda v: v.rearrange("(n a) -> n a", a=1)

        block = ctx.enter_context(nc.Block())

        @block.sync
        def _(sp):
            ab = dict(b=100)
            sp.dma_start(dst_line[1:E + 1].rearrange("(b n) -> b n", **ab), dst.rearrange("(b n) -> b n", **ab)).then_inc(lines_in, 16)
            sp.dma_start(src_line[0:E].rearrange("(b n) -> b n", **ab), src.rearrange("(b n) -> b n", **ab)).then_inc(lines_in, 16)
            sp.dma_start(ea_rows[0:E, :].rearrange("(b n) f -> b (n f)", **ab), edge_attr.rearrange("(b n) f -> b (n f)", **ab)).then_inc(lines_in, 16)
            sp.wait_ge(pads_ready, 3)
            NP_ = EP - E
            sp.dma_start(one_line(dst_line[0:1]), zpad[0:1, 1:2]).then_inc(pads_in, 16)
            sp.dma_start(dst_line[E + 1:EP + 2].rearrange("(n a) -> n a", a=1), zpad[0:NP_ + 1, 1:2]).then_inc(pads_in, 16)
            sp.dma_start(src_line[E:EP].rearrange("(n a) -> n a", a=1), zpad[0:NP_, 0:1]).then_inc(pads_in, 16)
            sp.dma_start(ea_rows[E:EP, :], fill[0:NP_, 0:EF].bitcast(F32)).then_inc(pads_in, 16)
            sp.wait_ge(lines_in, 48)
            sp.wait_ge(pads_in, 64)
            line = lambda ap: ap.rearrange("(a q p) -> q a p", a=2, p=P)
            for n, s in enumerate((src_line[0:EP], dst_line[1:EP + 1], dst_line[0:EP], dst_line[2:EP + 2])):
                sp.dma_start(raw[:, n], line(s)).then_inc(raw_in, 16)
            sp.wait_ge(zeroed, 1)
            for lo in (0, H):
                sp.dma_start(bd_u1[lo:lo + H, lo:lo + H], W_u1[0:H, :]).then_inc(weights_in, 16)
                sp.dma_start(bd_s1[lo:lo + H, lo:lo + H], W_self1).then_inc(weights_in, 16)
                sp.dma_start(cen[lo:lo + H, 0], W_u2).then_inc(weights_in, 16)
                sp.dma_start(cen[lo:lo + H, 1], W_self2).then_inc(weights_in, 16)
                sp.dma_start(bu1_c[lo:lo + H, :], col(b_u1)).then_inc(weights_in, 16)
                sp.dma_start(b1_c[lo:lo + H, :], col(b_1)).then_inc(weights_in, 16)
            sp.dma_start(cen[0:H, 2], W_neigh2).then_inc(weights_in, 16)
            sp.dma_start(cen[H:P, 2], W_self2).then_inc(weights_in, 16)
            for n, v in enumerate((b_u2, beta, b_2)):
                sp.dma_start(cen[:, 3 + n], v.partition_broadcast(P)).then_inc(weights_in, 16)
            sp.dma_start(brow[:, 2], b_1.partition_broadcast(96)).then_inc(weights_in, 16)
            sp.dma_start(gam[:, :], gamma.partition_broadcast(P)).then_inc(weights_in, 16)
            sp.dma_start(w_m1[0:H, :], W_m1[H:2 * H, :]).then_inc(weights_in, 16)
            sp.dma_start(w_m1[H:P, :], W_m1[0:H, :]).then_inc(weights_in, 16)
            for t in range(TC):
                sp.dma_start(w_m1e[EF * t:EF * (t + 1), t], W_m1[2 * H:2 * H + EF, :]).then_inc(weights_in, 16)
            sp.dma_start(w_m2[0:H, :], W_m2).then_inc(weights_in, 16)
            sp.dma_start(w_m2[H:H + 1, :], one_line(b_m2)).then_inc(weights_in, 16)
            sp.dma_start(w_u1a[:, H:P], W_u1[H:2 * H, :]).then_inc(weights_in, 16)
            sp.dma_start(w_n1[:, H:P], W_neigh1).then_inc(weights_in, 16)
            sp.dma_start(bm1_c[:, :], col(b_m1)).then_inc(weights_in, 16)
            sp.wait_ge(fill_ready, 1)
            sp.dma_start(row_of_node.rearrange("(b n) a -> b (n a)", b=80), fill[0:80, :]).then_inc(fill_out, 16)
            sp.wait_ge(rowf_ready, 1)
            sp.dma_start(line(same_line), rowf[:, 3]).then_inc(same_out, 16)
            sp.wait_ge(same_out, 16)

            def dense_rows(dram, s, late):
                at = s.value(DC, -OVER if late else 0)
                return dram[bass.ds(at, DC), :].rearrange("(p t) f -> p (t f)", p=P)

            def edge_rows(dram, c, base):
                return dram[bass.ds(c.value(EC, base), EC), :].rearrange("(t p) f -> p t f", p=P)

            def load_dense(s, late):
                at = dense_rows(x, s, late)
                sp.wait_ge(f_s_sb, s.done(2))
                sp.dma_start(xd[:, s.slot(2)], at).then_inc(xd_in[s.slot(2)], 16)

            def load_edge(c):
                at, line_at = edge_rows(ea_rows, c, 0), one_line(same_line)[:, bass.ds(c.value(EC, 0), EC)].rearrange("a n -> (a n)")
                sp.wait_ge(m_agg_sb, c.done(2))
                sp.dma_start(ea[:, c.slot(2)].rearrange("p (t f) -> p t f", f=EF), at).then_inc(ends_in[c.slot(2)], 16)
                sp.dma_start(same[:, c.slot(2)], line_at.partition_broadcast(H)).then_inc(ends_in[c.slot(2)], 16)

            def store_dense(s, late):
                at = dense_rows(out, s, late)
                sp.wait_ge(g_out_sb, s.done())
                sp.dma_start(at, g_out[:, s.slot(2)]).then_inc(out_stored[s.slot(2)], 16)

            def store_inv(c):
                at = one_line(inv_line)[:, bass.ds(c.value(EC, 0), EC)]
                sp.wait_ge(m_inv_sb, c.done())
                sp.dma_start(at, m_inv[:, c.slot(2)]).then_inc(inv_stored[c.slot(2)], 16)

            def store_x1(c):
                at_d, at_s = edge_rows(x1_rows, c, 0), edge_rows(x1_rows, c, EP)
                v = halves(n_x1[:, c.slot(2)])
                sp.wait_ge(n_x1_sb, c.done())
                sp.dma_start(at_s, v[:, :, 0]).then_inc(x1_stored[c.slot(2)], 16)
                sp.dma_start(at_d, v[:, :, 1]).then_inc(x1_stored[c.slot(2)], 16)

            load_dense(Step(sp, None, 0, {}), False)
            load_edge(Step(sp, None, 0, {}))

            def phase1(s, last=False):
                nxt = s.back(-1)
                if not last:
                    load_dense(nxt, False)
                    load_edge(nxt)
                if s.base > 0:
                    store_x1(s.back(1))
                    store_dense(s.back(1), False)
                store_inv(s)

            all_steps(sp, 0, NCH, phase1, peel=1 + UNROLL, last=lambda s: phase1(s, True))
            load_dense(Step(sp, None, NCH, {}), True)
            store_x1(Step(sp, None, NCH - 1, {}))
            for q in range(2):
                uses = (NCH + 1 - q) // 2
                sp.wait_ge(x1_stored[q], 32 * uses)
                sp.wait_ge(inv_stored[q], 16 * uses)

            def load_lines(c, into, agg_done):
                same_at = one_line(same_line)[:, bass.ds(c.value(EC, 0), EC)].rearrange("a n -> (a n)")
                inv_at = one_line(inv_line)[:, bass.ds(c.value(EC, 0), EC)].rearrange("a n -> (a n)")
                sp.wait_ge(agg_done, c.done(2))
                sp.sem_inc(lines_cleared, 1)
                sp.dma_start(same[:, c.slot(2)], same_at.partition_broadcast(H)).then_inc(into[c.slot(2)], 16)
                sp.dma_start(inv[:, c.slot(2)], inv_at.partition_broadcast(H)).then_inc(into[c.slot(2)], 16)

            def load_x1(c):
                at = edge_rows(x1_rows, c, 0)
                sp.wait_ge(q_T_ps, c.done(RING))
                sp.dma_start(halves(er[:, c.slot(RING)])[:, :, 1], at).then_inc(q_x1_in[c.slot(RING)], 16)

            def store_h1(c):
                at_d, at_s = edge_rows(h1_rows, c, 0), edge_rows(h1_rows, c, EP)
                v = halves(q_h[:, c.slot(2)])
                sp.wait_ge(q_h_sb, c.done())
                sp.dma_start(at_s, v[:, :, 0]).then_inc(h1_stored[c.slot(2)], 16)
                sp.dma_start(at_d, v[:, :, 1]).then_inc(h1_stored[c.slot(2)], 16)

            sp.wait_ge(n_s_sb, NCH)
            load_x1(Step(sp, None, 0, {}))
            load_lines(Step(sp, None, 0, {}), q_line_in, q_mean_sb)

            def phase2(c, last=False):
                s = c.back(-NCH)
                if not last:
                    load_dense(s.back(-1), True)
                    load_x1(c.back(-1))
                    load_lines(c.back(-1), q_line_in, q_mean_sb)
                if c.base == 0:
                    store_dense(s.back(1), False)
                    sp.wait_ge(out_stored[(NCH - 1) % 2], 16 * ((NCH - 1) // 2 + 1))
                else:
                    store_dense(s.back(1), True)
                store_h1(c)

            all_steps(sp, 0, NCH, phase2, peel=1 + UNROLL, last=lambda c: phase2(c, True))
            for q in range(2):
                sp.wait_ge(h1_stored[q], 32 * ((NCH + 1 - q) // 2))

            def load_h1(c):
                at, x1_at = edge_rows(h1_rows, c, 0), edge_rows(x1_rows, c, 0)
                sp.wait_ge(t_T_ps, c.done(RING))
                sp.dma_start(halves(er[:, c.slot(RING)])[:, :, 1], at).then_inc(t_h1_in[c.slot(RING)], 16)
                sp.wait_ge(t_r_sb, c.done(RING))
                sp.dma_start(tiles(t_x1[:, c.slot(RING)]), x1_at).then_inc(t_h1_in[c.slot(RING)], 16)

            load_h1(Step(sp, None, 0, {}))
            load_lines(Step(sp, None, 0, {}), t_line_in, t_mean_sb)
            store_dense(Step(sp, None, ND - 1, {}), True)

            def phase3(c):
                load_h1(c.back(-1))
                load_lines(c.back(-1), t_line_in, t_mean_sb)

            all_steps(sp, 0, NCH, phase3, peel=1 + UNROLL, last=lambda c: None)

        @block.gpsimd
        def _(pool):
            nc.gpsimd.memset(zpad[:, 0:1], 0).then_inc(pads_ready, 1)
            nc.gpsimd.memset(zpad[:, 1:2], -1).then_inc(pads_ready, 1)
            nc.gpsimd.memset(ident[:, :], 0.0).then_inc(pool_consts, 1)
            pool.wait_ge(pool_consts, 1)
            nc.gpsimd.affine_select(out=ident[:, :], in_=ident[:, :], compare_op=ALU.not_equal, fill=1.0, base=0,
                                    pattern=[[-1, P]], channel_multiplier=1).then_inc(pool_consts, 1)
            nc.gpsimd.iota(edges[:, ENUM, :], pattern=[[P, NTP]], base=0, channel_multiplier=1).then_inc(pool_consts, 1)

            bound_of = {n: pool.to_reg(n) for n in (N - 1, 2 * EP - 1)}

            def gather(into, table, index, bound, s):
                pool.indirect_dma_start(into, None, table, bass.IndirectOffsetOnAxis(index, 0),
                                        bounds_check=bound_of[bound], oob_is_err=False).then_inc(s, 16)

            def landed(stored, each, ring, steps=NCH):
                for r in range(ring):
                    pool.wait_ge(stored[r], each * ((steps - 1 - r) // ring + 1))

            def phase1(c):
                v, ix, r = halves(er[:, c.slot(RING)]), ix1[:, c.slot(RING)], c.slot(RING)
                pool.wait_ge(ix1_ready, c.done())
                pool.wait_ge(n_s_sb, c.done(RING))
                pool.sem_inc(pool_cleared, 1)
                for t in range(TC):
                    gather(v[:, t, 0], x, ix[:, SRC, t:t + 1], N - 1, er_in[r])
                    gather(v[:, t, 1], x, ix[:, DSTG, t:t + 1], N - 1, er_in[r])
                for t in range(TC):
                    pool.indirect_dma_start(row_of_node, bass.IndirectOffsetOnAxis(ix[:, SIDX, t:t + 1], 0),
                                            ix[:, ENUM, t:t + 1], None, bounds_check=bound_of[N - 1],
                                            oob_is_err=False).then_inc(rows_set[r], 16)

            pool.wait_ge(fill_out, 16)
            all_steps(pool, 0, NCH, phase1, peel=1 + UNROLL)
            landed(rows_set, 16 * TC, RING)

            def find_rows(c):
                pool.wait_ge(ix2_ready, c.done())
                pool.sem_inc(pool_cleared, 1)
                for t in range(TC):
                    gather(slots[:, c.slot(2), t:t + 1], row_of_node, ix2[:, c.slot(RING), SRC, t:t + 1], N - 1, slots_in[c.slot(2)])

            find_rows(Step(pool, None, 0, {}))
            landed(x1_stored, 32, 2)
            pool.wait_ge(n_s_sb, NCH)

            def phase2(c):
                find_rows(c.back(-1))
                pool.wait_ge(rowix_ready, c.done())
                pool.wait_ge(q_T_ps, c.done(RING))
                pool.sem_inc(pool_cleared, 1)
                for t in range(TC):
                    gather(halves(er[:, c.slot(RING)])[:, t, 0], x1_rows, rowix[:, c.slot(RING), t:t + 1], 2 * EP - 1,
                           q_er_in[c.slot(RING)])

            all_steps(pool, 0, NCH, phase2, peel=1 + UNROLL)

            def gather_h1(c):
                pool.wait_ge(ix3_ready, c.done())
                pool.wait_ge(t_T_ps, c.done(RING))
                pool.sem_inc(pool_cleared, 1)
                for t in range(TC):
                    gather(halves(er[:, c.slot(RING)])[:, t, 0], h1_rows, ix3[:, c.slot(RING), 0, t:t + 1], 2 * EP - 1,
                           t_er_in[c.slot(RING)])

            def scatter_out(c):
                pool.wait_ge(t_out_sb, c.done())
                pool.sem_inc(pool_cleared, 1)
                for t in range(TC):
                    pool.indirect_dma_start(out, bass.IndirectOffsetOnAxis(ix3[:, c.slot(RING), 1, t:t + 1], 0),
                                            tiles(t_out[:, c.slot(RING)])[:, t], None, bounds_check=bound_of[N - 1],
                                            oob_is_err=False).then_inc(rows_scattered[c.slot(RING)], 16)

            landed(h1_stored, 32, 2)
            gather_h1(Step(pool, None, 0, {}))
            landed(out_stored, 16, 2, ND)

            def phase3(c, last=False):
                if not last:
                    gather_h1(c.back(-1))
                if c.base > 0:
                    scatter_out(c.back(1))

            all_steps(pool, 0, NCH, phase3, peel=1 + UNROLL, last=lambda c: phase3(c, True))
            scatter_out(Step(pool, None, NCH - 1, {}))
            landed(rows_scattered, 16 * TC, RING)

        @block.tensor
        def _(pe):
            mm, tr = nc.tensor.matmul, nc.tensor.transpose
            pe.wait_ge(pool_consts, 2)
            pe.wait_ge(rowf_ready, 1)
            for kind in range(3):
                for a in range(2):
                    last = tr([psF0, psF1, psB0][kind][:, a * TA:(a + 1) * TA], rowf[:, kind, a], ident[0:TA, 0:TA])
            last.then_inc(edgesT, 1)
            pe.wait_ge(weights_in, 16 * 30)
            pe.wait_ge(setup_dve, 1)
            pe.wait_ge(edges_ready, 1)

            def transposes(ps, rows, done):
                for k in range(4):
                    last = tr(ps[:, k * P:(k + 1) * P], rows[:, k * P:(k + 1) * P], ident[:, :])
                last.then_inc(done, 1)

            def add_bias(ps, which, cols=BANK):
                return mm(ps[:, 0:cols], pick[:, :], bias3[:, which, 0:cols], start=True, stop=False, skip_group_check=True)

            def rows_out(ps, pairs, done):
                for k in range(4):
                    for n, (lhsT, w) in enumerate(pairs):
                        last = mm(ps[:, k * P:(k + 1) * P], lhsT[:, k * P:(k + 1) * P], w, start=False,
                                  stop=(k == 3 and n == len(pairs) - 1), skip_group_check=True)
                last.then_inc(done, 1)

            def f_in(s):
                pe.wait_ge(xd_in[s.slot(2)], s.done(0, 16, 2))
                pe.wait_ge(f_x1_sb, s.done(1))
                transposes(psF0, xd[:, s.slot(2)], f_xT_ps)

            def f_hidden(s):
                pe.wait_ge(f_xT_sb, s.done())
                mm(psF1[:, :], bd_u1[:, :], f_xT[:, :], start=True, stop=True).then_inc(f_u_ps, 1)

            def f_update(s):
                pe.wait_ge(f_U_sb, s.done())
                add_bias(psF0, 0)
                rows_out(psF0, [(f_U, bd_u2[:, :]), (f_xT, bd_c[:, :])], f_r_ps)

            def f_turn(s):
                pe.wait_ge(f_s_sb, s.done())
                transposes(psF1, f_s, f_sT_ps)

            def f_centre(s):
                pe.wait_ge(f_sT_sb, s.done())
                add_bias(psF0, 1)
                rows_out(psF0, [(f_sT, bd_c[:, :])], f_sc_ps)

            def g_in(s):
                pe.wait_ge(f_x1_sb, s.done())
                pe.wait_ge(g_r_sb, s.done(1))
                transposes(psB0, f_x1[:, s.slot(2)], g_xT_ps)

            def g_hidden(s):
                pe.wait_ge(g_xT_sb, s.done())
                mm(psB1[:, :], bd_s1[:, :], g_xT[:, :], start=True, stop=True).then_inc(g_h_ps, 1)

            def g_update(s):
                pe.wait_ge(g_h_sb, s.done())
                add_bias(psB0, 3)
                rows_out(psB0, [(g_h, bd_s2[:, :])], g_o_ps)

            def m_in(c):
                pe.wait_ge(er_in[c.slot(RING)], c.done(0, 16 * 2 * TC, RING))
                pe.wait_ge(ends_in[c.slot(2)], c.done(0, 32, 2))
                pe.wait_ge(m_agg_sb, c.done(1))
                pe.wait_ge(n_U_sb, c.done(1))
                rows = er[:, c.slot(RING)]
                tr(psM0[:, 0:P], rows[:, 0:P], ident[:, :])
                tr(psM1[0:TC * EF, 0:P], ea[:, c.slot(2)], ident[:, :])
                for k in range(1, 4):
                    last = tr(psM0[:, k * P:(k + 1) * P], rows[:, k * P:(k + 1) * P], ident[:, :])
                last.then_inc(m_T_ps, 1)

            def m_hidden(c):
                pe.wait_ge(m_eaT_sb, c.done())
                pe.wait_ge(m_xT_sb, c.done())
                mm(psM1[0:H, :], w_m1[:, :], m_xT[:, c.slot(2)], start=True, stop=False, skip_group_check=True)
                for t in range(TC):
                    last = mm(psM1[0:H, t * P:(t + 1) * P], w_m1e[:, t], m_eaT[:, :], start=False, stop=(t == TC - 1),
                              skip_group_check=True)
                last.then_inc(m_hid_ps, 1)

            def m_message(c):
                pe.wait_ge(m_hid_sb, c.done())
                mm(psM0[0:H, :], w_m2[:, :], m_hid[:, :], start=True, stop=True).then_inc(m_msg_ps, 1)

            def m_update(c):
                pe.wait_ge(m_agg_sb, c.done())
                mm(psM1[:, :], bd_u1[:, :], m_xT[:, c.slot(2)], start=True, stop=False)
                mm(psM1[:, :], w_u1a[:, :], m_agg[:, c.slot(2)], start=False, stop=True).then_inc(m_u_ps, 1)

            def n_update(c):
                pe.wait_ge(n_U_sb, c.done())
                pe.wait_ge(n_x1_sb, c.done(1))
                add_bias(psN[0], 0)
                rows_out(psN[0], [(n_U, bd_u2[:, :]), (m_xT[:, c.slot(2)], bd_c[:, :])], n_r_ps)

            def n_turn(c):
                pe.wait_ge(n_s_sb, c.done())
                transposes(psN[1], n_s, n_sT_ps)

            def n_centre(c):
                pe.wait_ge(n_sT_sb, c.done())
                add_bias(psN[0], 1)
                rows_out(psN[0], [(n_sT, bd_c[:, :])], n_sc_ps)

            def q_in(c):
                pe.wait_ge(q_er_in[c.slot(RING)], c.done(0, 16 * TC, RING))
                pe.wait_ge(q_x1_in[c.slot(RING)], c.done(0, 16, RING))
                transposes(psM0, er[:, c.slot(RING)], q_T_ps)

            def q_hidden(c):
                pe.wait_ge(q_T_sb, c.done())
                pe.wait_ge(q_h_sb, c.done(1))
                add_bias(psM1, 2)
                for k in range(TC):
                    mm(psM1[:, k * P:(k + 1) * P], q_T[:, k * P:(k + 1) * P], bd_s1[:, :], start=False, stop=False,
                       skip_group_check=True)
                pe.wait_ge(q_mean_sb, c.done())
                for k in range(TC):
                    last = mm(psM1[:, k * P:(k + 1) * P], q_mean[:, k * P:(k + 1) * P], w_n1[:, :], start=False,
                              stop=(k == TC - 1), skip_group_check=True)
                last.then_inc(q_h_ps, 1)

            def t_in(c):
                pe.wait_ge(t_er_in[c.slot(RING)], c.done(0, 16 * TC, RING))
                pe.wait_ge(t_h1_in[c.slot(RING)], c.done(0, 32, RING))
                transposes(psM0, er[:, c.slot(RING)], t_T_ps)

            def t_update(c):
                pe.wait_ge(t_T_sb, c.done())
                pe.wait_ge(t_mean_sb, c.done())
                pe.wait_ge(t_r_sb, c.done(2))
                ps = psN[c.slot(2)]
                add_bias(ps, 3, TC * H)
                for k in range(TC):
                    last = mm(ps[:, k * H:(k + 1) * H], t_T[:, k * P:(k + 1) * P], w_l2[:, :], start=False,
                              stop=(k == TC - 1), skip_group_check=True)
                last.then_inc(t_o_ps, 1)

            def phase1(s):
                b = s.back(1)
                on = s.base > 0
                f_in(s)
                if on:
                    g_in(b)
                    n_update(b)
                f_hidden(s)
                m_in(s)
                if on:
                    g_hidden(b)
                f_update(s)
                if on:
                    n_turn(b)
                m_hidden(s)
                if on:
                    g_update(b)
                    n_centre(b)
                m_message(s)
                f_turn(s)
                m_update(s)
                f_centre(s)

            all_steps(pe, 0, NCH, phase1)
            tail = Step(pe, None, NCH - 1, {})
            n_update(tail)
            n_turn(tail)
            n_centre(tail)

            def phase2(c):
                s = c.back(-NCH)
                b = s.back(1)
                f_in(s)
                g_in(b)
                q_in(c)
                f_hidden(s)
                g_hidden(b)
                f_update(s)
                g_update(b)
                f_turn(s)
                q_hidden(c)
                f_centre(s)

            all_steps(pe, 0, NCH, phase2)
            tail = Step(pe, None, ND - 1, {})
            g_in(tail)
            g_hidden(tail)
            g_update(tail)

            def phase3(c):
                t_in(c)
                t_update(c)

            all_steps(pe, 0, NCH, phase3)

        @block.scalar
        def _(act):
            A = nc.scalar.activation

            act.wait_ge(weights_in, 16 * 30)
            act.wait_ge(setup_dve, 1)

            def copy(into, ps, src_sem, done, s):
                act.wait_ge(src_sem, s.done())
                A(into, ps, ACT.Copy).then_inc(done, 1)

            def relu(into, ps, bias, src_sem, done, s):
                act.wait_ge(src_sem, s.done())
                A(into, ps, ACT.Relu, bias=bias).then_inc(done, 1)

            def square(into, of, src_sem, done, s):
                act.wait_ge(src_sem, s.done())
                A(into, of, ACT.Square).then_inc(done, 1)

            def std(into, var, src_sem, done, s):
                act.wait_ge(src_sem, s.done())
                A(into, var, ACT.Sqrt, bias=eps_c[:, :], scale=1.0 / H).then_inc(done, 1)

            f1 = lambda s: copy(f_xT[:, :], psF0[:, :], f_xT_ps, f_xT_sb, s)
            f2 = lambda s: relu(f_U[:, :], psF1[:, :], bu1_c[:, :], f_u_ps, f_U_sb, s)
            f3 = lambda s: square(f_sq[:, :], psF0[:, :], f_r_ps, f_sq1, s)
            f4 = lambda s: std(f_std[:, 0], f_var[:, 0], f_var1, f_std1, s)
            f5 = lambda s: copy(f_sT[:, :], psF1[:, :], f_sT_ps, f_sT_sb, s)
            f6 = lambda s: square(f_sq[:, :], psF0[:, :], f_sc_ps, f_sq2, s)
            f7 = lambda s: std(f_std[:, 1], f_var[:, 1], f_var2, f_std2, s)
            g1 = lambda s: copy(g_xT[:, :], psB0[:, :], g_xT_ps, g_xT_sb, s)
            g2 = lambda s: relu(g_h[:, :], psB1[:, :], b1_c[:, :], g_h_ps, g_h_sb, s)
            g3 = lambda s: square(g_sq[:, :], g_r[:, :], g_r_sb, g_sq_sb, s)
            g4 = lambda s: std(g_std[:, :], g_var[:, :], g_var_sb, g_std_sb, s)
            m1 = lambda s: copy(m_xT[:, s.slot(2)], psM0[:, :], m_T_ps, m_xT_sb, s)
            m2 = lambda s: relu(m_hid[0:H, :], psM1[0:H, :], bm1_c[:, :], m_hid_ps, m_hid_sb, s)
            n1 = lambda s: relu(n_U[:, :], psM1[:, :], bu1_c[:, :], m_u_ps, n_U_sb, s)
            n2 = lambda s: square(n_sq[:, :], psN[0][:, :], n_r_ps, n_sq1, s)
            n3 = lambda s: std(n_std[:, 0], n_var[:, 0], n_var1, n_std1, s)
            n4 = lambda s: copy(n_sT[:, :], psN[1][:, :], n_sT_ps, n_sT_sb, s)
            n5 = lambda s: square(n_sq[:, :], psN[0][:, :], n_sc_ps, n_sq2, s)
            n6 = lambda s: std(n_std[:, 1], n_var[:, 1], n_var2, n_std2, s)

            def phase1(s):
                b = s.back(1)
                on = s.base > 0
                if on:
                    n1(b)
                f1(s)
                if on:
                    g1(b)
                    n2(b)
                    n3(b)
                f2(s)
                m1(s)
                if on:
                    g2(b)
                f3(s)
                f4(s)
                if on:
                    n4(b)
                m2(s)
                if on:
                    g3(b)
                    n5(b)
                    g4(b)
                    n6(b)
                f5(s)
                f6(s)
                f7(s)

            all_steps(act, 0, NCH, phase1)
            tail = Step(act, None, NCH - 1, {})
            for stage in (n1, n2, n3, n4, n5, n6):
                stage(tail)

            q1 = lambda c: copy(q_T[:, :], psM0[:, :], q_T_ps, q_T_sb, c)

            def q2(c):
                act.wait_ge(h1_stored[c.slot(2)], c.done(2, 32, 2))
                act.wait_ge(q_h_ps, c.done())
                A(q_h[:, c.slot(2)], psM1[:, :], ACT.Relu).then_inc(q_h_sb, 1)

            def phase2(c):
                s = c.back(-NCH)
                b = s.back(1)
                f1(s)
                g1(b)
                q1(c)
                f2(s)
                g2(b)
                f3(s)
                f4(s)
                g3(b)
                g4(b)
                f5(s)
                q2(c)
                f6(s)
                f7(s)

            all_steps(act, 0, NCH, phase2)
            tail = Step(act, None, ND - 1, {})
            for stage in (g1, g2, g3, g4):
                stage(tail)

            t1 = lambda c: copy(t_T[H:P, :], psM0[H:P, :], t_T_ps, t_T_sb, c)
            t2 = lambda c: square(t_sq[:, :], t_r[:, :], t_r_sb, t_sq_sb, c)
            t3 = lambda c: std(t_std[:, :], t_var[:, :], t_var_sb, t_std_sb, c)

            def phase3(c):
                t1(c)
                if c.base > 0:
                    t2(c.back(1))
                    t3(c.back(1))

            all_steps(act, 0, NCH, phase3)
            tail = Step(act, None, NCH - 1, {})
            t2(tail)
            t3(tail)

        @block.vector
        def _(dve):
            V = nc.vector
            local = [0]

            def after(ins):
                local[0] += 1
                ins.then_inc(zeroed, 1)
                dve.wait_ge(zeroed, local[0])

            for w in (bd_c, bd_u1, bd_u2, bd_s1, bd_s2, w_m1e, w_u1a, w_n1, pick):
                V.memset(w[:], 0.0)
            V.memset(edges[:, 0:3, :], 0)
            V.memset(rows2[:, :], 0)
            V.memset(eps_c[:, :], EPS)
            V.memset(ones_r[:, :], 1.0)
            V.memset(m_hid[H:H + 1, :], 1.0)
            after(V.memset(cmean[:, :], 0.0))
            V.memset(fill[:, 0:EF], 0).then_inc(pads_ready, 1)
            for lo in (0, H):
                V.memset(bd_c[lo:lo + H, lo:lo + H], -1.0 / H)
            for lo in (0, 32):
                V.memset(pick[lo:lo + 1, :], 1.0)
            after(V.memset(pick[64:65, :], 1.0))
            dve.wait_ge(pool_consts, 3)
            V.tensor_tensor(bd_c[:, :], bd_c[:, :], ident[:, :], ALU.add)

            dve.wait_ge(raw_in, 64)
            rd = lambda n: raw[:, n].rearrange("q a p -> q (a p)")
            rf = lambda n: rowf[:, n].rearrange("q a p -> q (a p)")
            V.tensor_copy(rf(0), rd(0))
            V.tensor_scalar(rf(1), rd(1), 0.0, None, ALU.max)
            V.tensor_tensor(rf(3), rd(1), rd(2), ALU.is_equal)
            nl = notlast[:, :, :].rearrange("q a p -> q (a p)")
            after(V.tensor_tensor(nl, rd(1), rd(3), ALU.is_equal))
            V.scalar_tensor_tensor(rf(2), nl, float(NOWHERE), rd(1), ALU.mult, ALU.add).then_inc(rowf_ready, 1)
            dve.wait_ge(edgesT, 1)
            for kind, ps in ((SRC, psF0), (DSTG, psF1), (SIDX, psB0)):
                last = V.tensor_copy(edges[:, kind, 0:NT], ps[:, 0:NT])
            last.then_inc(edges_ready, 1)
            dve.wait_ge(edges_ready, 1)

            def stage1(c):
                if c.k is not None or c.base >= RING:
                    dve.wait_ge(er_in[c.slot(RING)], c.done(RING, 16 * 2 * TC, RING))
                    dve.wait_ge(rows_set[c.slot(RING)], c.done(RING, 16 * TC, RING))
                V.tensor_copy(ix1[:, c.slot(RING)], edges[:, :, bass.ds(c.value(TC, 0), TC)]).then_inc(ix1_ready, 1)

            stage1(Step(dve, None, 0, {}))
            stage1(Step(dve, None, 1, {}))

            dve.wait_ge(pads_in, 64)
            V.memset(fill[:, :], -1).then_inc(fill_ready, 1)

            dve.wait_ge(weights_in, 16 * 30)
            after(V.tensor_reduce(cmean[:, :], cen[:, :, :], AX_X, ALU.add))
            after(V.scalar_tensor_tensor(cen[:, :, :], cmean[:, :].unsqueeze(2).to_broadcast([P, 6, H]), -1.0 / H,
                                         cen[:, :, :], ALU.mult, ALU.add))
            for lo in (0, H):
                V.tensor_copy(bd_u2[lo:lo + H, lo:lo + H], cen[lo:lo + H, 0])
                V.tensor_copy(bd_s2[lo:lo + H, lo:lo + H], cen[lo:lo + H, 1])
            V.tensor_copy(w_l2[:, :], cen[:, 2])
            V.tensor_copy(brow[:, 0:2], cen[0:96, 3:5])
            after(V.tensor_copy(brow[:, 3], cen[0:96, 5]))
            after(V.tensor_copy(bpart[:, :, :], brow[:, :, :]))
            after(V.tensor_tensor(brest[:, :, :], brow[:, :, :], bpart[:, :, :], ALU.subtract))
            after(V.tensor_copy(bmid[:, :, :], brest[:, :, :]))
            after(V.tensor_copy(bpart[32:64, :, :], bmid[32:64, :, :]))
            after(V.tensor_tensor(brest[:, :, :], brest[:, :, :], bmid[:, :, :], ALU.subtract))
            after(V.tensor_copy(bpart[64:96, :, :], brest[64:96, :, :]))
            for t in range(8):
                last = V.tensor_copy(bias3[:, :, t * H:(t + 1) * H], bpart[:, :, :])
            last.then_inc(setup_dve, 1)
            dve.wait_ge(setup_dve, 1)

            def variance(into, sq, n, sq_sem, done, s):
                dve.wait_ge(sq_sem, s.done())
                V.tensor_reduce(into, tiles(sq), AX_X, ALU.add).then_inc(done, 1)

            def reciprocal(into, of, std_sem, done, s):
                dve.wait_ge(std_sem, s.done())
                V.reciprocal(into, of).then_inc(done, 1)

            def scaled(into, of, rstd, n, rstd_sem, done, s):
                dve.wait_ge(rstd_sem, s.done())
                V.tensor_tensor(tiles(into), tiles(of), per_row(rstd, n), ALU.mult).then_inc(done, 1)

            def times_gamma(into, of, src_sem, done, s):
                dve.wait_ge(src_sem, s.done())
                V.tensor_tensor(tiles(into), tiles(of), gam[:, :].unsqueeze(1).to_broadcast([P, 8, H]),
                                ALU.mult).then_inc(done, 1)

            def plus(into, a, b, src_sem, done, s):
                dve.wait_ge(src_sem, s.done())
                V.tensor_tensor(into, a, b, ALU.add).then_inc(done, 1)

            fa = lambda s: variance(f_var[:, 0], f_sq[:, :], 8, f_sq1, f_var1, s)
            fb = lambda s: reciprocal(f_rstd[:, 0], f_std[:, 0], f_std1, f_rstd1, s)
            fc = lambda s: scaled(f_y[:, :], psF0[:, :], f_rstd[:, 0], 8, f_rstd1, f_y_sb, s)
            fd = lambda s: times_gamma(f_yg[:, :], f_y[:, :], f_y_sb, f_yg_sb, s)
            fe = lambda s: plus(f_s[:, :], f_yg[:, :], xd[:, s.slot(2)], f_yg_sb, f_s_sb, s)
            ff = lambda s: variance(f_var[:, 1], f_sq[:, :], 8, f_sq2, f_var2, s)
            fg = lambda s: reciprocal(f_rstd[:, 1], f_std[:, 1], f_std2, f_rstd2, s)
            fh = lambda s: scaled(f_x1[:, s.slot(2)], psF0[:, :], f_rstd[:, 1], 8, f_rstd2, f_x1_sb, s)
            ga = lambda s: plus(g_r[:, :], psB0[:, :], f_x1[:, s.slot(2)], g_o_ps, g_r_sb, s)
            gb = lambda s: variance(g_var[:, :], g_sq[:, :], 8, g_sq_sb, g_var_sb, s)
            gc = lambda s: reciprocal(g_rstd[:, :], g_std[:, :], g_std_sb, g_rstd_sb, s)

            def gd(s):
                dve.wait_ge(out_stored[s.slot(2)], s.done(2, 16, 2))
                scaled(g_out[:, s.slot(2)], g_r[:, :], g_rstd[:, :], 8, g_rstd_sb, g_out_sb, s)

            def ma(c):
                dve.wait_ge(m_T_ps, c.done())
                V.tensor_copy(m_eaT[:, :], psM1[0:TC * EF, 0:P]).then_inc(m_eaT_sb, 1)

            def scan(into, c, flags, data, done):
                first = c.k is None and c.base == 0
                carry = 0.0 if first else into[:, 1 - c.slot(2), EC - 1:EC]
                dve.wait_ge(done, c.done(1))
                V.tensor_tensor_scan(into[:, c.slot(2)], flags, data, carry, ALU.mult, ALU.add).then_inc(done, 1)

            def mb(c):
                dve.wait_ge(ends_in[c.slot(2)], c.done(0, 32, 2))
                scan(m_cnt, c, same[0:1, c.slot(2)], ones_r[:, :], m_cnt_sb)

            def mc(c):
                dve.wait_ge(m_msg_ps, c.done())
                scan(m_agg, c, same[:, c.slot(2)], psM0[0:H, :], m_agg_sb)

            def md(c):
                dve.wait_ge(inv_stored[c.slot(2)], c.done(2, 16, 2))
                dve.wait_ge(m_cnt_sb, c.done())
                V.reciprocal(m_inv[:, c.slot(2)], m_cnt[:, c.slot(2)]).then_inc(m_inv_sb, 1)

            na = lambda s: variance(n_var[:, 0], n_sq[:, :], 8, n_sq1, n_var1, s)
            nb = lambda s: reciprocal(n_rstd[:, 0], n_std[:, 0], n_std1, n_rstd1, s)
            nc_ = lambda s: scaled(n_y[:, :], psN[0][:, :], n_rstd[:, 0], 8, n_rstd1, n_y_sb, s)
            nd = lambda s: times_gamma(n_yg[:, :], n_y[:, :], n_y_sb, n_yg_sb, s)
            ne = lambda s: plus(n_s[:, :], n_yg[:, :], er[:, s.slot(RING)], n_yg_sb, n_s_sb, s)
            nf = lambda s: variance(n_var[:, 1], n_sq[:, :], 8, n_sq2, n_var2, s)
            ng = lambda s: reciprocal(n_rstd[:, 1], n_std[:, 1], n_std2, n_rstd2, s)

            def nh(s):
                dve.wait_ge(x1_stored[s.slot(2)], s.done(2, 32, 2))
                scaled(n_x1[:, s.slot(2)], psN[0][:, :], n_rstd[:, 1], 8, n_rstd2, n_x1_sb, s)

            def phase1(s):
                b = s.back(1)
                on = s.base > 0
                stage1(s.back(-2))
                mb(s)
                if on:
                    na(b)
                    nb(b)
                    nc_(b)
                ma(s)
                if on:
                    nd(b)
                    ne(b)
                md(s)
                fa(s)
                fb(s)
                fc(s)
                if on:
                    ga(b)
                fd(s)
                if on:
                    gb(b)
                fe(s)
                if on:
                    nf(b)
                    gc(b)
                mc(s)
                if on:
                    ng(b)
                    gd(b)
                    nh(b)
                ff(s)
                fg(s)
                fh(s)

            all_steps(dve, 0, NCH, phase1)
            tail = Step(dve, None, NCH - 1, {})
            for stage in (na, nb, nc_, nd, ne, nf, ng, nh):
                stage(tail)

            def stage2(c):
                if c.k is not None or c.base >= RING:
                    dve.wait_ge(slots_in[c.slot(2)], c.done(RING, 16 * TC, 2))
                V.tensor_copy(ix2[:, c.slot(RING)], edges[:, :, bass.ds(c.value(TC, 0), TC)]).then_inc(ix2_ready, 1)

            def rows_of(c):
                at = c.value(TC, 0)
                dve.wait_ge(slots_in[c.slot(2)], c.done(0, 16 * TC, 2))
                V.tensor_scalar(absent[:, :], slots[:, c.slot(2)], 0.0, None, ALU.is_lt).then_inc(absent_sb, 1)
                dve.wait_ge(absent_sb, c.done())
                V.scalar_tensor_tensor(away[:, :], ix2[:, c.slot(RING), ENUM], float(EP + 1), absent[:, :],
                                       ALU.add, ALU.mult).then_inc(away_sb, 1)
                if c.k is not None or c.base >= RING:
                    dve.wait_ge(q_er_in[c.slot(RING)], c.done(RING, 16 * TC, RING))
                dve.wait_ge(away_sb, c.done())
                V.tensor_tensor(rowix[:, c.slot(RING)], away[:, :], slots[:, c.slot(2)], ALU.add)
                V.tensor_tensor(rows2[:, bass.ds(at, TC)], away[:, :], slots[:, c.slot(2)], ALU.add).then_inc(rowix_ready, 1)

            def qa(c):
                dve.wait_ge(q_T_sb, c.done())
                dve.wait_ge(q_line_in[c.slot(2)], c.done(0, 32, 2))
                scan(m_agg, c, same[:, c.slot(2)], q_T[0:H, :], q_agg_sb)

            def mean(into, c, agg_sem, done):
                dve.wait_ge(agg_sem, c.done())
                V.tensor_tensor(into, m_agg[:, c.slot(2)], inv[:, c.slot(2)], ALU.mult).then_inc(done, 1)

            qb = lambda c: mean(q_mean[:, :], c, q_agg_sb, q_mean_sb)

            stage2(Step(dve, None, 0, {}))
            stage2(Step(dve, None, 1, {}))
            rows_of(Step(dve, None, 0, {}))

            def phase2(c):
                s = c.back(-NCH)
                b = s.back(1)
                stage2(c.back(-2))
                rows_of(c.back(-1))
                qa(c)
                qb(c)
                fa(s)
                fb(s)
                fc(s)
                ga(b)
                fd(s)
                fe(s)
                gb(b)
                gc(b)
                gd(b)
                ff(s)
                fg(s)
                fh(s)

            all_steps(dve, 0, NCH, phase2)
            tail = Step(dve, None, ND - 1, {})
            for stage in (ga, gb, gc, gd):
                stage(tail)

            def stage3(c):
                at = c.value(TC, 0)
                if c.k is not None or c.base >= RING:
                    dve.wait_ge(t_er_in[c.slot(RING)], c.done(RING, 16 * TC, RING))
                    dve.wait_ge(rows_scattered[c.slot(RING)], c.done(RING, 16 * TC, RING))
                V.tensor_copy(ix3[:, c.slot(RING), 0], rows2[:, bass.ds(at, TC)])
                V.tensor_copy(ix3[:, c.slot(RING), 1], edges[:, SIDX, bass.ds(at, TC)]).then_inc(ix3_ready, 1)

            def ta(c):
                dve.wait_ge(t_T_ps, c.done())
                dve.wait_ge(t_line_in[c.slot(2)], c.done(0, 32, 2))
                scan(m_agg, c, same[:, c.slot(2)], psM0[0:H, :], t_agg_sb)

            tb = lambda c: mean(t_T[0:H, :], c, t_agg_sb, t_mean_sb)

            def tc(c):
                dve.wait_ge(t_out_sb, c.done(1))
                plus(t_r[:, :], psN[c.slot(2)][:, 0:TC * H], t_x1[:, c.slot(RING)], t_o_ps, t_r_sb, c)

            td = lambda c: variance(t_var[:, :], t_sq[:, :], TC, t_sq_sb, t_var_sb, c)
            te = lambda c: reciprocal(t_rstd[:, :], t_std[:, :], t_std_sb, t_rstd_sb, c)

            def tf(c):
                dve.wait_ge(rows_scattered[c.slot(RING)], c.done(RING, 16 * TC, RING))
                scaled(t_out[:, c.slot(RING)], t_r[:, :], t_rstd[:, :], TC, t_rstd_sb, t_out_sb, c)

            dve.wait_ge(rowix_ready, NCH + 1)
            stage3(Step(dve, None, 0, {}))
            stage3(Step(dve, None, 1, {}))

            def phase3(c):
                stage3(c.back(-2))
                if c.base > 0:
                    tc(c.back(1))
                ta(c)
                if c.base > 0:
                    td(c.back(1))
                tb(c)
                if c.base > 0:
                    te(c.back(1))
                    tf(c.back(1))

            all_steps(dve, 0, NCH, phase3)
            tail = Step(dve, None, NCH - 1, {})
            for stage in (tc, td, te, tf):
                stage(tail)


_INS = ["x", "src", "dst", "edge_attr_16", "L0_gnn_W_m1", "L0_gnn_b_m1", "L0_gnn_W_m2", "L0_gnn_b_m2", "L0_gnn_W_u1",
        "L0_gnn_b_u1", "L0_gnn_W_u2", "L0_gnn_b_u2", "L0_gnn_gamma", "L0_gnn_beta", "L1_gnn_W_self1",
        "L1_gnn_W_neigh1", "L1_gnn_b1", "L1_gnn_W_self2", "L1_gnn_W_neigh2", "L1_gnn_b2"]


def kernel(**inputs):
    import numpy as np
    import concourse.bacc as bacc
    from concourse import mybir as mb
    from concourse.bass_utils import run_bass_kernel_spmd

    nc = bacc.Bacc("TRN2", target_bir_lowering=False, num_devices=1)
    arrays, args = {}, []
    for name in _INS:
        a = np.ascontiguousarray(inputs[name])
        arrays[f"in_{name}"] = a
        args.append(nc.dram_tensor(f"in_{name}", a.shape, mb.dt.from_np(a.dtype), kind="ExternalInput").ap())
    rows, cols = inputs["x"].shape
    out = nc.dram_tensor("out_rows", (rows, cols), mb.dt.float32, kind="ExternalOutput").ap()
    build_gnn(nc, *args, out)
    r = run_bass_kernel_spmd(nc, [arrays], core_ids=[0])
    return r.results[0]["out_rows"]
```

```python
from contextlib import ExitStack

import concourse.bass as bass
from concourse import mybir

P = 128
H = 64
EPS = 1e-5
BANK = 512
RING = 4
UNROLL = 4

ALU = mybir.AluOpType
ACT = mybir.ActivationFunctionType
F32 = mybir.dt.float32
BF16 = mybir.dt.bfloat16
I32 = mybir.dt.int32
AX_X = mybir.AxisListType.X


class Step:

    def __init__(self, eng, k, base, kept):
        self.eng, self.k, self.base, self.kept = eng, k, base, kept

    def back(self, n):
        return Step(self.eng, self.k, self.base - n, self.kept)

    def value(self, per_step, plus):
        add = per_step * self.base + plus
        if self.k is None:
            return max(add, 0)
        key = (per_step, add)
        if key not in self.kept:
            self.kept[key] = self.eng.snap(self.k * (per_step * UNROLL) + add)
        return self.kept[key]

    def done(self, lag=0, each=1, ring=1):
        add = each * ((self.base - lag) // ring + 1)
        if self.k is None:
            return max(add, 0)
        assert add > 0
        key = (each, ring, add)
        if key not in self.kept:
            self.kept[key] = self.eng.snap(self.k * (each * UNROLL // ring) + add)
        return self.kept[key]

    def slot(self, ring):
        return self.base % ring


def all_steps(eng, first, count, body, peel):
    assert (count - peel) % UNROLL == 0
    for i in range(peel):
        body(Step(eng, None, first + i, {}))
    with eng.Fori(0, (count - peel) // UNROLL) as k:
        kept = {}
        for i in range(UNROLL):
            body(Step(eng, k, first + peel + i, kept))


def written_out(eng, first, count, body):
    for i in range(count):
        body(Step(eng, None, first + i, {}))


def within(count):
    def run(stage, c):
        if c.k is not None or 0 <= c.base < count:
            stage(c)
    return run


def build_gnn(nc, x, src, dst, edge_attr, W_m1, b_m1, W_m2, b_m2, W_u1, b_u1, W_u2, b_u2, gamma, beta,
              W_self1, W_neigh1, b_1, W_self2, W_neigh2, b_2, out):
    N = x.shape[0]
    E = src.shape[0]
    EF = edge_attr.shape[1]
    TC = 4
    EC = TC * P
    NCH = -(-E // EC)
    EP = NCH * EC
    NT = EP // P
    TA = NT // 2
    DC = 8 * P
    ND = 2 * NCH
    OVER = ND * DC - N
    assert 0 <= OVER < DC and NT % 2 == 0 and TA <= P and E % 100 == 0
    NTP = NT + 2 * TC
    Q0 = NCH + 2
    DRAIN = 4
    dense, edge = within(ND), within(NCH)
    OP, PIECES, LEFT = 125, 10, 5
    OT, OW = E // OP, E // PIECES
    OWP = LEFT << (OW // LEFT - 1).bit_length()
    assert OP * OT == E and PIECES * OW == E and E % 4 == 0 and E < 1 << 22
    NOWHERE = 1 << 20
    assert N < NOWHERE

    def scratch(name, shape, dt):
        return nc.dram_tensor(name, shape, dt, kind="Internal").ap()

    dst_line = scratch("dst_line", (EP + 2,), I32)
    src_line = scratch("src_line", (EP,), I32)
    ea_rows = scratch("ea_rows", (EP, EF), F32)
    same_line = scratch("same_line", (EP,), F32)
    count_line = scratch("count_line", (EP,), F32)
    inv_line = scratch("inv_line", (EP,), F32)
    row_of_node = scratch("row_of_node", (N, 1), I32)
    x1_rows = scratch("x1_rows", (2 * EP, H), F32)
    h1_rows = scratch("h1_rows", (2 * EP, H), F32)

    with ExitStack() as ctx:
        def sb(name, shape, dt=F32):
            return ctx.enter_context(nc.sbuf_tensor(name, shape, dt))

        def sem(name):
            return ctx.enter_context(nc.semaphore(name))

        def sems(name, n):
            return [sem(f"{name}{i}") for i in range(n)]

        def bank(name):
            return ctx.enter_context(nc.psum_tensor(name, [P, BANK], F32))

        psF = [bank("psF0"), bank("psF1")]
        psG = [bank("psG0"), bank("psG1")]
        psM = [bank("psM0"), bank("psM1")]
        psE = [bank("psE0"), bank("psE1")]

        ident = sb("ident", [P, P])
        bd_c = sb("bd_c", [P, P])
        bd_u1 = sb("bd_u1", [P, P])
        bd_u2 = sb("bd_u2", [P, P])
        bd_s1 = sb("bd_s1", [P, P])
        bd_s2 = sb("bd_s2", [P, P])
        w_m1 = sb("w_m1", [P, H])
        w_m1e = sb("w_m1e", [TC * EF, TC, H])
        w_m2 = sb("w_m2", [H + 1, H])
        w_m2T = sb("w_m2T", [H, H + 1])
        w_u1n = sb("w_u1n", [H, H])
        w_comb = sb("w_comb", [H + 1, P])
        w_n1 = sb("w_n1", [H, P])
        w_l2 = sb("w_l2", [P, H])
        cen = sb("cen", [P, 6, H])
        cmean = sb("cmean", [P, 6])
        bm1_c = sb("bm1_c", [H, 1])
        bu1_c = sb("bu1_c", [P, 1])
        b1_c = sb("b1_c", [P, 1])
        eps_c = sb("eps_c", [P, 1])
        gam_c = sb("gam_c", [P, 1])
        brow = sb("brow", [96, 4, H])
        brest = sb("brest", [96, 4, H])
        bpart = sb("bpart", [96, 4, H], BF16)
        bmid = sb("bmid", [96, 4, H], BF16)
        bias3 = sb("bias3", [96, 4, BANK], BF16)
        pick = sb("pick", [96, P], BF16)

        raw = sb("raw", [TA, 4, 2, P], I32)
        rowf = sb("rowf", [TA, 4, 2, P])
        notlast = sb("notlast", [TA, 2, P])
        edges = sb("edges", [P, 4, NTP], I32)
        SRC, DSTG, SIDX, ENUM = range(4)
        rows2 = sb("rows2", [P, NTP], I32)
        fill = sb("fill", [P, N // 80], I32)
        zpad = sb("zpad", [P, 16], I32)

        pair_a, pair_b = sb("pair_a", [OP, OT], I32), sb("pair_b", [OP, OT], I32)
        falls, falls_lane = sb("falls", [OP, OT]), sb("falls_lane", [P, P])
        falls_any, falls_flag = sb("falls_any", [1, 1]), sb("falls_flag", [1, 1], I32)
        o_dst, o_src, o_ea = sb("o_dst", [OP, OT], I32), sb("o_src", [OP, OT], I32), sb("o_ea", [OP, OT * EF])
        o_key, o_pos = sb("o_key", [OP, OT]), sb("o_pos", [OP, OT])
        o_rank, o_row = sb("o_rank", [OP, OT, LEFT]), sb("o_row", [OP, OT, 2], I32)
        line_raw = sb("line_raw", [OP, OW], I32)
        line_key, line_pos, line_hit = sb("line_key", [OP, OW]), sb("line_pos", [OP, OW]), sb("line_hit", [OP, OWP])
        s_key, s_int, s_ea = sb("s_key", [OP, 2]), sb("s_int", [OP, 4], I32), sb("s_ea", [OP, EF])

        xd = sb("xd", [P, 2, BANK])
        f_xT = sb("f_xT", [P, 2, BANK])
        f_U, f_sT, f_sq_a, f_sq_b, f_y = (sb(n, [P, BANK]) for n in ("f_U", "f_sT", "f_sq_a", "f_sq_b", "f_y"))
        f_x1 = sb("f_x1", [P, 2, BANK])
        f_var, f_std, f_rstd = (sb(n, [P, 2, 8]) for n in ("f_var", "f_std", "f_rstd"))
        g_xT, g_h, g_r, g_sq = (sb(n, [P, BANK]) for n in ("g_xT", "g_h", "g_r", "g_sq"))
        g_out = sb("g_out", [P, 2, BANK])
        g_var, g_std, g_rstd = (sb(n, [P, 8]) for n in ("g_var", "g_std", "g_rstd"))

        er = sb("er", [P, RING, BANK])
        ea = sb("ea", [P, 2, TC * EF])
        same = sb("same", [H + 1, 2, EC])
        inv = sb("inv", [H, 2, EC])
        counts = sb("counts", [TA, 2 * P])
        m_xT = sb("m_xT", [P, 2, BANK])
        m_eaT = sb("m_eaT", [TC * EF, P])
        m_hid = sb("m_hid", [H + 1, EC])
        m_agg = sb("m_agg", [H + 1, 2, EC])
        n_U, n_sT, n_sq_a, n_sq_b, n_y = (sb(n, [P, BANK]) for n in ("n_U", "n_sT", "n_sq_a", "n_sq_b", "n_y"))
        n_x1 = sb("n_x1", [P, 2, BANK])
        n_var, n_std, n_rstd = (sb(n, [P, 2, 8]) for n in ("n_var", "n_std", "n_rstd"))
        ix1 = sb("ix1", [P, RING, 4, TC], I32)
        ix2 = sb("ix2", [P, RING, 4, TC], I32)
        ix_h1 = sb("ix_h1", [P, RING, TC], I32)
        ix_out = sb("ix_out", [P, RING, TC], I32)
        slots = sb("slots", [P, 2, TC], I32)
        absent = sb("absent", [P, TC])
        away = sb("away", [P, TC])
        rowix = sb("rowix", [P, RING, TC], I32)
        q_T, q_mean = sb("q_T", [P, BANK]), sb("q_mean", [H, EC])
        q_h = sb("q_h", [P, 2, BANK])
        t_T = sb("t_T", [P, 2, BANK])
        t_x1 = sb("t_x1", [P, RING, TC * H])
        t_r, t_sq = sb("t_r", [P, TC * H]), sb("t_sq", [P, TC * H])
        t_var, t_std, t_rstd = (sb(n, [P, TC]) for n in ("t_var", "t_std", "t_rstd"))
        t_out = sb("t_out", [P, RING, TC * H])

        weights_in, lines_in, pads_in = sem("weights_in"), sem("lines_in"), sem("pads_in")
        raw_in, same_out, fill_out = sem("raw_in"), sem("same_out"), sem("fill_out")
        pool_consts, zeroed, setup_dve = sem("pool_consts"), sem("zeroed"), sem("setup_dve")
        rowf_ready, edgesT, edges_ready = sem("rowf_ready"), sem("edgesT"), sem("edges_ready")
        pads_ready, fill_ready = sem("pads_ready"), sem("fill_ready")

        lines_cleared, pool_cleared = sem("lines_cleared"), sem("pool_cleared")

        pairs_in, falls_ready, falls_T = sem("pairs_in"), sem("falls_ready"), sem("falls_T")
        flag_ready, ordered = sem("flag_ready"), sem("ordered")
        own_in, piece_in, rows_moved = sem("own_in"), sem("piece_in"), sem("rows_moved")
        w_m2T_ps, w_m2T_sb, w_comb_ps, w_comb_sb = map(sem, "w_m2T_ps w_m2T_sb w_comb_ps w_comb_sb".split())

        xd_in = sems("xd_in", 2)
        f_xT_ps, f_xT_sb, f_u_ps, f_U_sb, f_r_ps, f_sq1, f_var1, f_std1, f_rstd1 = map(
            sem, "f_xT_ps f_xT_sb f_u_ps f_U_sb f_r_ps f_sq1 f_var1 f_std1 f_rstd1".split())
        f_y_sb, f_yT_ps, f_sT_sb, f_sc_ps, f_sq2, f_var2, f_std2, f_rstd2, f_x1_sb = map(
            sem, "f_y_sb f_yT_ps f_sT_sb f_sc_ps f_sq2 f_var2 f_std2 f_rstd2 f_x1_sb".split())
        g_xT_ps, g_xT_sb, g_h_ps, g_h_sb, g_o_ps, g_r_sb, g_sq_sb, g_var_sb, g_std_sb, g_rstd_sb, g_out_sb = map(
            sem, "g_xT_ps g_xT_sb g_h_ps g_h_sb g_o_ps g_r_sb g_sq_sb g_var_sb g_std_sb g_rstd_sb g_out_sb".split())
        out_stored = sems("out_stored", 2)

        ix1_ready, er_in, ends_in = sem("ix1_ready"), sems("er_in", RING), sems("ends_in", 2)
        rows_set = sems("rows_set", RING)
        m_T_ps, m_xT_sb, m_eaT_sb, m_hid_ps, m_hid_sb, m_agg_sb, m_u_ps = map(
            sem, "m_T_ps m_xT_sb m_eaT_sb m_hid_ps m_hid_sb m_agg_sb m_u_ps".split())
        count_stored, counts_in, counts_inv, inv_stored = (
            sems("count_stored", 2), sem("counts_in"), sem("counts_inv"), sem("inv_stored"))
        n_U_sb, n_r_ps, n_sq1, n_var1, n_std1, n_rstd1, n_y_sb = map(
            sem, "n_U_sb n_r_ps n_sq1 n_var1 n_std1 n_rstd1 n_y_sb".split())
        n_yT_ps, n_sT_sb, n_sc_ps, n_sq2, n_var2, n_std2, n_rstd2, n_x1_sb = map(
            sem, "n_yT_ps n_sT_sb n_sc_ps n_sq2 n_var2 n_std2 n_rstd2 n_x1_sb".split())
        x1_stored = sems("x1_stored", 2)

        ix2_ready, absent_sb, away_sb, rowix_ready = map(sem, "ix2_ready absent_sb away_sb rowix_ready".split())
        slots_in = sems("slots_in", 2)
        q_er_in, q_x1_in, q_line_in = sems("q_er_in", RING), sems("q_x1_in", RING), sems("q_line_in", 2)
        q_T_ps, q_T_sb, q_agg_sb, q_mean_sb, q_h_ps, q_h_sb = map(
            sem, "q_T_ps q_T_sb q_agg_sb q_mean_sb q_h_ps q_h_sb".split())
        h1_stored = sems("h1_stored", 2)

        ix_h1_ready, ix_out_ready = sem("ix_h1_ready"), sem("ix_out_ready")
        t_er_in, t_h1_in, t_line_in = sems("t_er_in", RING), sems("t_h1_in", RING), sems("t_line_in", 2)
        t_T_ps, t_T_sb, t_agg_sb, t_mean_sb, t_o_ps, t_r_sb, t_sq_sb, t_var_sb, t_std_sb, t_rstd_sb, t_out_sb = map(
            sem, "t_T_ps t_T_sb t_agg_sb t_mean_sb t_o_ps t_r_sb t_sq_sb t_var_sb t_std_sb t_rstd_sb t_out_sb".split())
        rows_scattered = sems("rows_scattered", RING)

        def tiles(ap):
            return ap.rearrange("p (t f) -> p t f", f=H)

        def halves(ap):
            return ap.rearrange("p (t h f) -> p t h f", h=2, f=H)

        def per_row(ap, n):
            return ap.unsqueeze(2).to_broadcast([P, n, H])

        def one_line(ap):
            return ap.rearrange("(a n) -> a n", a=1)

        col = lambda v: v.rearrange("(n a) -> n a", a=1)

        block = ctx.enter_context(nc.Block())

        @block.sync
        def _(sp):
            ab = dict(b=100)
            lanes = lambda ap: ap.rearrange("(p t) -> p t", p=OP)
            for half, at in enumerate((0, E // 2 - 1)):
                into = slice(half * OT // 2, (half + 1) * OT // 2)
                sp.dma_start(pair_a[:, into], lanes(dst[at:at + E // 2])).then_inc(pairs_in, 16)
                sp.dma_start(pair_b[:, into], lanes(dst[at + 1:at + 1 + E // 2])).then_inc(pairs_in, 16)
            sp.dma_start(dst_line[1:E + 1].rearrange("(b n) -> b n", **ab), dst.rearrange("(b n) -> b n", **ab)).then_inc(lines_in, 16)
            sp.dma_start(src_line[0:E].rearrange("(b n) -> b n", **ab), src.rearrange("(b n) -> b n", **ab)).then_inc(lines_in, 16)
            sp.dma_start(ea_rows[0:E, :].rearrange("(b n) f -> b (n f)", **ab), edge_attr.rearrange("(b n) f -> b (n f)", **ab)).then_inc(lines_in, 16)
            sp.wait_ge(pads_ready, 3)
            NP_ = EP - E
            sp.dma_start(one_line(dst_line[0:1]), zpad[0:1, 1:2]).then_inc(pads_in, 16)
            sp.dma_start(dst_line[E + 1:EP + 2].rearrange("(n a) -> n a", a=1), zpad[0:NP_ + 1, 1:2]).then_inc(pads_in, 16)
            sp.dma_start(src_line[E:EP].rearrange("(n a) -> n a", a=1), zpad[0:NP_, 0:1]).then_inc(pads_in, 16)
            sp.dma_start(ea_rows[E:EP, :], fill[0:NP_, 0:EF].bitcast(F32)).then_inc(pads_in, 16)
            sp.wait_ge(lines_in, 48)
            sp.wait_ge(pads_in, 64)
            sp.wait_ge(ordered, 1)
            line = lambda ap: ap.rearrange("(a q p) -> q a p", a=2, p=P)
            for n, s in enumerate((src_line[0:EP], dst_line[1:EP + 1], dst_line[0:EP], dst_line[2:EP + 2])):
                sp.dma_start(raw[:, n], line(s)).then_inc(raw_in, 16)
            sp.wait_ge(zeroed, 1)
            for lo in (0, H):
                sp.dma_start(bd_u1[lo:lo + H, lo:lo + H], W_u1[0:H, :]).then_inc(weights_in, 16)
                sp.dma_start(bd_s1[lo:lo + H, lo:lo + H], W_self1).then_inc(weights_in, 16)
                sp.dma_start(cen[lo:lo + H, 0], W_u2).then_inc(weights_in, 16)
                sp.dma_start(cen[lo:lo + H, 1], W_self2).then_inc(weights_in, 16)
                sp.dma_start(bu1_c[lo:lo + H, :], col(b_u1)).then_inc(weights_in, 16)
                sp.dma_start(b1_c[lo:lo + H, :], col(b_1)).then_inc(weights_in, 16)
            sp.dma_start(cen[0:H, 2], W_neigh2).then_inc(weights_in, 16)
            sp.dma_start(cen[H:P, 2], W_self2).then_inc(weights_in, 16)
            for n, v in enumerate((b_u2, beta, b_2)):
                sp.dma_start(cen[:, 3 + n], v.partition_broadcast(P)).then_inc(weights_in, 16)
            sp.dma_start(brow[:, 2], b_1.partition_broadcast(96)).then_inc(weights_in, 16)
            for lo in (0, H):
                sp.dma_start(gam_c[lo:lo + H, :], col(gamma)).then_inc(weights_in, 16)
            sp.dma_start(w_m1[0:H, :], W_m1[H:2 * H, :]).then_inc(weights_in, 16)
            sp.dma_start(w_m1[H:P, :], W_m1[0:H, :]).then_inc(weights_in, 16)
            for t in range(TC):
                sp.dma_start(w_m1e[EF * t:EF * (t + 1), t], W_m1[2 * H:2 * H + EF, :]).then_inc(weights_in, 16)
            sp.dma_start(w_m2[0:H, :], W_m2).then_inc(weights_in, 16)
            sp.dma_start(w_m2[H:H + 1, :], one_line(b_m2)).then_inc(weights_in, 16)
            sp.dma_start(w_u1n[:, :], W_u1[H:2 * H, :]).then_inc(weights_in, 16)
            sp.dma_start(w_n1[:, H:P], W_neigh1).then_inc(weights_in, 16)
            sp.dma_start(bm1_c[:, :], col(b_m1)).then_inc(weights_in, 16)
            sp.wait_ge(fill_ready, 1)
            sp.dma_start(row_of_node.rearrange("(b n) a -> b (n a)", b=80), fill[0:80, :]).then_inc(fill_out, 16)
            sp.wait_ge(rowf_ready, 1)
            sp.dma_start(line(same_line), rowf[:, 3]).then_inc(same_out, 16)
            sp.wait_ge(same_out, 16)

            def dense_rows(dram, s):
                at = s.value(DC, -OVER if s.base >= NCH else 0)
                return dram[bass.ds(at, DC), :].rearrange("(p t) f -> p (t f)", p=P)

            def edge_rows(dram, c, base):
                return dram[bass.ds(c.value(EC, base), EC), :].rearrange("(t p) f -> p t f", p=P)

            def edge_line(dram, c):
                return one_line(dram)[:, bass.ds(c.value(EC, 0), EC)]

            def to_all(line, n):
                return line.rearrange("a n -> (a n)").partition_broadcast(n)

            def load_dense(s):
                at = dense_rows(x, s)
                sp.wait_ge(f_xT_ps, s.done(2))
                sp.dma_start(xd[:, s.slot(2)], at).then_inc(xd_in[s.slot(2)], 16)

            def store_dense(s):
                at = dense_rows(out, s)
                sp.wait_ge(g_out_sb, s.done())
                if s.base == NCH:
                    sp.wait_ge(out_stored[(NCH - 1) % 2], 16 * ((NCH - 1) // 2 + 1))
                sp.dma_start(at, g_out[:, s.slot(2)]).then_inc(out_stored[s.slot(2)], 16)

            def load_ea(c):
                at = edge_rows(ea_rows, c, 0)
                sp.wait_ge(m_T_ps, c.done(2))
                sp.dma_start(ea[:, c.slot(2)].rearrange("p (t f) -> p t f", f=EF), at).then_inc(ends_in[c.slot(2)], 16)

            def load_same(c):
                at = edge_line(same_line, c)
                sp.wait_ge(m_agg_sb, c.done(2))
                sp.sem_inc(lines_cleared, 1)
                sp.dma_start(same[:, c.slot(2)], to_all(at, H + 1)).then_inc(ends_in[c.slot(2)], 16)

            def store_count(c):
                at = edge_line(count_line, c)
                sp.wait_ge(m_agg_sb, c.done())
                sp.dma_start(at, m_agg[H:H + 1, c.slot(2)]).then_inc(count_stored[c.slot(2)], 16)

            def store_ends(table, rows, done, stored, c):
                at_d, at_s = edge_rows(table, c, 0), edge_rows(table, c, EP)
                v = halves(rows[:, c.slot(2)])
                sp.wait_ge(done, c.done())
                sp.dma_start(at_s, v[:, :, 0]).then_inc(stored[c.slot(2)], 16)
                sp.dma_start(at_d, v[:, :, 1]).then_inc(stored[c.slot(2)], 16)

            store_x1 = lambda c: store_ends(x1_rows, n_x1, n_x1_sb, x1_stored, c)
            store_h1 = lambda c: store_ends(h1_rows, q_h, q_h_sb, h1_stored, c)

            for first in range(2):
                load_dense(Step(sp, None, first, {}))
                load_ea(Step(sp, None, first, {}))
            load_same(Step(sp, None, 0, {}))

            def phase1(s):
                dense(load_dense, s.back(-2))
                edge(load_same, s.back(-1))
                edge(store_count, s.back(1))
                edge(store_x1, s.back(2))
                edge(load_ea, s.back(-2))
                dense(store_dense, s.back(3))

            all_steps(sp, 0, NCH - UNROLL, phase1, peel=1 + UNROLL)
            written_out(sp, NCH - UNROLL, UNROLL + 1, phase1)
            pair = lambda ap: ap.rearrange("(q n) -> q n", q=TA)
            for q in range(2):
                sp.wait_ge(count_stored[q], 16 * ((NCH + 1 - q) // 2))
            sp.dma_start(counts[:, :], pair(count_line)).then_inc(counts_in, 16)
            written_out(sp, NCH + 1, 1, phase1)
            sp.wait_ge(counts_inv, 1)
            sp.dma_start(pair(inv_line), counts[:, :]).then_inc(inv_stored, 16)

            def load_lines(c, into, agg_done):
                same_at, inv_at = edge_line(same_line, c), edge_line(inv_line, c)
                sp.wait_ge(agg_done, c.done(2))
                sp.sem_inc(lines_cleared, 1)
                sp.dma_start(same[0:H, c.slot(2)], to_all(same_at, H)).then_inc(into[c.slot(2)], 16)
                sp.dma_start(inv[:, c.slot(2)], to_all(inv_at, H)).then_inc(into[c.slot(2)], 16)

            q_lines = lambda c: load_lines(c, q_line_in, q_mean_sb)
            t_lines = lambda c: load_lines(c, t_line_in, t_mean_sb)

            def load_x1(c):
                at = edge_rows(x1_rows, c, 0)
                sp.wait_ge(q_T_ps, c.done(RING))
                sp.dma_start(halves(er[:, c.slot(RING)])[:, :, 1], at).then_inc(q_x1_in[c.slot(RING)], 16)

            for q in range(2):
                sp.wait_ge(x1_stored[q], 32 * ((NCH + 1 - q) // 2))
            written_out(sp, 0, 3, load_x1)
            sp.wait_ge(inv_stored, 16)
            written_out(sp, 0, 2, q_lines)

            def phase2(s):
                c = s.back(Q0)
                dense(load_dense, s.back(-2))
                edge(store_h1, c.back(2))
                edge(load_x1, c.back(-3))
                if c.base > 0:
                    edge(q_lines, c.back(-1))
                dense(store_dense, s.back(3))

            all_steps(sp, Q0, ND - Q0 - 2 * UNROLL, phase2, peel=3 + UNROLL)
            written_out(sp, ND - 2 * UNROLL, 2 * UNROLL + DRAIN, phase2)
            for q in range(2):
                sp.wait_ge(h1_stored[q], 32 * ((NCH + 1 - q) // 2))

            def load_h1(c):
                at = edge_rows(h1_rows, c, 0)
                sp.wait_ge(t_T_ps, c.done(RING))
                sp.dma_start(halves(er[:, c.slot(RING)])[:, :, 1], at).then_inc(t_h1_in[c.slot(RING)], 16)

            def load_t_x1(c):
                at = edge_rows(x1_rows, c, 0)
                sp.wait_ge(t_r_sb, c.done(RING))
                sp.dma_start(tiles(t_x1[:, c.slot(RING)]), at).then_inc(t_h1_in[c.slot(RING)], 16)

            written_out(sp, 0, 3, load_h1)
            written_out(sp, 0, 2, t_lines)
            written_out(sp, 0, 2, load_t_x1)

            def phase3(c):
                edge(load_h1, c.back(-3))
                edge(load_t_x1, c.back(-2))
                edge(t_lines, c.back(-2))

            all_steps(sp, 0, NCH - UNROLL, phase3, peel=1 + UNROLL)
            written_out(sp, NCH - UNROLL, UNROLL, phase3)

        @block.gpsimd
        def _(pool):
            nc.gpsimd.memset(zpad[:, 0:1], 0).then_inc(pads_ready, 1)
            nc.gpsimd.memset(zpad[:, 1:2], -1).then_inc(pads_ready, 1)
            nc.gpsimd.memset(ident[:, :], 0.0).then_inc(pool_consts, 1)
            pool.wait_ge(pool_consts, 1)
            nc.gpsimd.affine_select(out=ident[:, :], in_=ident[:, :], compare_op=ALU.not_equal, fill=1.0, base=0,
                                    pattern=[[-1, P]], channel_multiplier=1).then_inc(pool_consts, 1)
            nc.gpsimd.iota(edges[:, ENUM, :], pattern=[[P, NTP]], base=0, channel_multiplier=1).then_inc(pool_consts, 1)

            bound_of = {n: pool.to_reg(n) for n in (N - 1, 2 * EP - 1, EP)}

            def order_edges():
                G = nc.gpsimd
                lanes = dict(p=OP)
                pool.dma_start(o_dst[:, :], dst.rearrange("(p t) -> p t", **lanes)).then_inc(own_in, 16)
                pool.dma_start(o_src[:, :], src.rearrange("(p t) -> p t", **lanes)).then_inc(own_in, 16)
                pool.dma_start(o_ea[:, :], edge_attr.rearrange("(p t) f -> p (t f)", **lanes)).then_inc(own_in, 16)
                G.iota(o_row[:, :, 0], pattern=[[1, OT]], base=0, channel_multiplier=OT)
                G.iota(line_raw[:, :], pattern=[[1, OW]], base=0, channel_multiplier=0)
                G.memset(line_hit[:, :], 0.0)
                G.memset(o_rank[:, :, :], 0.0)
                pool.drain()
                G.tensor_copy(o_pos[:, :], o_row[:, :, 0])
                G.tensor_copy(line_pos[:, :], line_raw[:, :])
                pool.wait_ge(own_in, 48)
                G.tensor_copy(o_key[:, :], o_dst[:, :])
                pool.drain()
                with pool.Fori(0, PIECES) as j:
                    pool.dma_start(line_raw[:, :], dst[bass.ds(j * OW, OW)].partition_broadcast(OP)).then_inc(piece_in, 16)
                    pool.wait_ge(piece_in, pool.snap(j * 16 + 16))
                    pool.sem_inc(pool_cleared, 1)
                    G.tensor_copy(line_key[:, :], line_raw[:, :])
                    pool.drain()
                    with pool.Fori(0, OT) as t:
                        G.tensor_copy(s_key[:, 0:1], o_key[:, bass.ds(t, 1)])
                        G.tensor_copy(s_key[:, 1:2], o_pos[:, bass.ds(t, 1)])
                        pool.drain()
                        G.tensor_scalar(line_hit[:, 0:OW], line_pos[:, :], s_key[:, 1:2], 0.5, ALU.is_lt, ALU.mult)
                        pool.drain()
                        G.tensor_tensor(line_hit[:, 0:OW], line_key[:, :], line_hit[:, 0:OW], ALU.subtract)
                        pool.drain()
                        G.tensor_scalar(line_hit[:, 0:OW], line_hit[:, 0:OW], s_key[:, 0:1], None, ALU.is_lt)
                        pool.drain()
                        n = OWP
                        while n > LEFT:
                            n //= 2
                            G.tensor_tensor(line_hit[:, 0:n], line_hit[:, 0:n], line_hit[:, n:2 * n], ALU.add)
                            pool.drain()
                        G.tensor_tensor(o_rank[:, bass.ds(t, 1), :], o_rank[:, bass.ds(t, 1), :],
                                        line_hit[:, 0:LEFT].unsqueeze(1), ALU.add)
                        pool.drain()
                    G.tensor_scalar(o_pos[:, :], o_pos[:, :], -float(OW), None, ALU.add)
                    pool.drain()
                for n in range(1, LEFT):
                    G.tensor_tensor(o_rank[:, :, 0], o_rank[:, :, 0], o_rank[:, :, n], ALU.add)
                    pool.drain()
                G.tensor_copy(o_row[:, :, 0], o_rank[:, :, 0])
                G.tensor_scalar(o_row[:, :, 1], o_rank[:, :, 0], 1.0, None, ALU.add)
                pool.drain()
                pool.wait_ge(lines_in, 48)
                with pool.Fori(0, OT) as t:
                    G.tensor_copy(s_int[:, 0:2], o_row[:, bass.ds(t, 1), :])
                    G.tensor_copy(s_int[:, 2:3], o_src[:, bass.ds(t, 1)])
                    G.tensor_copy(s_int[:, 3:4], o_dst[:, bass.ds(t, 1)])
                    G.tensor_copy(s_ea[:, :], o_ea[:, bass.ds(t * EF, EF)])
                    pool.drain()
                    for table, ix, rows in ((col(src_line), 0, s_int[:, 2:3]), (col(dst_line), 1, s_int[:, 3:4]),
                                            (ea_rows, 0, s_ea[:, :])):
                        pool.indirect_dma_start(table, bass.IndirectOffsetOnAxis(s_int[:, ix:ix + 1], 0), rows, None,
                                                bounds_check=bound_of[EP], oob_is_err=False).then_inc(rows_moved, 16)
                    pool.wait_ge(rows_moved, pool.snap(t * 48 + 48))
                    pool.sem_inc(pool_cleared, 1)

            def gather(into, table, index, bound, s):
                pool.indirect_dma_start(into, None, table, bass.IndirectOffsetOnAxis(index, 0),
                                        bounds_check=bound_of[bound], oob_is_err=False).then_inc(s, 16)

            def landed(stored, each, ring, steps=NCH):
                for r in range(ring):
                    pool.wait_ge(stored[r], each * ((steps - 1 - r) // ring + 1))

            pool.wait_ge(flag_ready, 1)
            falling = pool.value_load(falls_flag[0:1, 0:1], min_val=0, max_val=1)
            with pool.If(falling > 0):
                order_edges()
                pool.sem_inc(pool_cleared, 1)
            with pool.Else():
                pool.sem_inc(pool_cleared, 1)
            pool.sem_inc(ordered, 1)

            def phase1(c):
                v, ix, r = halves(er[:, c.slot(RING)]), ix1[:, c.slot(RING)], c.slot(RING)
                pool.wait_ge(ix1_ready, c.done())
                pool.wait_ge(m_T_ps, c.done(RING))
                pool.sem_inc(pool_cleared, 1)
                for t in range(TC):
                    gather(v[:, t, 0], x, ix[:, SRC, t:t + 1], N - 1, er_in[r])
                    gather(v[:, t, 1], x, ix[:, DSTG, t:t + 1], N - 1, er_in[r])
                if c.k is None and c.base == 0:
                    pool.wait_ge(fill_out, 16)
                for t in range(TC):
                    pool.indirect_dma_start(row_of_node, bass.IndirectOffsetOnAxis(ix[:, SIDX, t:t + 1], 0),
                                            ix[:, ENUM, t:t + 1], None, bounds_check=bound_of[N - 1],
                                            oob_is_err=False).then_inc(rows_set[r], 16)

            all_steps(pool, 0, NCH, phase1, peel=1 + UNROLL)
            landed(rows_set, 16 * TC, RING)

            def find_rows(c):
                pool.wait_ge(ix2_ready, c.done())
                pool.wait_ge(rowix_ready, c.done(2))
                pool.sem_inc(pool_cleared, 1)
                for t in range(TC):
                    gather(slots[:, c.slot(2), t:t + 1], row_of_node, ix2[:, c.slot(RING), SRC, t:t + 1], N - 1, slots_in[c.slot(2)])

            written_out(pool, 0, 2, find_rows)
            landed(x1_stored, 32, 2)

            def phase2(c):
                pool.wait_ge(rowix_ready, c.done())
                pool.wait_ge(q_T_ps, c.done(RING))
                pool.sem_inc(pool_cleared, 1)
                for t in range(TC):
                    gather(halves(er[:, c.slot(RING)])[:, t, 0], x1_rows, rowix[:, c.slot(RING), t:t + 1], 2 * EP - 1,
                           q_er_in[c.slot(RING)])
                edge(find_rows, c.back(-2))

            all_steps(pool, 0, NCH - UNROLL, phase2, peel=1 + UNROLL)
            written_out(pool, NCH - UNROLL, UNROLL, phase2)

            def gather_h1(c):
                pool.wait_ge(ix_h1_ready, c.done())
                pool.wait_ge(t_T_ps, c.done(RING))
                pool.sem_inc(pool_cleared, 1)
                for t in range(TC):
                    gather(halves(er[:, c.slot(RING)])[:, t, 0], h1_rows, ix_h1[:, c.slot(RING), t:t + 1], 2 * EP - 1,
                           t_er_in[c.slot(RING)])

            def scatter_out(c):
                pool.wait_ge(ix_out_ready, c.done())
                pool.wait_ge(t_out_sb, c.done())
                pool.sem_inc(pool_cleared, 1)
                for t in range(TC):
                    pool.indirect_dma_start(out, bass.IndirectOffsetOnAxis(ix_out[:, c.slot(RING), t:t + 1], 0),
                                            tiles(t_out[:, c.slot(RING)])[:, t], None, bounds_check=bound_of[N - 1],
                                            oob_is_err=False).then_inc(rows_scattered[c.slot(RING)], 16)

            landed(h1_stored, 32, 2)
            gather_h1(Step(pool, None, 0, {}))
            landed(out_stored, 16, 2, ND)

            def phase3(c):
                edge(gather_h1, c.back(-1))
                edge(scatter_out, c.back(2))

            all_steps(pool, 0, NCH - UNROLL, phase3, peel=1 + UNROLL)
            written_out(pool, NCH - UNROLL, UNROLL + 2, phase3)
            landed(rows_scattered, 16 * TC, RING)

        @block.tensor
        def _(pe):
            mm, tr = nc.tensor.matmul, nc.tensor.transpose
            pe.wait_ge(pool_consts, 2)
            pe.wait_ge(falls_ready, 1)
            tr(psE[0][:, 0:P], falls_lane[:, :], ident[:, :]).then_inc(falls_T, 1)
            pe.wait_ge(rowf_ready, 1)
            for kind in range(3):
                for a in range(2):
                    last = tr([psF[0], psF[1], psG[0]][kind][:, a * TA:(a + 1) * TA], rowf[:, kind, a], ident[0:TA, 0:TA])
            last.then_inc(edgesT, 1)
            pe.wait_ge(weights_in, 16 * 31)
            tr(psM[0][0:H, 0:H + 1], w_m2[:, :], ident[0:H + 1, 0:H + 1]).then_inc(w_m2T_ps, 1)
            pe.wait_ge(w_m2T_sb, 1)
            mm(psM[1][0:H + 1, 0:H], w_m2T[:, :], w_u1n[:, :], start=True, stop=True).then_inc(w_comb_ps, 1)
            pe.wait_ge(w_comb_sb, 1)
            pe.wait_ge(setup_dve, 1)
            pe.wait_ge(edges_ready, 1)

            def transposes(ps, rows, done):
                for k in range(4):
                    last = tr(ps[:, k * P:(k + 1) * P], rows[:, k * P:(k + 1) * P], ident[:, :])
                last.then_inc(done, 1)

            def add_bias(ps, which, cols=BANK):
                return mm(ps[:, 0:cols], pick[:, :], bias3[:, which, 0:cols], start=True, stop=False, skip_group_check=True)

            def rows_out(ps, pairs, done):
                for k in range(4):
                    for n, (lhsT, w) in enumerate(pairs):
                        last = mm(ps[:, k * P:(k + 1) * P], lhsT[:, k * P:(k + 1) * P], w, start=False,
                                  stop=(k == 3 and n == len(pairs) - 1), skip_group_check=True)
                last.then_inc(done, 1)

            def f_in(s):
                pe.wait_ge(xd_in[s.slot(2)], s.done(0, 16, 2))
                pe.wait_ge(f_x1_sb, s.done(2))
                transposes(psF[s.slot(2)], xd[:, s.slot(2)], f_xT_ps)

            def f_u(s):
                pe.wait_ge(f_xT_sb, s.done())
                mm(psF[s.slot(2)][:, :], bd_u1[:, :], f_xT[:, s.slot(2)], start=True, stop=True).then_inc(f_u_ps, 1)

            def f_r(s):
                pe.wait_ge(f_U_sb, s.done())
                add_bias(psF[s.slot(2)], 0)
                rows_out(psF[s.slot(2)], [(f_U, bd_u2[:, :]), (f_xT[:, s.slot(2)], bd_c[:, :])], f_r_ps)

            def f_yT(s):
                pe.wait_ge(f_y_sb, s.done())
                transposes(psF[s.slot(2)], f_y, f_yT_ps)

            def f_sc(s):
                pe.wait_ge(f_sT_sb, s.done())
                add_bias(psF[s.slot(2)], 1)
                rows_out(psF[s.slot(2)], [(f_sT, bd_c[:, :])], f_sc_ps)

            def g_in(s):
                pe.wait_ge(f_x1_sb, s.done())
                pe.wait_ge(g_r_sb, s.done(2))
                transposes(psG[s.slot(2)], f_x1[:, s.slot(2)], g_xT_ps)

            def g_hp(s):
                pe.wait_ge(g_xT_sb, s.done())
                mm(psG[s.slot(2)][:, :], bd_s1[:, :], g_xT[:, :], start=True, stop=True).then_inc(g_h_ps, 1)

            def g_o(s):
                pe.wait_ge(g_h_sb, s.done())
                add_bias(psG[s.slot(2)], 3)
                rows_out(psG[s.slot(2)], [(g_h, bd_s2[:, :])], g_o_ps)

            def m_in(c):
                pe.wait_ge(er_in[c.slot(RING)], c.done(0, 16 * 2 * TC, RING))
                pe.wait_ge(ends_in[c.slot(2)], c.done(0, 32, 2))
                pe.wait_ge(n_x1_sb, c.done(2))
                pe.wait_ge(m_eaT_sb, c.done(2))
                ps, rows = psM[c.slot(2)], er[:, c.slot(RING)]
                tr(ps[:, 0:P], rows[:, 0:P], ident[:, :])
                tr(psE[c.slot(2)][0:TC * EF, 0:P], ea[:, c.slot(2)], ident[:, :])
                for k in range(1, 4):
                    last = tr(ps[:, k * P:(k + 1) * P], rows[:, k * P:(k + 1) * P], ident[:, :])
                last.then_inc(m_T_ps, 1)

            def m_hidden(c):
                pe.wait_ge(m_eaT_sb, c.done())
                pe.wait_ge(m_xT_sb, c.done())
                ps = psM[c.slot(2)]
                mm(ps[0:H, :], w_m1[:, :], m_xT[:, c.slot(2)], start=True, stop=False, skip_group_check=True)
                for t in range(TC):
                    last = mm(ps[0:H, t * P:(t + 1) * P], w_m1e[:, t], m_eaT[:, :], start=False, stop=(t == TC - 1),
                              skip_group_check=True)
                last.then_inc(m_hid_ps, 1)

            def m_u(c):
                pe.wait_ge(m_agg_sb, c.done())
                ps = psM[c.slot(2)]
                mm(ps[:, :], bd_u1[:, :], m_xT[:, c.slot(2)], start=True, stop=False)
                mm(ps[:, :], w_comb[:, :], m_agg[:, c.slot(2)], start=False, stop=True).then_inc(m_u_ps, 1)

            def n_r(c):
                pe.wait_ge(n_U_sb, c.done())
                add_bias(psM[c.slot(2)], 0)
                rows_out(psM[c.slot(2)], [(n_U, bd_u2[:, :]), (m_xT[:, c.slot(2)], bd_c[:, :])], n_r_ps)

            def n_yT(c):
                pe.wait_ge(n_y_sb, c.done())
                transposes(psM[c.slot(2)], n_y, n_yT_ps)

            def n_sc(c):
                pe.wait_ge(n_sT_sb, c.done())
                add_bias(psM[c.slot(2)], 1)
                rows_out(psM[c.slot(2)], [(n_sT, bd_c[:, :])], n_sc_ps)

            def q_in(c):
                pe.wait_ge(q_er_in[c.slot(RING)], c.done(0, 16 * TC, RING))
                pe.wait_ge(q_x1_in[c.slot(RING)], c.done(0, 16, RING))
                pe.wait_ge(q_T_sb, c.done(2))
                transposes(psM[c.slot(2)], er[:, c.slot(RING)], q_T_ps)

            def q_hidden(c):
                pe.wait_ge(q_T_sb, c.done())
                pe.wait_ge(q_mean_sb, c.done())
                pe.wait_ge(q_h_sb, c.done(2))
                add_bias(psE[c.slot(2)], 2)
                rows_out(psE[c.slot(2)], [(q_T, bd_s1[:, :]), (q_mean, w_n1[:, :])], q_h_ps)

            def t_in(c):
                pe.wait_ge(t_er_in[c.slot(RING)], c.done(0, 16 * TC, RING))
                pe.wait_ge(t_h1_in[c.slot(RING)], c.done(0, 32, RING))
                pe.wait_ge(t_T_sb, c.done(2))
                pe.wait_ge(t_agg_sb, c.done(2))
                transposes(psM[c.slot(2)], er[:, c.slot(RING)], t_T_ps)

            def t_o(c):
                pe.wait_ge(t_T_sb, c.done())
                pe.wait_ge(t_mean_sb, c.done())
                pe.wait_ge(t_r_sb, c.done(2))
                ps = psG[c.slot(2)]
                add_bias(ps, 3, TC * H)
                for k in range(TC):
                    last = mm(ps[:, k * H:(k + 1) * H], t_T[:, c.slot(2), k * P:(k + 1) * P], w_l2[:, :], start=False,
                              stop=(k == TC - 1), skip_group_check=True)
                last.then_inc(t_o_ps, 1)

            def phase1(s):
                dense(g_in, s.back(2))
                dense(f_in, s)
                edge(n_yT, s.back(2))
                dense(g_o, s.back(3))
                edge(m_u, s.back(1))
                dense(f_u, s)
                edge(n_sc, s.back(2))
                dense(f_yT, s.back(1))
                dense(f_r, s)
                dense(f_sc, s.back(1))
                edge(m_in, s)
                edge(n_r, s.back(1))
                dense(g_hp, s.back(2))
                edge(m_hidden, s)

            all_steps(pe, 0, NCH, phase1, peel=1 + UNROLL)
            written_out(pe, NCH, Q0 - NCH, phase1)

            def phase2(s):
                c = s.back(Q0)
                edge(q_hidden, c.back(2))
                dense(f_in, s)
                dense(g_in, s.back(2))
                dense(g_o, s.back(3))
                dense(f_yT, s.back(1))
                edge(q_in, c.back(1))
                dense(f_u, s)
                dense(f_sc, s.back(1))
                dense(g_hp, s.back(2))
                dense(f_r, s)

            all_steps(pe, Q0, ND - Q0, phase2, peel=3 + UNROLL)
            written_out(pe, ND, DRAIN, phase2)

            def phase3(c):
                edge(t_in, c)
                edge(t_o, c.back(1))

            all_steps(pe, 0, NCH, phase3, peel=1 + UNROLL)
            written_out(pe, NCH, 2, phase3)

        @block.scalar
        def _(act):
            A = nc.scalar.activation

            act.wait_ge(weights_in, 16 * 31)
            act.wait_ge(setup_dve, 1)

            def copy(into, ps, src_sem, done, s):
                act.wait_ge(src_sem, s.done())
                A(into, ps, ACT.Copy).then_inc(done, 1)

            def relu(into, ps, bias, src_sem, done, s):
                act.wait_ge(src_sem, s.done())
                A(into, ps, ACT.Relu, bias=bias).then_inc(done, 1)

            def square(into, of, src_sem, done, s):
                act.wait_ge(src_sem, s.done())
                A(into, of, ACT.Square).then_inc(done, 1)

            def std(into, var, src_sem, done, s):
                act.wait_ge(src_sem, s.done())
                A(into, var, ACT.Sqrt, bias=eps_c[:, :], scale=1.0 / H).then_inc(done, 1)

            def f_xT_copy(s):
                act.wait_ge(f_sT_sb, s.done(2))
                copy(f_xT[:, s.slot(2)], psF[s.slot(2)][:, :], f_xT_ps, f_xT_sb, s)

            def f_relu(s):
                act.wait_ge(f_r_ps, s.done(1))
                relu(f_U[:, :], psF[s.slot(2)][:, :], bu1_c[:, :], f_u_ps, f_U_sb, s)

            def f_square1(s):
                act.wait_ge(f_var1, s.done(1))
                square(f_sq_a[:, :], psF[s.slot(2)][:, :], f_r_ps, f_sq1, s)

            def f_square2(s):
                act.wait_ge(f_var2, s.done(1))
                square(f_sq_b[:, :], psF[s.slot(2)][:, :], f_sc_ps, f_sq2, s)

            f_root1 = lambda s: std(f_std[:, 0], f_var[:, 0], f_var1, f_std1, s)
            f_root2 = lambda s: std(f_std[:, 1], f_var[:, 1], f_var2, f_std2, s)

            def g_xT_copy(s):
                act.wait_ge(g_h_ps, s.done(1))
                copy(g_xT[:, :], psG[s.slot(2)][:, :], g_xT_ps, g_xT_sb, s)

            def g_relu(s):
                act.wait_ge(g_o_ps, s.done(1))
                relu(g_h[:, :], psG[s.slot(2)][:, :], b1_c[:, :], g_h_ps, g_h_sb, s)

            def g_square(s):
                act.wait_ge(g_var_sb, s.done(1))
                square(g_sq[:, :], g_r[:, :], g_r_sb, g_sq_sb, s)

            g_root = lambda s: std(g_std[:, :], g_var[:, :], g_var_sb, g_std_sb, s)

            def m_xT_copy(c):
                act.wait_ge(n_sT_sb, c.done(2))
                copy(m_xT[:, c.slot(2)], psM[c.slot(2)][:, :], m_T_ps, m_xT_sb, c)

            def m_relu(c):
                act.wait_ge(m_agg_sb, c.done(1))
                relu(m_hid[0:H, :], psM[c.slot(2)][0:H, :], bm1_c[:, :], m_hid_ps, m_hid_sb, c)

            def n_relu(c):
                act.wait_ge(n_r_ps, c.done(1))
                relu(n_U[:, :], psM[c.slot(2)][:, :], bu1_c[:, :], m_u_ps, n_U_sb, c)

            def n_square1(c):
                act.wait_ge(n_var1, c.done(1))
                square(n_sq_a[:, :], psM[c.slot(2)][:, :], n_r_ps, n_sq1, c)

            def n_square2(c):
                act.wait_ge(n_var2, c.done(1))
                square(n_sq_b[:, :], psM[c.slot(2)][:, :], n_sc_ps, n_sq2, c)

            n_root1 = lambda c: std(n_std[:, 0], n_var[:, 0], n_var1, n_std1, c)
            n_root2 = lambda c: std(n_std[:, 1], n_var[:, 1], n_var2, n_std2, c)

            def phase1(s):
                edge(m_relu, s.back(1))
                dense(f_xT_copy, s)
                dense(g_square, s.back(3))
                dense(f_relu, s)
                edge(n_square2, s.back(2))
                edge(n_relu, s.back(1))
                dense(g_root, s.back(3))
                edge(n_root2, s.back(2))
                dense(f_square1, s)
                dense(g_xT_copy, s.back(2))
                dense(f_square2, s.back(1))
                edge(m_xT_copy, s)
                dense(f_root1, s)
                dense(f_root2, s.back(1))
                edge(n_square1, s.back(1))
                dense(g_relu, s.back(2))
                edge(n_root1, s.back(1))

            all_steps(act, 0, NCH, phase1, peel=1 + UNROLL)
            written_out(act, NCH, Q0 - NCH, phase1)

            def q_T_copy(c):
                act.wait_ge(q_h_ps, c.done(1))
                act.wait_ge(q_agg_sb, c.done(1))
                copy(q_T[:, :], psM[c.slot(2)][:, :], q_T_ps, q_T_sb, c)

            def q_relu(c):
                act.wait_ge(h1_stored[c.slot(2)], c.done(2, 32, 2))
                act.wait_ge(q_h_ps, c.done())
                A(q_h[:, c.slot(2)], psE[c.slot(2)][:, :], ACT.Relu).then_inc(q_h_sb, 1)

            def phase2(s):
                c = s.back(Q0)
                dense(g_xT_copy, s.back(2))
                dense(f_xT_copy, s)
                edge(q_relu, c.back(2))
                edge(q_T_copy, c.back(1))
                dense(g_square, s.back(3))
                dense(f_relu, s)
                dense(f_square2, s.back(1))
                dense(g_relu, s.back(2))
                dense(f_root2, s.back(1))
                dense(f_square1, s)
                dense(g_root, s.back(3))
                dense(f_root1, s)

            all_steps(act, Q0, ND - Q0, phase2, peel=3 + UNROLL)
            written_out(act, ND, DRAIN, phase2)

            def t_T_copy(c):
                act.wait_ge(t_o_ps, c.done(2))
                copy(t_T[H:P, c.slot(2)], psM[c.slot(2)][H:P, :], t_T_ps, t_T_sb, c)

            def t_square(c):
                act.wait_ge(t_var_sb, c.done(1))
                square(t_sq[:, :], t_r[:, :], t_r_sb, t_sq_sb, c)

            t_root = lambda c: std(t_std[:, :], t_var[:, :], t_var_sb, t_std_sb, c)

            def phase3(c):
                edge(t_T_copy, c.back(1))
                edge(t_square, c.back(2))
                edge(t_root, c.back(2))

            all_steps(act, 0, NCH, phase3, peel=1 + UNROLL)
            written_out(act, NCH, 2, phase3)

        @block.vector
        def _(dve):
            V = nc.vector
            local = [0]

            def after(ins):
                local[0] += 1
                ins.then_inc(zeroed, 1)
                dve.wait_ge(zeroed, local[0])

            for w in (bd_c, bd_u1, bd_u2, bd_s1, bd_s2, w_m1e, w_comb, w_n1, pick, falls_lane):
                V.memset(w[:], 0.0)
            V.memset(edges[:, 0:3, :], 0)
            V.memset(rows2[:, :], 0)
            V.memset(eps_c[:, :], EPS)
            V.memset(m_hid[H:H + 1, :], 1.0)
            after(V.memset(cmean[:, :], 0.0))
            V.memset(fill[:, 0:EF], 0).then_inc(pads_ready, 1)
            for lo in (0, H):
                V.memset(bd_c[lo:lo + H, lo:lo + H], -1.0 / H)
            for lo in (0, 32):
                V.memset(pick[lo:lo + 1, :], 1.0)
            after(V.memset(pick[64:65, :], 1.0))
            dve.wait_ge(pairs_in, 64)
            after(V.tensor_tensor(falls[:, :], pair_a[:, :], pair_b[:, :], ALU.is_gt))
            V.tensor_reduce(falls_lane[0:OP, 0:1], falls[:, :], AX_X, ALU.max).then_inc(falls_ready, 1)
            dve.wait_ge(falls_T, 1)
            after(V.tensor_reduce(falls_any[:, :], psE[0][0:1, 0:P], AX_X, ALU.max))
            V.tensor_copy(falls_flag[:, :], falls_any[:, :]).then_inc(flag_ready, 1)
            dve.wait_ge(pool_consts, 3)
            V.tensor_tensor(bd_c[:, :], bd_c[:, :], ident[:, :], ALU.add)

            dve.wait_ge(raw_in, 64)
            rd = lambda n: raw[:, n].rearrange("q a p -> q (a p)")
            rf = lambda n: rowf[:, n].rearrange("q a p -> q (a p)")
            V.tensor_copy(rf(0), rd(0))
            V.tensor_scalar(rf(1), rd(1), 0.0, None, ALU.max)
            V.tensor_tensor(rf(3), rd(1), rd(2), ALU.is_equal)
            nl = notlast[:, :, :].rearrange("q a p -> q (a p)")
            after(V.tensor_tensor(nl, rd(1), rd(3), ALU.is_equal))
            V.scalar_tensor_tensor(rf(2), nl, float(NOWHERE), rd(1), ALU.mult, ALU.add).then_inc(rowf_ready, 1)
            dve.wait_ge(edgesT, 1)
            for kind, ps in ((SRC, psF[0]), (DSTG, psF[1]), (SIDX, psG[0])):
                last = V.tensor_copy(edges[:, kind, 0:NT], ps[:, 0:NT])
            last.then_inc(edges_ready, 1)
            dve.wait_ge(edges_ready, 1)

            def stage1(c):
                if c.k is not None or c.base >= RING:
                    dve.wait_ge(er_in[c.slot(RING)], c.done(RING, 16 * 2 * TC, RING))
                    dve.wait_ge(rows_set[c.slot(RING)], c.done(RING, 16 * TC, RING))
                V.tensor_copy(ix1[:, c.slot(RING)], edges[:, :, bass.ds(c.value(TC, 0), TC)]).then_inc(ix1_ready, 1)

            stage1(Step(dve, None, 0, {}))
            stage1(Step(dve, None, 1, {}))

            dve.wait_ge(pads_in, 64)
            V.memset(fill[:, :], -1).then_inc(fill_ready, 1)

            dve.wait_ge(weights_in, 16 * 31)
            dve.wait_ge(w_m2T_ps, 1)
            V.tensor_copy(w_m2T[:, :], psM[0][0:H, 0:H + 1]).then_inc(w_m2T_sb, 1)
            dve.wait_ge(w_comb_ps, 1)
            V.tensor_copy(w_comb[:, H:P], psM[1][0:H + 1, 0:H]).then_inc(w_comb_sb, 1)
            after(V.tensor_reduce(cmean[:, :], cen[:, :, :], AX_X, ALU.add))
            after(V.scalar_tensor_tensor(cen[:, :, :], cmean[:, :].unsqueeze(2).to_broadcast([P, 6, H]), -1.0 / H,
                                         cen[:, :, :], ALU.mult, ALU.add))
            for lo in (0, H):
                V.tensor_copy(bd_u2[lo:lo + H, lo:lo + H], cen[lo:lo + H, 0])
                V.tensor_copy(bd_s2[lo:lo + H, lo:lo + H], cen[lo:lo + H, 1])
            V.tensor_copy(w_l2[:, :], cen[:, 2])
            V.tensor_copy(brow[:, 0:2], cen[0:96, 3:5])
            after(V.tensor_copy(brow[:, 3], cen[0:96, 5]))
            after(V.tensor_copy(bpart[:, :, :], brow[:, :, :]))
            after(V.tensor_tensor(brest[:, :, :], brow[:, :, :], bpart[:, :, :], ALU.subtract))
            after(V.tensor_copy(bmid[:, :, :], brest[:, :, :]))
            after(V.tensor_copy(bpart[32:64, :, :], bmid[32:64, :, :]))
            after(V.tensor_tensor(brest[:, :, :], brest[:, :, :], bmid[:, :, :], ALU.subtract))
            after(V.tensor_copy(bpart[64:96, :, :], brest[64:96, :, :]))
            for t in range(8):
                last = V.tensor_copy(bias3[:, :, t * H:(t + 1) * H], bpart[:, :, :])
            last.then_inc(setup_dve, 1)
            dve.wait_ge(setup_dve, 1)

            def variance(into, sq, n, sq_sem, done, s):
                dve.wait_ge(sq_sem, s.done())
                V.tensor_reduce(into, tiles(sq), AX_X, ALU.add).then_inc(done, 1)

            def reciprocal(into, of, std_sem, done, s):
                dve.wait_ge(std_sem, s.done())
                V.reciprocal(into, of).then_inc(done, 1)

            def scaled(into, of, rstd, n, rstd_sem, done, s):
                dve.wait_ge(rstd_sem, s.done())
                V.tensor_tensor(tiles(into), tiles(of), per_row(rstd, n), ALU.mult).then_inc(done, 1)

            def turned_sum(into, yT, xT, src_sem, done, s):
                dve.wait_ge(src_sem, s.done())
                V.scalar_tensor_tensor(into, yT, gam_c[:, :], xT, ALU.mult, ALU.add).then_inc(done, 1)

            def plus(into, a, b, src_sem, done, s):
                dve.wait_ge(src_sem, s.done())
                V.tensor_tensor(into, a, b, ALU.add).then_inc(done, 1)

            f_variance1 = lambda s: variance(f_var[:, 0], f_sq_a[:, :], 8, f_sq1, f_var1, s)
            f_variance2 = lambda s: variance(f_var[:, 1], f_sq_b[:, :], 8, f_sq2, f_var2, s)
            f_recip1 = lambda s: reciprocal(f_rstd[:, 0], f_std[:, 0], f_std1, f_rstd1, s)
            f_recip2 = lambda s: reciprocal(f_rstd[:, 1], f_std[:, 1], f_std2, f_rstd2, s)

            def f_scale(s):
                dve.wait_ge(f_yT_ps, s.done(1))
                scaled(f_y[:, :], psF[s.slot(2)][:, :], f_rstd[:, 0], 8, f_rstd1, f_y_sb, s)

            def f_sum(s):
                dve.wait_ge(f_sc_ps, s.done(1))
                turned_sum(f_sT[:, :], psF[s.slot(2)][:, :], f_xT[:, s.slot(2)], f_yT_ps, f_sT_sb, s)

            def f_x1_rows(s):
                dve.wait_ge(g_xT_ps, s.done(2))
                dve.wait_ge(g_r_sb, s.done(2))
                scaled(f_x1[:, s.slot(2)], psF[s.slot(2)][:, :], f_rstd[:, 1], 8, f_rstd2, f_x1_sb, s)

            def g_sum(s):
                dve.wait_ge(g_out_sb, s.done(1))
                plus(g_r[:, :], psG[s.slot(2)][:, :], f_x1[:, s.slot(2)], g_o_ps, g_r_sb, s)

            g_variance = lambda s: variance(g_var[:, :], g_sq[:, :], 8, g_sq_sb, g_var_sb, s)
            g_recip = lambda s: reciprocal(g_rstd[:, :], g_std[:, :], g_std_sb, g_rstd_sb, s)

            def g_scale(s):
                dve.wait_ge(out_stored[s.slot(2)], s.done(2, 16, 2))
                scaled(g_out[:, s.slot(2)], g_r[:, :], g_rstd[:, :], 8, g_rstd_sb, g_out_sb, s)

            def m_ea(c):
                dve.wait_ge(m_T_ps, c.done())
                dve.wait_ge(m_hid_ps, c.done(1))
                V.tensor_copy(m_eaT[:, :], psE[c.slot(2)][0:TC * EF, 0:P]).then_inc(m_eaT_sb, 1)

            def scan(rows, c, data, done):
                first = c.k is None and c.base == 0
                carry = 0.0 if first else m_agg[0:rows, 1 - c.slot(2), EC - 1:EC]
                dve.wait_ge(done, c.done(1))
                V.tensor_tensor_scan(m_agg[0:rows, c.slot(2)], same[0:rows, c.slot(2)], data, carry, ALU.mult,
                                     ALU.add).then_inc(done, 1)

            def m_scan(c):
                dve.wait_ge(ends_in[c.slot(2)], c.done(0, 32, 2))
                dve.wait_ge(m_u_ps, c.done(2))
                dve.wait_ge(count_stored[c.slot(2)], c.done(2, 16, 2))
                dve.wait_ge(m_hid_sb, c.done())
                scan(H + 1, c, m_hid[:, :], m_agg_sb)

            n_variance1 = lambda c: variance(n_var[:, 0], n_sq_a[:, :], 8, n_sq1, n_var1, c)
            n_variance2 = lambda c: variance(n_var[:, 1], n_sq_b[:, :], 8, n_sq2, n_var2, c)
            n_recip1 = lambda c: reciprocal(n_rstd[:, 0], n_std[:, 0], n_std1, n_rstd1, c)
            n_recip2 = lambda c: reciprocal(n_rstd[:, 1], n_std[:, 1], n_std2, n_rstd2, c)

            def n_scale(c):
                dve.wait_ge(n_yT_ps, c.done(1))
                scaled(n_y[:, :], psM[c.slot(2)][:, :], n_rstd[:, 0], 8, n_rstd1, n_y_sb, c)

            def n_sum(c):
                dve.wait_ge(n_sc_ps, c.done(1))
                turned_sum(n_sT[:, :], psM[c.slot(2)][:, :], m_xT[:, c.slot(2)], n_yT_ps, n_sT_sb, c)

            def n_x1_rows(c):
                dve.wait_ge(x1_stored[c.slot(2)], c.done(2, 32, 2))
                scaled(n_x1[:, c.slot(2)], psM[c.slot(2)][:, :], n_rstd[:, 1], 8, n_rstd2, n_x1_sb, c)

            def phase1(s):
                edge(m_scan, s.back(1))
                dense(g_sum, s.back(3))
                edge(n_sum, s.back(2))
                dense(g_variance, s.back(3))
                dense(f_scale, s.back(1))
                edge(n_variance2, s.back(2))
                dense(f_sum, s.back(1))
                edge(n_recip2, s.back(2))
                edge(n_x1_rows, s.back(2))
                dense(f_variance1, s)
                edge(stage1, s.back(-2))
                dense(f_variance2, s.back(1))
                dense(g_recip, s.back(3))
                dense(f_recip2, s.back(1))
                dense(f_recip1, s)
                dense(f_x1_rows, s.back(1))
                edge(m_ea, s)
                dense(g_scale, s.back(3))
                edge(n_variance1, s.back(1))
                edge(n_recip1, s.back(1))
                edge(n_scale, s.back(1))

            all_steps(dve, 0, NCH, phase1, peel=1 + UNROLL)

            def stage2(c):
                if c.k is not None or c.base >= RING:
                    dve.wait_ge(slots_in[c.slot(2)], c.done(RING, 16 * TC, 2))
                V.tensor_copy(ix2[:, c.slot(RING)], edges[:, :, bass.ds(c.value(TC, 0), TC)]).then_inc(ix2_ready, 1)

            def rows_of(c):
                at = c.value(TC, 0)
                dve.wait_ge(slots_in[c.slot(2)], c.done(0, 16 * TC, 2))
                V.tensor_scalar(absent[:, :], slots[:, c.slot(2)], 0.0, None, ALU.is_lt).then_inc(absent_sb, 1)
                dve.wait_ge(absent_sb, c.done())
                V.scalar_tensor_tensor(away[:, :], ix2[:, c.slot(RING), ENUM], float(EP + 1), absent[:, :],
                                       ALU.add, ALU.mult).then_inc(away_sb, 1)
                if c.k is not None or c.base >= RING:
                    dve.wait_ge(q_er_in[c.slot(RING)], c.done(RING, 16 * TC, RING))
                dve.wait_ge(away_sb, c.done())
                V.tensor_tensor(rowix[:, c.slot(RING)], away[:, :], slots[:, c.slot(2)], ALU.add)
                V.tensor_tensor(rows2[:, bass.ds(at, TC)], away[:, :], slots[:, c.slot(2)], ALU.add).then_inc(rowix_ready, 1)

            def q_scan(c):
                dve.wait_ge(q_T_sb, c.done())
                dve.wait_ge(q_line_in[c.slot(2)], c.done(0, 32, 2))
                dve.wait_ge(q_mean_sb, c.done(2))
                scan(H, c, q_T[0:H, :], q_agg_sb)

            def mean(into, c, agg_sem, done):
                dve.wait_ge(agg_sem, c.done())
                V.tensor_tensor(into, m_agg[0:H, c.slot(2)], inv[:, c.slot(2)], ALU.mult).then_inc(done, 1)

            def q_average(c):
                dve.wait_ge(q_h_ps, c.done(1))
                mean(q_mean[:, :], c, q_agg_sb, q_mean_sb)

            written_out(dve, 0, 2, stage2)

            def between(s):
                phase1(s)
                c = s.back(Q0)
                stage2(c.back(-4))
                rows_of(c.back(-2))

            written_out(dve, NCH, Q0 - NCH, between)
            dve.wait_ge(counts_in, 16)
            V.reciprocal(counts[:, :], counts[:, :]).then_inc(counts_inv, 1)

            def phase2(s):
                c = s.back(Q0)
                dense(f_scale, s.back(1))
                edge(rows_of, c.back(-2))
                dense(f_sum, s.back(1))
                dense(g_sum, s.back(3))
                edge(q_scan, c.back(1))
                edge(q_average, c.back(1))
                dense(f_variance2, s.back(1))
                dense(f_recip2, s.back(1))
                dense(f_x1_rows, s.back(1))
                edge(stage2, c.back(-4))
                dense(g_variance, s.back(3))
                dense(f_variance1, s)
                dense(g_recip, s.back(3))
                dense(f_recip1, s)
                dense(g_scale, s.back(3))

            all_steps(dve, Q0, ND - Q0, phase2, peel=3 + UNROLL)
            written_out(dve, ND, DRAIN, phase2)

            def stage_h1(c):
                if c.k is not None or c.base >= RING:
                    dve.wait_ge(t_er_in[c.slot(RING)], c.done(RING, 16 * TC, RING))
                V.tensor_copy(ix_h1[:, c.slot(RING)], rows2[:, bass.ds(c.value(TC, 0), TC)]).then_inc(ix_h1_ready, 1)

            def stage_out(c):
                if c.k is not None or c.base >= RING:
                    dve.wait_ge(rows_scattered[c.slot(RING)], c.done(RING, 16 * TC, RING))
                V.tensor_copy(ix_out[:, c.slot(RING)], edges[:, SIDX, bass.ds(c.value(TC, 0), TC)]).then_inc(ix_out_ready, 1)

            def t_scan(c):
                dve.wait_ge(t_T_ps, c.done())
                dve.wait_ge(t_line_in[c.slot(2)], c.done(0, 32, 2))
                dve.wait_ge(t_mean_sb, c.done(2))
                scan(H, c, psM[c.slot(2)][0:H, :], t_agg_sb)

            def t_average(c):
                dve.wait_ge(t_o_ps, c.done(2))
                mean(t_T[0:H, c.slot(2)], c, t_agg_sb, t_mean_sb)

            def t_sum(c):
                dve.wait_ge(t_out_sb, c.done(1))
                dve.wait_ge(t_h1_in[c.slot(RING)], c.done(0, 32, RING))
                plus(t_r[:, :], psG[c.slot(2)][:, 0:TC * H], t_x1[:, c.slot(RING)], t_o_ps, t_r_sb, c)

            t_variance = lambda c: variance(t_var[:, :], t_sq[:, :], TC, t_sq_sb, t_var_sb, c)
            t_recip = lambda c: reciprocal(t_rstd[:, :], t_std[:, :], t_std_sb, t_rstd_sb, c)

            def t_scale(c):
                dve.wait_ge(rows_scattered[c.slot(RING)], c.done(RING, 16 * TC, RING))
                scaled(t_out[:, c.slot(RING)], t_r[:, :], t_rstd[:, :], TC, t_rstd_sb, t_out_sb, c)

            dve.wait_ge(rowix_ready, NCH)
            written_out(dve, 0, 2, stage_h1)

            def phase3(c):
                edge(t_scan, c)
                edge(t_variance, c.back(2))
                edge(t_average, c)
                edge(t_recip, c.back(2))
                edge(stage_h1, c.back(-2))
                edge(t_scale, c.back(2))
                edge(stage_out, c)
                edge(t_sum, c.back(1))

            all_steps(dve, 0, NCH, phase3, peel=1 + 2 * UNROLL)
            written_out(dve, NCH, 2, phase3)


_INS = ["x", "src", "dst", "edge_attr_16", "L0_gnn_W_m1", "L0_gnn_b_m1", "L0_gnn_W_m2", "L0_gnn_b_m2", "L0_gnn_W_u1",
        "L0_gnn_b_u1", "L0_gnn_W_u2", "L0_gnn_b_u2", "L0_gnn_gamma", "L0_gnn_beta", "L1_gnn_W_self1",
        "L1_gnn_W_neigh1", "L1_gnn_b1", "L1_gnn_W_self2", "L1_gnn_W_neigh2", "L1_gnn_b2"]


def kernel(**inputs):
    import numpy as np
    import concourse.bacc as bacc
    from concourse import mybir as mb
    from concourse.bass_utils import run_bass_kernel_spmd

    nc = bacc.Bacc("TRN2", target_bir_lowering=False, num_devices=1)
    arrays, args = {}, []
    for name in _INS:
        a = np.ascontiguousarray(inputs[name])
        arrays[f"in_{name}"] = a
        args.append(nc.dram_tensor(f"in_{name}", a.shape, mb.dt.from_np(a.dtype), kind="ExternalInput").ap())
    rows, cols = inputs["x"].shape
    out = nc.dram_tensor("out_rows", (rows, cols), mb.dt.float32, kind="ExternalOutput").ap()
    build_gnn(nc, *args, out)
    r = run_bass_kernel_spmd(nc, [arrays], core_ids=[0])
    return r.results[0]["out_rows"]
```

```python
from contextlib import ExitStack

import concourse.bass as bass
from concourse import mybir

P = 128
H = 64
EPS = 1e-5
BANK = 512
RING = 4
UNROLL = 4

ALU = mybir.AluOpType
ACT = mybir.ActivationFunctionType
F32 = mybir.dt.float32
BF16 = mybir.dt.bfloat16
I32 = mybir.dt.int32
AX_X = mybir.AxisListType.X


class Step:

    def __init__(self, eng, k, base, kept, stride=UNROLL):
        self.eng, self.k, self.base, self.kept, self.stride = eng, k, base, kept, stride

    def back(self, n):
        return Step(self.eng, self.k, self.base - n, self.kept, self.stride)

    def pair(self):
        return [Step(self.eng, self.k, 2 * self.base + i, self.kept, 2 * self.stride) for i in range(2)]

    def value(self, per_step, plus):
        add = per_step * self.base + plus
        if self.k is None:
            return add
        key = (per_step * self.stride, add)
        if key not in self.kept:
            self.kept[key] = self.eng.snap(self.k * key[0] + add)
        return self.kept[key]

    def done(self, lag=0, each=1, ring=1):
        add = each * ((self.base - lag) // ring + 1)
        if self.k is None:
            return max(add, 0)
        assert add > 0 and self.stride % ring == 0
        key = (each * self.stride // ring, add)
        if key not in self.kept:
            self.kept[key] = self.eng.snap(self.k * key[0] + add)
        return self.kept[key]

    def slot(self, ring):
        return self.base % ring


def all_steps(eng, first, count, body, peel):
    assert (count - peel) % UNROLL == 0
    for i in range(peel):
        body(Step(eng, None, first + i, {}))
    with eng.Fori(0, (count - peel) // UNROLL) as k:
        kept = {}
        for i in range(UNROLL):
            body(Step(eng, k, first + peel + i, kept))


def written_out(eng, first, count, body):
    for i in range(count):
        body(Step(eng, None, first + i, {}))


def within(count):
    def run(stage, c):
        if c.k is not None or 0 <= c.base < count:
            stage(c)
    return run


def build_gnn(nc, x, src, dst, edge_attr, W_m1, b_m1, W_m2, b_m2, W_u1, b_u1, W_u2, b_u2, gamma, beta,
              W_self1, W_neigh1, b_1, W_self2, W_neigh2, b_2, out):
    N = x.shape[0]
    E = src.shape[0]
    EF = edge_attr.shape[1]
    TC = 4
    EC = TC * P
    NCH = -(-E // EC)
    EP = NCH * EC
    NT = EP // P
    TA = NT // 2
    DT, DT3 = 6, 4
    DC, DC3 = DT * P, DT3 * P
    DW = DT * H
    assert NT % 2 == 0 and TA <= P and E % 100 == 0
    NTP = NT + 2 * TC
    Q0 = NCH + 3
    T0 = Q0 + NCH + 1
    NPAIR = (NCH + 1) // 2
    ND = T0 + NPAIR + -(-(N - T0 * DC - NPAIR * DC3) // DC)
    OVER = (ND - NPAIR) * DC + NPAIR * DC3 - N
    assert 0 <= OVER < DC and ND > T0 + NPAIR
    END = ND + 3
    LOOPED3 = 1 + (NPAIR - 4) // UNROLL * UNROLL
    assert END >= T0 + NPAIR and ND % 2 == 1 and (NCH - 1) * EC <= E
    LATE = Q0
    HEAD = NCH - 5 * UNROLL
    dense, edge = within(ND), within(NCH)
    OP, PIECES, LEFT = 125, 10, 5
    OT, OW = E // OP, E // PIECES
    OWP = LEFT << (OW // LEFT - 1).bit_length()
    assert OP * OT == E and PIECES * OW == E and E % 4 == 0 and E < 1 << 22
    NOWHERE = 1 << 20
    assert N < NOWHERE

    def scratch(name, shape, dt):
        return nc.dram_tensor(name, shape, dt, kind="Internal").ap()

    dst_line = scratch("dst_line", (EP + 2,), I32)
    src_line = scratch("src_line", (EP,), I32)
    ea_rows = scratch("ea_rows", (EP, EF), F32)
    same_line = scratch("same_line", (EP,), F32)
    count_line = scratch("count_line", (EP,), F32)
    inv_line = scratch("inv_line", (EP,), F32)
    row_of_node = scratch("row_of_node", (N, 1), I32)
    x1_rows = scratch("x1_rows", (2 * EP, H), F32)
    h1_rows = scratch("h1_rows", (2 * EP, H), F32)

    with ExitStack() as ctx:
        def sb(name, shape, dt=F32):
            return ctx.enter_context(nc.sbuf_tensor(name, shape, dt))

        def sem(name):
            return ctx.enter_context(nc.semaphore(name))

        def sems(name, n):
            return [sem(f"{name}{i}") for i in range(n)]

        def bank(name):
            return ctx.enter_context(nc.psum_tensor(name, [P, BANK], F32))

        psF = [bank("psF0"), bank("psF1")]
        psG = [bank("psG0"), bank("psG1")]
        psM = [bank("psM0"), bank("psM1")]
        psE = [bank("psE0"), bank("psE1")]

        ident = sb("ident", [P, P])
        bd_c = sb("bd_c", [P, P])
        bd_u1 = sb("bd_u1", [P, P])
        bd_u2 = sb("bd_u2", [P, P])
        bd_s1 = sb("bd_s1", [P, P])
        bd_s2 = sb("bd_s2", [P, P])
        w_m1 = sb("w_m1", [P, H])
        w_m1e = sb("w_m1e", [TC * EF, TC, H])
        w_m2 = sb("w_m2", [H + 1, H])
        w_m2T = sb("w_m2T", [H, H + 1])
        w_u1n = sb("w_u1n", [H, H])
        w_comb = sb("w_comb", [H + 1, P])
        w_n1 = sb("w_n1", [H, P])
        w_l2 = sb("w_l2", [P, H])
        cen = sb("cen", [P, 6, H])
        cmean = sb("cmean", [P, 6])
        bm1_c = sb("bm1_c", [H, 1])
        bu1_c = sb("bu1_c", [P, 1])
        b1_c = sb("b1_c", [P, 1])
        eps_c = sb("eps_c", [P, 1])
        gam_c = sb("gam_c", [P, 1])
        brow = sb("brow", [96, 4, H])
        brest = sb("brest", [96, 4, H])
        bpart = sb("bpart", [96, 4, H], BF16)
        bmid = sb("bmid", [96, 4, H], BF16)
        bias3 = sb("bias3", [96, 4, BANK], BF16)
        pick = sb("pick", [96, P], BF16)

        raw = sb("raw", [TA, 4, 2, P], I32)
        rowf = sb("rowf", [TA, 4, 2, P])
        notlast = sb("notlast", [TA, 2, P])
        edges = sb("edges", [P, 4, NTP], I32)
        SRC, DSTG, SIDX, ENUM = range(4)
        rows2 = sb("rows2", [P, NTP], I32)
        fill = sb("fill", [P, N // 80], I32)
        zpad = sb("zpad", [P, 16], I32)

        pair_a, pair_b = sb("pair_a", [OP, OT], I32), sb("pair_b", [OP, OT], I32)
        falls, falls_lane = sb("falls", [OP, OT]), sb("falls_lane", [P, P])
        falls_any, falls_flag = sb("falls_any", [1, 1]), sb("falls_flag", [1, 1], I32)
        held = sb("held", [P, NCH * TC * H])
        taken = [0]

        def part(n):
            taken[0] += n
            return held[0:OP, taken[0] - n:taken[0]]

        o_dst, o_src, o_key, o_pos = part(OT).bitcast(I32), part(OT).bitcast(I32), part(OT), part(OT)
        o_rank = part(OT * LEFT).rearrange("p (t n) -> p t n", n=LEFT)
        line_raw, line_key, line_pos, line_hit = part(OW).bitcast(I32), part(OW), part(OW), part(OWP)
        assert taken[0] <= NCH * TC * H
        o_ea, o_row = sb("o_ea", [OP, OT * EF]), sb("o_row", [OP, OT, 2], I32)
        s_key, s_int, s_ea = sb("s_key", [OP, 2]), sb("s_int", [OP, 4], I32), sb("s_ea", [OP, EF])

        xd = sb("xd", [P, 2, DW])
        f_xT = sb("f_xT", [P, 2, DW])
        f_U, f_sT, f_sq_a, f_sq_b, f_y = (sb(n, [P, DW]) for n in ("f_U", "f_sT", "f_sq_a", "f_sq_b", "f_y"))
        f_x1 = sb("f_x1", [P, 2, DW])
        f_var, f_std, f_rstd = (sb(n, [P, 2, DT]) for n in ("f_var", "f_std", "f_rstd"))
        g_xT, g_h, g_r, g_sq = (sb(n, [P, DW]) for n in ("g_xT", "g_h", "g_r", "g_sq"))
        g_out = sb("g_out", [P, 2, DW])
        g_var, g_std, g_rstd = (sb(n, [P, DT]) for n in ("g_var", "g_std", "g_rstd"))

        er = sb("er", [P, RING, BANK])
        ea = sb("ea", [P, 2, TC * EF])
        same = sb("same", [H + 1, 2, EC])
        inv = sb("inv", [H, 2, EC])
        counts = sb("counts", [TA, 2 * P])
        m_xT = sb("m_xT", [P, 2, BANK])
        m_eaT = sb("m_eaT", [TC * EF, P])
        m_hid = sb("m_hid", [H + 1, EC])
        m_agg = sb("m_agg", [H + 1, 2, EC])
        n_U, n_sT, n_sq_a, n_sq_b, n_y = (sb(n, [P, BANK]) for n in ("n_U", "n_sT", "n_sq_a", "n_sq_b", "n_y"))
        n_x1 = sb("n_x1", [P, 2, BANK])
        n_var, n_std, n_rstd = (sb(n, [P, 2, 8]) for n in ("n_var", "n_std", "n_rstd"))
        ix1 = sb("ix1", [P, RING, 4, TC], I32)
        ix2 = sb("ix2", [P, RING, 4, TC], I32)
        last_dst, last_chunk = sb("last_dst", [1, NCH], I32), sb("last_chunk", [1, NCH])
        last_narrow = sb("last_narrow", [1, NCH])
        pairs_below, stored_by = sb("pairs_below", [1, NCH], I32), sb("stored_by", [1, 2, NCH], I32)
        ix_h1 = sb("ix_h1", [P, RING, TC], I32)
        ix_out = sb("ix_out", [P, RING, TC], I32)
        slots = sb("slots", [P, RING, TC], I32)
        absent = sb("absent", [P, TC])
        away = sb("away", [P, TC])
        rowix = sb("rowix", [P, RING, TC], I32)
        q_T, q_mean = sb("q_T", [P, BANK]), sb("q_mean", [H, EC])
        q_h = sb("q_h", [P, 2, BANK])
        t_T = sb("t_T", [P, 2, BANK])
        t_x1 = sb("t_x1", [P, RING, TC * H])
        t_r, t_sq = sb("t_r", [P, 2, TC * H]), sb("t_sq", [P, 2, TC * H])
        t_var, t_std, t_rstd = (sb(n, [P, 2, TC]) for n in ("t_var", "t_std", "t_rstd"))
        t_out = sb("t_out", [P, RING, TC * H])

        weights_in, lines_in, pads_in = sem("weights_in"), sem("lines_in"), sem("pads_in")
        raw_in, same_out, fill_out = sem("raw_in"), sem("same_out"), sem("fill_out")
        pool_consts, zeroed, setup_dve = sem("pool_consts"), sem("zeroed"), sem("setup_dve")
        rowf_ready, edgesT, edges_ready = sem("rowf_ready"), sem("edgesT"), sem("edges_ready")
        pads_ready, fill_ready = sem("pads_ready"), sem("fill_ready")

        lines_cleared, pool_cleared, dve_cleared = sem("lines_cleared"), sem("pool_cleared"), sem("dve_cleared")

        pairs_in, falls_ready, falls_T = sem("pairs_in"), sem("falls_ready"), sem("falls_T")
        flag_ready, ordered = sem("flag_ready"), sem("ordered")
        stored_by_ready, attrs_in = sem("stored_by_ready"), sem("attrs_in")
        own_in, rows_moved = sem("own_in"), sem("rows_moved")
        w_m2T_ps, w_m2T_sb, w_comb_ps, w_comb_sb = map(sem, "w_m2T_ps w_m2T_sb w_comb_ps w_comb_sb".split())

        xd_in = sems("xd_in", 2)
        f_xT_ps, f_xT_sb, f_u_ps, f_U_sb, f_r_ps, f_sq1, f_var1, f_std1, f_rstd1 = map(
            sem, "f_xT_ps f_xT_sb f_u_ps f_U_sb f_r_ps f_sq1 f_var1 f_std1 f_rstd1".split())
        f_y_sb, f_yT_ps, f_sT_sb, f_sc_ps, f_sq2, f_var2, f_std2, f_rstd2, f_x1_sb = map(
            sem, "f_y_sb f_yT_ps f_sT_sb f_sc_ps f_sq2 f_var2 f_std2 f_rstd2 f_x1_sb".split())
        g_xT_ps, g_xT_sb, g_h_ps, g_h_sb, g_o_ps, g_r_sb, g_sq_sb, g_var_sb, g_std_sb, g_rstd_sb, g_out_sb = map(
            sem, "g_xT_ps g_xT_sb g_h_ps g_h_sb g_o_ps g_r_sb g_sq_sb g_var_sb g_std_sb g_rstd_sb g_out_sb".split())
        out_stored = sems("out_stored", 2)

        ix1_ready, er_in, ends_in = sem("ix1_ready"), sems("er_in", RING), sems("ends_in", 2)
        rows_set = sems("rows_set", RING)
        m_T_ps, m_xT_sb, m_eaT_sb, m_hid_ps, m_hid_sb, m_agg_sb, m_u_ps = map(
            sem, "m_T_ps m_xT_sb m_eaT_sb m_hid_ps m_hid_sb m_agg_sb m_u_ps".split())
        count_stored, counts_in, counts_inv, inv_stored = (
            sems("count_stored", 2), sem("counts_in"), sem("counts_inv"), sem("inv_stored"))
        n_U_sb, n_r_ps, n_sq1, n_var1, n_std1, n_rstd1, n_y_sb = map(
            sem, "n_U_sb n_r_ps n_sq1 n_var1 n_std1 n_rstd1 n_y_sb".split())
        n_yT_ps, n_sT_sb, n_sc_ps, n_sq2, n_var2, n_std2, n_rstd2, n_x1_sb = map(
            sem, "n_yT_ps n_sT_sb n_sc_ps n_sq2 n_var2 n_std2 n_rstd2 n_x1_sb".split())
        x1_stored = sems("x1_stored", 2)

        ix2_ready, absent_sb, away_sb, rows_found, rowix_ready = map(
            sem, "ix2_ready absent_sb away_sb rows_found rowix_ready".split())
        slots_in = sems("slots_in", RING)
        q_er_in, q_x1_in, q_line_in = sems("q_er_in", RING), sems("q_x1_in", RING), sems("q_line_in", 2)
        q_T_ps, q_T_sb, q_agg_sb, q_mean_sb, q_h_ps, q_h_sb = map(
            sem, "q_T_ps q_T_sb q_agg_sb q_mean_sb q_h_ps q_h_sb".split())
        h1_stored = sems("h1_stored", 2)

        ix_h1_ready, rows_staged = sem("ix_h1_ready"), sem("rows_staged")
        t_er_in, t_h1_in, t_line_in = sems("t_er_in", RING), sems("t_h1_in", RING), sems("t_line_in", 2)
        t_T_ps, t_T_sb, t_agg_sb, t_mean_sb, t_o_ps, t_r_sb, t_sq_sb, t_var_sb, t_std_sb, t_rstd_sb, t_out_sb = map(
            sem, "t_T_ps t_T_sb t_agg_sb t_mean_sb t_o_ps t_r_sb t_sq_sb t_var_sb t_std_sb t_rstd_sb t_out_sb".split())
        rows_scattered = sems("rows_scattered", RING)

        def width(s):
            return (DT3 if T0 <= s.base < T0 + NPAIR else DT) * H

        def tiles(ap):
            return ap.rearrange("p (t f) -> p t f", f=H)

        def halves(ap):
            return ap.rearrange("p (t h f) -> p t h f", h=2, f=H)

        def per_row(ap, n):
            return ap.unsqueeze(2).to_broadcast([P, n, H])

        def one_line(ap):
            return ap.rearrange("(a n) -> a n", a=1)

        col = lambda v: v.rearrange("(n a) -> n a", a=1)

        block = ctx.enter_context(nc.Block())

        @block.sync
        def _(sp):
            ab = dict(b=100)
            lanes = lambda ap: ap.rearrange("(p t) -> p t", p=OP)
            for half, at in enumerate((0, E // 2 - 1)):
                into = slice(half * OT // 2, (half + 1) * OT // 2)
                sp.dma_start(pair_a[:, into], lanes(dst[at:at + E // 2])).then_inc(pairs_in, 16)
                sp.dma_start(pair_b[:, into], lanes(dst[at + 1:at + 1 + E // 2])).then_inc(pairs_in, 16)
            sp.dma_start(dst_line[1:E + 1].rearrange("(b n) -> b n", **ab), dst.rearrange("(b n) -> b n", **ab)).then_inc(lines_in, 16)
            sp.dma_start(src_line[0:E].rearrange("(b n) -> b n", **ab), src.rearrange("(b n) -> b n", **ab)).then_inc(lines_in, 16)
            sp.wait_ge(pads_ready, 3)
            NP_ = EP - E
            sp.dma_start(one_line(dst_line[0:1]), zpad[0:1, 1:2]).then_inc(pads_in, 16)
            sp.dma_start(dst_line[E + 1:EP + 2].rearrange("(n a) -> n a", a=1), zpad[0:NP_ + 1, 1:2]).then_inc(pads_in, 16)
            sp.dma_start(src_line[E:EP].rearrange("(n a) -> n a", a=1), zpad[0:NP_, 0:1]).then_inc(pads_in, 16)
            sp.dma_start(ea_rows[E:EP, :], fill[0:NP_, 0:EF].bitcast(F32)).then_inc(pads_in, 16)
            sp.dma_start(ea_rows[0:E, :].rearrange("(b n) f -> b (n f)", **ab), edge_attr.rearrange("(b n) f -> b (n f)", **ab)).then_inc(attrs_in, 16)
            sp.wait_ge(lines_in, 32)
            sp.wait_ge(pads_in, 64)
            sp.wait_ge(ordered, 1)
            line = lambda ap: ap.rearrange("(a q p) -> q a p", a=2, p=P)
            for n, s in enumerate((src_line[0:EP], dst_line[1:EP + 1], dst_line[0:EP], dst_line[2:EP + 2])):
                sp.dma_start(raw[:, n], line(s)).then_inc(raw_in, 16)
            with nc.allow_non_contiguous_dma(reason="one number for each edge chunk"):
                sp.dma_start(last_dst[:, :], dst_line[1:EP + 1].rearrange("(c n) -> n c", n=EC)[EC - 1:EC, :]).then_inc(raw_in, 16)
            sp.wait_ge(zeroed, 1)
            for lo in (0, H):
                sp.dma_start(bd_u1[lo:lo + H, lo:lo + H], W_u1[0:H, :]).then_inc(weights_in, 16)
                sp.dma_start(bd_s1[lo:lo + H, lo:lo + H], W_self1).then_inc(weights_in, 16)
                sp.dma_start(cen[lo:lo + H, 0], W_u2).then_inc(weights_in, 16)
                sp.dma_start(cen[lo:lo + H, 1], W_self2).then_inc(weights_in, 16)
                sp.dma_start(bu1_c[lo:lo + H, :], col(b_u1)).then_inc(weights_in, 16)
                sp.dma_start(b1_c[lo:lo + H, :], col(b_1)).then_inc(weights_in, 16)
            sp.dma_start(cen[0:H, 2], W_neigh2).then_inc(weights_in, 16)
            sp.dma_start(cen[H:P, 2], W_self2).then_inc(weights_in, 16)
            for n, v in enumerate((b_u2, beta, b_2)):
                sp.dma_start(cen[:, 3 + n], v.partition_broadcast(P)).then_inc(weights_in, 16)
            sp.dma_start(brow[:, 2], b_1.partition_broadcast(96)).then_inc(weights_in, 16)
            for lo in (0, H):
                sp.dma_start(gam_c[lo:lo + H, :], col(gamma)).then_inc(weights_in, 16)
            sp.dma_start(w_m1[0:H, :], W_m1[H:2 * H, :]).then_inc(weights_in, 16)
            sp.dma_start(w_m1[H:P, :], W_m1[0:H, :]).then_inc(weights_in, 16)
            for t in range(TC):
                sp.dma_start(w_m1e[EF * t:EF * (t + 1), t], W_m1[2 * H:2 * H + EF, :]).then_inc(weights_in, 16)
            sp.dma_start(w_m2[0:H, :], W_m2).then_inc(weights_in, 16)
            sp.dma_start(w_m2[H:H + 1, :], one_line(b_m2)).then_inc(weights_in, 16)
            sp.dma_start(w_u1n[:, :], W_u1[H:2 * H, :]).then_inc(weights_in, 16)
            sp.dma_start(w_n1[:, H:P], W_neigh1).then_inc(weights_in, 16)
            sp.dma_start(bm1_c[:, :], col(b_m1)).then_inc(weights_in, 16)
            sp.wait_ge(fill_ready, 1)
            sp.dma_start(row_of_node.rearrange("(b n) a -> b (n a)", b=80), fill[0:80, :]).then_inc(fill_out, 16)
            sp.wait_ge(rowf_ready, 1)
            sp.dma_start(line(same_line), rowf[:, 3]).then_inc(same_out, 16)
            sp.wait_ge(same_out, 16)

            def dense_rows(dram, s):
                over = OVER if s.base >= LATE else 0
                if s.base < T0:
                    at, rows = s.value(DC, -over), DC
                elif s.base < T0 + NPAIR:
                    at, rows = s.value(DC3, T0 * (DC - DC3) - over), DC3
                else:
                    at, rows = s.value(DC, -NPAIR * (DC - DC3) - over), DC
                return dram[bass.ds(at, rows), :].rearrange("(p t) f -> p (t f)", p=P)

            def edge_rows(dram, c, base):
                return dram[bass.ds(c.value(EC, base), EC), :].rearrange("(t p) f -> p t f", p=P)

            def edge_line(dram, c):
                return one_line(dram)[:, bass.ds(c.value(EC, 0), EC)]

            def to_all(line, n):
                return line.rearrange("a n -> (a n)").partition_broadcast(n)

            def load_dense(s):
                at = dense_rows(x, s)
                sp.wait_ge(f_xT_ps, s.done(2))
                sp.dma_start(xd[:, s.slot(2), 0:width(s)], at).then_inc(xd_in[s.slot(2)], 16)

            def store_dense(s):
                at = dense_rows(out, s)
                sp.wait_ge(g_out_sb, s.done())
                if s.base == LATE:
                    sp.wait_ge(out_stored[(LATE - 1) % 2], 16 * ((LATE - 1) // 2 + 1))
                sp.dma_start(at, g_out[:, s.slot(2), 0:width(s)]).then_inc(out_stored[s.slot(2)], 16)

            def load_ea(c):
                at = edge_rows(ea_rows, c, 0)
                sp.wait_ge(m_T_ps, c.done(2))
                sp.dma_start(ea[:, c.slot(2)].rearrange("p (t f) -> p t f", f=EF), at).then_inc(ends_in[c.slot(2)], 16)

            def load_same(c):
                at = edge_line(same_line, c)
                sp.wait_ge(m_agg_sb, c.done(2))
                sp.sem_inc(lines_cleared, 1)
                sp.dma_start(same[:, c.slot(2)], to_all(at, H + 1)).then_inc(ends_in[c.slot(2)], 16)

            def store_count(c):
                at = edge_line(count_line, c)
                sp.wait_ge(m_agg_sb, c.done())
                sp.dma_start(at, m_agg[H:H + 1, c.slot(2)]).then_inc(count_stored[c.slot(2)], 16)

            def store_ends(table, rows, done, stored, c):
                at_d, at_s = edge_rows(table, c, 0), edge_rows(table, c, EP)
                v = halves(rows[:, c.slot(2)])
                sp.wait_ge(done, c.done())
                sp.dma_start(at_s, v[:, :, 0]).then_inc(stored[c.slot(2)], 16)
                sp.dma_start(at_d, v[:, :, 1]).then_inc(stored[c.slot(2)], 16)

            store_x1 = lambda c: store_ends(x1_rows, n_x1, n_x1_sb, x1_stored, c)
            store_h1 = lambda c: store_ends(h1_rows, q_h, q_h_sb, h1_stored, c)

            sp.wait_ge(attrs_in, 16)
            for first in range(2):
                load_dense(Step(sp, None, first, {}))
                load_ea(Step(sp, None, first, {}))
            load_same(Step(sp, None, 0, {}))

            def phase1(s):
                dense(load_dense, s.back(-2))
                edge(load_same, s.back(-1))
                edge(store_count, s.back(1))
                edge(store_x1, s.back(2))
                edge(load_ea, s.back(-2))
                dense(store_dense, s.back(3))

            all_steps(sp, 0, NCH - UNROLL, phase1, peel=1 + UNROLL)
            written_out(sp, NCH - UNROLL, UNROLL + 1, phase1)
            pair = lambda ap: ap.rearrange("(q n) -> q n", q=TA)
            for q in range(2):
                sp.wait_ge(count_stored[q], 16 * ((NCH + 1 - q) // 2))
            sp.dma_start(counts[:, :], pair(count_line)).then_inc(counts_in, 16)
            written_out(sp, NCH + 1, Q0 - NCH - 1, phase1)
            sp.wait_ge(counts_inv, 1)
            sp.dma_start(pair(inv_line), counts[:, :]).then_inc(inv_stored, 16)

            def load_lines(c, into, agg_done):
                same_at, inv_at = edge_line(same_line, c), edge_line(inv_line, c)
                sp.wait_ge(agg_done, c.done(2))
                sp.sem_inc(lines_cleared, 1)
                sp.dma_start(same[0:H, c.slot(2)], to_all(same_at, H)).then_inc(into[c.slot(2)], 16)
                sp.dma_start(inv[:, c.slot(2)], to_all(inv_at, H)).then_inc(into[c.slot(2)], 16)

            q_lines = lambda c: load_lines(c, q_line_in, q_mean_sb)
            t_lines = lambda c: load_lines(c, t_line_in, t_mean_sb)

            def load_x1(c):
                at = edge_rows(x1_rows, c, 0)
                sp.wait_ge(q_T_ps, c.done(RING))
                sp.dma_start(halves(er[:, c.slot(RING)])[:, :, 1], at).then_inc(q_x1_in[c.slot(RING)], 16)

            for q in range(2):
                sp.wait_ge(x1_stored[q], 32 * ((NCH + 1 - q) // 2))
            written_out(sp, 0, 3, load_x1)
            sp.wait_ge(inv_stored, 16)
            written_out(sp, 0, 2, q_lines)

            def only_dense(s):
                dense(load_dense, s.back(-2))
                dense(store_dense, s.back(3))

            def phase2(s):
                c = s.back(Q0)
                dense(load_dense, s.back(-2))
                edge(store_h1, c.back(2))
                edge(load_x1, c.back(-3))
                if c.base > 0:
                    edge(q_lines, c.back(-1))
                dense(store_dense, s.back(3))

            all_steps(sp, Q0, NCH - UNROLL, phase2, peel=1 + UNROLL)
            written_out(sp, Q0 + NCH - UNROLL, UNROLL - 1, phase2)
            written_out(sp, NCH - 3, 3, store_h1)
            written_out(sp, Q0 + NCH - 1, T0 - Q0 - NCH, only_dense)
            for q in range(2):
                sp.wait_ge(h1_stored[q], 32 * ((NCH + 1 - q) // 2))

            def load_h1(c):
                at = edge_rows(h1_rows, c, 0)
                sp.wait_ge(t_T_ps, c.done(RING))
                sp.dma_start(halves(er[:, c.slot(RING)])[:, :, 1], at).then_inc(t_h1_in[c.slot(RING)], 16)

            def load_t_x1(c):
                at = edge_rows(x1_rows, c, 0)
                sp.wait_ge(t_r_sb, c.done(RING))
                sp.dma_start(tiles(t_x1[:, c.slot(RING)]), at).then_inc(t_h1_in[c.slot(RING)], 16)

            def load_pair(v):
                A, B = v.pair()
                for c in (A, B):
                    edge(load_h1, c)
                for c in (A, B):
                    edge(load_t_x1, c)

            def load_pair_lines(v):
                A, B = v.pair()
                for c in (A, B):
                    edge(t_lines, c)

            load_pair(Step(sp, None, 0, {}))
            load_pair_lines(Step(sp, None, 0, {}))
            written_out(sp, T0 - 1, 1, only_dense)

            def phase3(s):
                load_pair(s.back(T0 - 1))
                load_pair_lines(s.back(T0 - 1))
                dense(load_dense, s.back(-2))
                dense(store_dense, s.back(3))

            all_steps(sp, T0, LOOPED3, phase3, peel=1 + UNROLL)
            written_out(sp, T0 + LOOPED3, END - T0 - LOOPED3, phase3)

        @block.gpsimd
        def _(pool):
            nc.gpsimd.memset(zpad[:, 0:1], 0).then_inc(pads_ready, 1)
            nc.gpsimd.memset(zpad[:, 1:2], -1).then_inc(pads_ready, 1)
            nc.gpsimd.memset(ident[:, :], 0.0).then_inc(pool_consts, 1)
            pool.wait_ge(pool_consts, 1)
            nc.gpsimd.affine_select(out=ident[:, :], in_=ident[:, :], compare_op=ALU.not_equal, fill=1.0, base=0,
                                    pattern=[[-1, P]], channel_multiplier=1).then_inc(pool_consts, 1)
            nc.gpsimd.iota(edges[:, ENUM, :], pattern=[[P, NTP]], base=0, channel_multiplier=1).then_inc(pool_consts, 1)

            bound_of = {n: pool.to_reg(n) for n in (N - 1, 2 * EP - 1, EP)}

            def order_edges():
                G = nc.gpsimd
                lanes = dict(p=OP)
                pool.dma_start(o_dst[:, :], dst.rearrange("(p t) -> p t", **lanes)).then_inc(own_in, 16)
                pool.dma_start(o_src[:, :], src.rearrange("(p t) -> p t", **lanes)).then_inc(own_in, 16)
                pool.dma_start(o_ea[:, :], edge_attr.rearrange("(p t) f -> p (t f)", **lanes)).then_inc(own_in, 16)
                G.iota(o_row[:, :, 0], pattern=[[1, OT]], base=0, channel_multiplier=OT)
                G.iota(line_raw[:, :], pattern=[[1, OW]], base=0, channel_multiplier=0)
                G.memset(line_hit[:, :], 0.0)
                G.memset(o_rank[:, :, :], 0.0)
                pool.drain()
                G.tensor_copy(o_pos[:, :], o_row[:, :, 0])
                G.tensor_copy(line_pos[:, :], line_raw[:, :])
                pool.wait_ge(own_in, 48)
                G.tensor_copy(o_key[:, :], o_dst[:, :])
                pool.drain()
                with pool.Fori(0, PIECES) as j:
                    pool.dma_start(line_raw[:, :], dst[bass.ds(j * OW, OW)].partition_broadcast(OP)).then_inc(own_in, 16)
                    pool.wait_ge(own_in, pool.snap(j * 16 + 16 + 48))
                    pool.sem_inc(pool_cleared, 1)
                    G.tensor_copy(line_key[:, :], line_raw[:, :])
                    pool.drain()
                    with pool.Fori(0, OT) as t:
                        G.tensor_copy(s_key[:, 0:1], o_key[:, bass.ds(t, 1)])
                        G.tensor_copy(s_key[:, 1:2], o_pos[:, bass.ds(t, 1)])
                        pool.drain()
                        G.tensor_scalar(line_hit[:, 0:OW], line_pos[:, :], s_key[:, 1:2], 0.5, ALU.is_lt, ALU.mult)
                        pool.drain()
                        G.tensor_tensor(line_hit[:, 0:OW], line_key[:, :], line_hit[:, 0:OW], ALU.subtract)
                        pool.drain()
                        G.tensor_scalar(line_hit[:, 0:OW], line_hit[:, 0:OW], s_key[:, 0:1], None, ALU.is_lt)
                        pool.drain()
                        n = OWP
                        while n > LEFT:
                            n //= 2
                            G.tensor_tensor(line_hit[:, 0:n], line_hit[:, 0:n], line_hit[:, n:2 * n], ALU.add)
                            pool.drain()
                        G.tensor_tensor(o_rank[:, bass.ds(t, 1), :], o_rank[:, bass.ds(t, 1), :],
                                        line_hit[:, 0:LEFT].unsqueeze(1), ALU.add)
                        pool.drain()
                    G.tensor_scalar(o_pos[:, :], o_pos[:, :], -float(OW), None, ALU.add)
                    pool.drain()
                for n in range(1, LEFT):
                    G.tensor_tensor(o_rank[:, :, 0], o_rank[:, :, 0], o_rank[:, :, n], ALU.add)
                    pool.drain()
                G.tensor_copy(o_row[:, :, 0], o_rank[:, :, 0])
                G.tensor_scalar(o_row[:, :, 1], o_rank[:, :, 0], 1.0, None, ALU.add)
                pool.drain()
                pool.wait_ge(lines_in, 32)
                pool.wait_ge(attrs_in, 16)
                with pool.Fori(0, OT) as t:
                    G.tensor_copy(s_int[:, 0:2], o_row[:, bass.ds(t, 1), :])
                    G.tensor_copy(s_int[:, 2:3], o_src[:, bass.ds(t, 1)])
                    G.tensor_copy(s_int[:, 3:4], o_dst[:, bass.ds(t, 1)])
                    G.tensor_copy(s_ea[:, :], o_ea[:, bass.ds(t * EF, EF)])
                    pool.drain()
                    for table, ix, rows in ((col(src_line), 0, s_int[:, 2:3]), (col(dst_line), 1, s_int[:, 3:4]),
                                            (ea_rows, 0, s_ea[:, :])):
                        pool.indirect_dma_start(table, bass.IndirectOffsetOnAxis(s_int[:, ix:ix + 1], 0), rows, None,
                                                bounds_check=bound_of[EP], oob_is_err=False).then_inc(rows_moved, 16)
                    pool.wait_ge(rows_moved, pool.snap(t * 48 + 48))
                    pool.sem_inc(pool_cleared, 1)

            def gather(into, table, index, bound, s):
                pool.indirect_dma_start(into, None, table, bass.IndirectOffsetOnAxis(index, 0),
                                        bounds_check=bound_of[bound], oob_is_err=False).then_inc(s, 16)

            def landed(stored, each, ring, steps=NCH):
                for r in range(ring):
                    pool.wait_ge(stored[r], each * ((steps - 1 - r) // ring + 1))

            pool.wait_ge(flag_ready, 1)
            falling = pool.value_load(falls_flag[0:1, 0:1], min_val=0, max_val=1)
            with pool.If(falling > 0):
                order_edges()
                pool.sem_inc(pool_cleared, 1)
            with pool.Else():
                pool.sem_inc(pool_cleared, 1)
            pool.sem_inc(ordered, 1)

            def phase1(c):
                v, ix, r = halves(er[:, c.slot(RING)]), ix1[:, c.slot(RING)], c.slot(RING)
                pool.wait_ge(ix1_ready, c.done())
                pool.wait_ge(m_T_ps, c.done(RING))
                pool.sem_inc(pool_cleared, 1)
                for t in range(TC):
                    gather(v[:, t, 0], x, ix[:, SRC, t:t + 1], N - 1, er_in[r])
                    gather(v[:, t, 1], x, ix[:, DSTG, t:t + 1], N - 1, er_in[r])
                if c.k is None and c.base == 0:
                    pool.wait_ge(fill_out, 16)
                for t in range(TC):
                    pool.indirect_dma_start(row_of_node, bass.IndirectOffsetOnAxis(ix[:, SIDX, t:t + 1], 0),
                                            ix[:, ENUM, t:t + 1], None, bounds_check=bound_of[N - 1],
                                            oob_is_err=False).then_inc(rows_set[r], 16)

            all_steps(pool, 0, NCH, phase1, peel=1 + UNROLL)
            landed(rows_set, 16 * TC, RING)

            def find_rows(c):
                pool.wait_ge(ix2_ready, c.done())
                pool.wait_ge(rows_found, c.done(RING))
                pool.sem_inc(pool_cleared, 1)
                for t in range(TC):
                    gather(slots[:, c.slot(RING), t:t + 1], row_of_node, ix2[:, c.slot(RING), SRC, t:t + 1], N - 1, slots_in[c.slot(RING)])

            written_out(pool, 0, RING, find_rows)
            landed(x1_stored, 32, 2)

            def phase2(c):
                pool.wait_ge(rowix_ready, c.done())
                pool.wait_ge(q_T_ps, c.done(RING))
                pool.sem_inc(pool_cleared, 1)
                for t in range(TC):
                    gather(halves(er[:, c.slot(RING)])[:, t, 0], x1_rows, rowix[:, c.slot(RING), t:t + 1], 2 * EP - 1,
                           q_er_in[c.slot(RING)])
                edge(find_rows, c.back(-RING))

            all_steps(pool, 0, NCH - UNROLL, phase2, peel=1 + UNROLL)
            written_out(pool, NCH - UNROLL, UNROLL, phase2)

            def gather_h1(c):
                pool.wait_ge(ix_h1_ready, c.done())
                pool.wait_ge(t_T_ps, c.done(RING))
                pool.sem_inc(pool_cleared, 1)
                for t in range(TC):
                    gather(halves(er[:, c.slot(RING)])[:, t, 0], h1_rows, ix_h1[:, c.slot(RING), t:t + 1], 2 * EP - 1,
                           t_er_in[c.slot(RING)])

            landed(h1_stored, 32, 2)
            all_steps(pool, 0, NCH, gather_h1, peel=1 + UNROLL)

            def scatter(index, rows, c):
                pool.indirect_dma_start(out, bass.IndirectOffsetOnAxis(index, 0), rows, None, bounds_check=bound_of[N - 1],
                                        oob_is_err=False).then_inc(rows_scattered[c.slot(RING)], 16)

            def dense_landed(c):
                at = c.value(1, 0)
                stored = [pool.value_load(stored_by[0:1, q, bass.ds(at, 1)], min_val=16, max_val=16 * (ND + 1) // 2)
                          for q in range(2)]
                for q in range(2):
                    pool.wait_ge(out_stored[q], stored[q])
                pool.sem_inc(pool_cleared, 1)

            def scatter_held(c):
                if c.base % UNROLL == 0:
                    dense_landed(c.back(1 - UNROLL))
                pool.wait_ge(t_out_sb, c.done())
                for t in range(c.base * TC, (c.base + 1) * TC):
                    scatter(edges[:, SIDX, t:t + 1], held[:, t * H:(t + 1) * H], c)

            def scatter_staged(c):
                pool.wait_ge(rows_staged, c.back(HEAD).done())
                pool.sem_inc(pool_cleared, 1)
                for t in range(TC):
                    scatter(ix_out[:, c.slot(RING), t:t + 1], tiles(t_out[:, c.slot(RING)])[:, t], c)

            def scatter_next(c):
                if (c.base - HEAD) % UNROLL == 0:
                    dense_landed(c.back(1 - UNROLL))
                scatter_staged(c)

            pool.wait_ge(stored_by_ready, 1)
            written_out(pool, 0, HEAD, scatter_held)
            all_steps(pool, HEAD, NCH - UNROLL - HEAD, scatter_next, peel=UNROLL)
            landed(out_stored, 16, 2, ND)
            written_out(pool, NCH - UNROLL, UNROLL, scatter_staged)
            landed(rows_scattered, 16 * TC, RING)

        @block.tensor
        def _(pe):
            mm, tr = nc.tensor.matmul, nc.tensor.transpose
            pe.wait_ge(pool_consts, 2)
            pe.wait_ge(falls_ready, 1)
            tr(psE[0][:, 0:P], falls_lane[:, :], ident[:, :]).then_inc(falls_T, 1)
            pe.wait_ge(rowf_ready, 1)
            for kind in range(3):
                for a in range(2):
                    last = tr([psF[0], psF[1], psG[0]][kind][:, a * TA:(a + 1) * TA], rowf[:, kind, a], ident[0:TA, 0:TA])
            last.then_inc(edgesT, 1)
            pe.wait_ge(weights_in, 16 * 31)
            tr(psM[0][0:H, 0:H + 1], w_m2[:, :], ident[0:H + 1, 0:H + 1]).then_inc(w_m2T_ps, 1)
            pe.wait_ge(w_m2T_sb, 1)
            mm(psM[1][0:H + 1, 0:H], w_m2T[:, :], w_u1n[:, :], start=True, stop=True).then_inc(w_comb_ps, 1)
            pe.wait_ge(w_comb_sb, 1)
            pe.wait_ge(setup_dve, 1)
            pe.wait_ge(edges_ready, 1)

            def transposes(ps, rows, done, cols=BANK):
                for k in range(cols // P):
                    last = tr(ps[:, k * P:(k + 1) * P], rows[:, k * P:(k + 1) * P], ident[:, :])
                last.then_inc(done, 1)

            def add_bias(ps, which, cols=BANK):
                return mm(ps[:, 0:cols], pick[:, :], bias3[:, which, 0:cols], start=True, stop=False, skip_group_check=True)

            def rows_out(ps, pairs, done, cols=BANK):
                for k in range(cols // P):
                    for n, (lhsT, w) in enumerate(pairs):
                        last = mm(ps[:, k * P:(k + 1) * P], lhsT[:, k * P:(k + 1) * P], w, start=False,
                                  stop=(k == cols // P - 1 and n == len(pairs) - 1), skip_group_check=True)
                last.then_inc(done, 1)

            def f_in(s):
                pe.wait_ge(xd_in[s.slot(2)], s.done(0, 16, 2))
                pe.wait_ge(f_x1_sb, s.done(2))
                transposes(psF[s.slot(2)], xd[:, s.slot(2), 0:width(s)], f_xT_ps, width(s))

            def f_u(s):
                pe.wait_ge(f_xT_sb, s.done())
                mm(psF[s.slot(2)][:, 0:width(s)], bd_u1[:, :], f_xT[:, s.slot(2), 0:width(s)], start=True, stop=True).then_inc(f_u_ps, 1)

            def f_r(s):
                pe.wait_ge(f_U_sb, s.done())
                add_bias(psF[s.slot(2)], 0, width(s))
                rows_out(psF[s.slot(2)], [(f_U, bd_u2[:, :]), (f_xT[:, s.slot(2), 0:width(s)], bd_c[:, :])], f_r_ps, width(s))

            def f_yT(s):
                pe.wait_ge(f_y_sb, s.done())
                transposes(psF[s.slot(2)], f_y, f_yT_ps, width(s))

            def f_sc(s):
                pe.wait_ge(f_sT_sb, s.done())
                add_bias(psF[s.slot(2)], 1, width(s))
                rows_out(psF[s.slot(2)], [(f_sT, bd_c[:, :])], f_sc_ps, width(s))

            def g_in(s):
                pe.wait_ge(f_x1_sb, s.done())
                pe.wait_ge(g_r_sb, s.done(2))
                transposes(psG[s.slot(2)], f_x1[:, s.slot(2), 0:width(s)], g_xT_ps, width(s))

            def g_hp(s):
                pe.wait_ge(g_xT_sb, s.done())
                mm(psG[s.slot(2)][:, 0:width(s)], bd_s1[:, :], g_xT[:, 0:width(s)], start=True, stop=True).then_inc(g_h_ps, 1)

            def g_o(s):
                pe.wait_ge(g_h_sb, s.done())
                add_bias(psG[s.slot(2)], 3, width(s))
                rows_out(psG[s.slot(2)], [(g_h, bd_s2[:, :])], g_o_ps, width(s))

            def m_in(c):
                pe.wait_ge(er_in[c.slot(RING)], c.done(0, 16 * 2 * TC, RING))
                pe.wait_ge(ends_in[c.slot(2)], c.done(0, 32, 2))
                pe.wait_ge(n_x1_sb, c.done(2))
                pe.wait_ge(m_eaT_sb, c.done(2))
                ps, rows = psM[c.slot(2)], er[:, c.slot(RING)]
                tr(ps[:, 0:P], rows[:, 0:P], ident[:, :])
                tr(psE[c.slot(2)][0:TC * EF, 0:P], ea[:, c.slot(2)], ident[:, :])
                for k in range(1, 4):
                    last = tr(ps[:, k * P:(k + 1) * P], rows[:, k * P:(k + 1) * P], ident[:, :])
                last.then_inc(m_T_ps, 1)

            def m_hidden(c):
                pe.wait_ge(m_eaT_sb, c.done())
                pe.wait_ge(m_xT_sb, c.done())
                ps = psM[c.slot(2)]
                mm(ps[0:H, :], w_m1[:, :], m_xT[:, c.slot(2)], start=True, stop=False, skip_group_check=True)
                for t in range(TC):
                    last = mm(ps[0:H, t * P:(t + 1) * P], w_m1e[:, t], m_eaT[:, :], start=False, stop=(t == TC - 1),
                              skip_group_check=True)
                last.then_inc(m_hid_ps, 1)

            def m_u(c):
                pe.wait_ge(m_agg_sb, c.done())
                ps = psM[c.slot(2)]
                mm(ps[:, :], bd_u1[:, :], m_xT[:, c.slot(2)], start=True, stop=False)
                mm(ps[:, :], w_comb[:, :], m_agg[:, c.slot(2)], start=False, stop=True).then_inc(m_u_ps, 1)

            def n_r(c):
                pe.wait_ge(n_U_sb, c.done())
                add_bias(psM[c.slot(2)], 0)
                rows_out(psM[c.slot(2)], [(n_U, bd_u2[:, :]), (m_xT[:, c.slot(2)], bd_c[:, :])], n_r_ps)

            def n_yT(c):
                pe.wait_ge(n_y_sb, c.done())
                transposes(psM[c.slot(2)], n_y, n_yT_ps)

            def n_sc(c):
                pe.wait_ge(n_sT_sb, c.done())
                add_bias(psM[c.slot(2)], 1)
                rows_out(psM[c.slot(2)], [(n_sT, bd_c[:, :])], n_sc_ps)

            def q_in(c):
                pe.wait_ge(q_er_in[c.slot(RING)], c.done(0, 16 * TC, RING))
                pe.wait_ge(q_x1_in[c.slot(RING)], c.done(0, 16, RING))
                pe.wait_ge(q_T_sb, c.done(2))
                transposes(psM[c.slot(2)], er[:, c.slot(RING)], q_T_ps)

            def q_hidden(c):
                pe.wait_ge(q_T_sb, c.done())
                pe.wait_ge(q_mean_sb, c.done())
                pe.wait_ge(q_h_sb, c.done(2))
                add_bias(psE[c.slot(2)], 2)
                rows_out(psE[c.slot(2)], [(q_T, bd_s1[:, :]), (q_mean, w_n1[:, :])], q_h_ps)

            def t_in(c):
                pe.wait_ge(t_er_in[c.slot(RING)], c.done(0, 16 * TC, RING))
                pe.wait_ge(t_h1_in[c.slot(RING)], c.done(0, 32, RING))
                pe.wait_ge(t_T_sb, c.done(2))
                pe.wait_ge(t_agg_sb, c.done(2))
                transposes(psM[c.slot(2)], er[:, c.slot(RING)], t_T_ps)

            def t_o(c):
                pe.wait_ge(t_T_sb, c.done())
                pe.wait_ge(t_mean_sb, c.done())
                pe.wait_ge(t_r_sb, c.done(2))
                ps = psE[c.slot(2)]
                add_bias(ps, 3, TC * H)
                for k in range(TC):
                    last = mm(ps[:, k * H:(k + 1) * H], t_T[:, c.slot(2), k * P:(k + 1) * P], w_l2[:, :], start=False,
                              stop=(k == TC - 1), skip_group_check=True)
                last.then_inc(t_o_ps, 1)

            def phase1(s):
                dense(f_in, s)
                dense(g_in, s.back(2))
                dense(g_o, s.back(3))
                edge(n_yT, s.back(2))
                dense(g_hp, s.back(2))
                dense(f_u, s)
                dense(f_yT, s.back(1))
                edge(n_sc, s.back(2))
                dense(f_r, s)
                edge(m_u, s.back(1))
                edge(m_in, s)
                dense(f_sc, s.back(1))
                edge(n_r, s.back(1))
                edge(m_hidden, s)

            all_steps(pe, 0, NCH, phase1, peel=1 + UNROLL)
            written_out(pe, NCH, Q0 - NCH, phase1)

            def phase2(s):
                c = s.back(Q0)
                edge(q_hidden, c.back(2))
                dense(f_in, s)
                dense(g_in, s.back(2))
                dense(g_o, s.back(3))
                dense(f_yT, s.back(1))
                edge(q_in, c.back(1))
                dense(f_u, s)
                dense(f_sc, s.back(1))
                dense(g_hp, s.back(2))
                dense(f_r, s)

            def phase3(s):
                A, B = s.back(T0).pair()
                dense(g_o, s.back(3))
                edge(t_in, A)
                edge(t_in, B)
                dense(g_in, s.back(2))
                dense(f_in, s)
                dense(f_u, s)
                dense(g_hp, s.back(2))
                dense(f_yT, s.back(1))
                dense(f_r, s)
                edge(t_o, A)
                dense(f_sc, s.back(1))
                edge(t_o, B)

            all_steps(pe, Q0, NCH - UNROLL, phase2, peel=1 + UNROLL)
            written_out(pe, Q0 + NCH - UNROLL, UNROLL - 1, phase2)
            written_out(pe, NCH - 3, 1, q_hidden)
            written_out(pe, NCH - 2, 2, q_in)
            written_out(pe, NCH - 2, 2, q_hidden)

            written_out(pe, Q0 + NCH - 1, T0 - Q0 - NCH + 1, phase3)
            all_steps(pe, T0, LOOPED3, phase3, peel=1 + UNROLL)
            written_out(pe, T0 + LOOPED3, NPAIR - LOOPED3, phase3)
            written_out(pe, T0 + NPAIR, END - T0 - NPAIR, phase2)

        @block.scalar
        def _(act):
            A = nc.scalar.activation

            act.wait_ge(weights_in, 16 * 31)
            act.wait_ge(setup_dve, 1)

            def copy(into, ps, src_sem, done, s):
                act.wait_ge(src_sem, s.done())
                A(into, ps, ACT.Copy).then_inc(done, 1)

            def relu(into, ps, bias, src_sem, done, s):
                act.wait_ge(src_sem, s.done())
                A(into, ps, ACT.Relu, bias=bias).then_inc(done, 1)

            def square(into, of, src_sem, done, s):
                act.wait_ge(src_sem, s.done())
                A(into, of, ACT.Square).then_inc(done, 1)

            def std(into, var, src_sem, done, s):
                act.wait_ge(src_sem, s.done())
                A(into, var, ACT.Sqrt, bias=eps_c[:, :], scale=1.0 / H).then_inc(done, 1)

            def f_xT_copy(s):
                act.wait_ge(f_sT_sb, s.done(2))
                copy(f_xT[:, s.slot(2), 0:width(s)], psF[s.slot(2)][:, 0:width(s)], f_xT_ps, f_xT_sb, s)

            def f_relu(s):
                act.wait_ge(f_r_ps, s.done(1))
                relu(f_U[:, 0:width(s)], psF[s.slot(2)][:, 0:width(s)], bu1_c[:, :], f_u_ps, f_U_sb, s)

            def f_square1(s):
                act.wait_ge(f_var1, s.done(1))
                square(f_sq_a[:, 0:width(s)], psF[s.slot(2)][:, 0:width(s)], f_r_ps, f_sq1, s)

            def f_square2(s):
                act.wait_ge(f_var2, s.done(1))
                square(f_sq_b[:, 0:width(s)], psF[s.slot(2)][:, 0:width(s)], f_sc_ps, f_sq2, s)

            f_root1 = lambda s: std(f_std[:, 0, 0:width(s) // H], f_var[:, 0, 0:width(s) // H], f_var1, f_std1, s)
            f_root2 = lambda s: std(f_std[:, 1, 0:width(s) // H], f_var[:, 1, 0:width(s) // H], f_var2, f_std2, s)

            def g_xT_copy(s):
                act.wait_ge(g_h_ps, s.done(1))
                copy(g_xT[:, 0:width(s)], psG[s.slot(2)][:, 0:width(s)], g_xT_ps, g_xT_sb, s)

            def g_relu(s):
                act.wait_ge(g_o_ps, s.done(1))
                relu(g_h[:, 0:width(s)], psG[s.slot(2)][:, 0:width(s)], b1_c[:, :], g_h_ps, g_h_sb, s)

            def g_square(s):
                act.wait_ge(g_var_sb, s.done(1))
                square(g_sq[:, 0:width(s)], g_r[:, 0:width(s)], g_r_sb, g_sq_sb, s)

            g_root = lambda s: std(g_std[:, 0:width(s) // H], g_var[:, 0:width(s) // H], g_var_sb, g_std_sb, s)

            def m_xT_copy(c):
                act.wait_ge(n_sT_sb, c.done(2))
                copy(m_xT[:, c.slot(2)], psM[c.slot(2)][:, :], m_T_ps, m_xT_sb, c)

            def m_relu(c):
                act.wait_ge(m_agg_sb, c.done(1))
                relu(m_hid[0:H, :], psM[c.slot(2)][0:H, :], bm1_c[:, :], m_hid_ps, m_hid_sb, c)

            def n_relu(c):
                act.wait_ge(n_r_ps, c.done(1))
                relu(n_U[:, :], psM[c.slot(2)][:, :], bu1_c[:, :], m_u_ps, n_U_sb, c)

            def n_square1(c):
                act.wait_ge(n_var1, c.done(1))
                square(n_sq_a[:, :], psM[c.slot(2)][:, :], n_r_ps, n_sq1, c)

            def n_square2(c):
                act.wait_ge(n_var2, c.done(1))
                square(n_sq_b[:, :], psM[c.slot(2)][:, :], n_sc_ps, n_sq2, c)

            n_root1 = lambda c: std(n_std[:, 0], n_var[:, 0], n_var1, n_std1, c)
            n_root2 = lambda c: std(n_std[:, 1], n_var[:, 1], n_var2, n_std2, c)

            def phase1(s):
                dense(g_xT_copy, s.back(2))
                edge(m_relu, s.back(1))
                dense(f_xT_copy, s)
                dense(f_relu, s)
                edge(n_square2, s.back(2))
                dense(g_square, s.back(3))
                edge(n_root2, s.back(2))
                dense(g_root, s.back(3))
                edge(n_relu, s.back(1))
                dense(f_square1, s)
                dense(f_square2, s.back(1))
                dense(g_relu, s.back(2))
                edge(m_xT_copy, s)
                dense(f_root2, s.back(1))
                dense(f_root1, s)
                edge(n_square1, s.back(1))
                edge(n_root1, s.back(1))

            all_steps(act, 0, NCH, phase1, peel=1 + UNROLL)
            written_out(act, NCH, Q0 - NCH, phase1)

            def q_T_copy(c):
                act.wait_ge(q_h_ps, c.done(1))
                act.wait_ge(q_agg_sb, c.done(1))
                copy(q_T[:, :], psM[c.slot(2)][:, :], q_T_ps, q_T_sb, c)

            def q_relu(c):
                act.wait_ge(h1_stored[c.slot(2)], c.done(2, 32, 2))
                act.wait_ge(q_h_ps, c.done())
                A(q_h[:, c.slot(2)], psE[c.slot(2)][:, :], ACT.Relu).then_inc(q_h_sb, 1)

            def phase2(s):
                c = s.back(Q0)
                dense(g_xT_copy, s.back(2))
                dense(f_xT_copy, s)
                edge(q_relu, c.back(2))
                edge(q_T_copy, c.back(1))
                dense(g_square, s.back(3))
                dense(f_relu, s)
                dense(f_square2, s.back(1))
                dense(g_relu, s.back(2))
                dense(f_root2, s.back(1))
                dense(f_square1, s)
                dense(g_root, s.back(3))
                dense(f_root1, s)

            def t_T_copy(c):
                act.wait_ge(t_o_ps, c.done(2))
                copy(t_T[H:P, c.slot(2)], psM[c.slot(2)][H:P, :], t_T_ps, t_T_sb, c)

            def t_square(c):
                act.wait_ge(t_var_sb, c.done(2))
                square(t_sq[:, c.slot(2)], t_r[:, c.slot(2)], t_r_sb, t_sq_sb, c)

            t_root = lambda c: std(t_std[:, c.slot(2)], t_var[:, c.slot(2)], t_var_sb, t_std_sb, c)

            def phase3(s):
                A, B = s.back(T0).pair()
                edge(t_T_copy, A)
                dense(f_xT_copy, s)
                dense(g_xT_copy, s.back(2))
                edge(t_T_copy, B)
                dense(f_relu, s)
                dense(g_relu, s.back(2))
                dense(g_square, s.back(3))
                dense(f_square1, s)
                dense(f_square2, s.back(1))
                edge(t_square, A)
                dense(f_root1, s)
                dense(g_root, s.back(3))
                edge(t_square, B)
                dense(f_root2, s.back(1))
                edge(t_root, A)
                edge(t_root, B)

            all_steps(act, Q0, NCH - UNROLL, phase2, peel=1 + UNROLL)
            written_out(act, Q0 + NCH - UNROLL, UNROLL - 1, phase2)
            written_out(act, NCH - 3, 1, q_relu)
            written_out(act, NCH - 2, 2, q_T_copy)
            written_out(act, NCH - 2, 2, q_relu)

            written_out(act, Q0 + NCH - 1, T0 - Q0 - NCH + 1, phase3)
            all_steps(act, T0, LOOPED3, phase3, peel=1 + UNROLL)
            written_out(act, T0 + LOOPED3, NPAIR - LOOPED3, phase3)
            written_out(act, T0 + NPAIR, END - T0 - NPAIR, phase2)

        @block.vector
        def _(dve):
            V = nc.vector
            local = [0]

            def after(ins):
                local[0] += 1
                ins.then_inc(zeroed, 1)
                dve.wait_ge(zeroed, local[0])

            for w in (bd_c, bd_u1, bd_u2, bd_s1, bd_s2, w_m1e, w_comb, w_n1, pick, falls_lane):
                V.memset(w[:], 0.0)
            V.memset(edges[:, 0:3, :], 0)
            V.memset(rows2[:, :], 0)
            V.memset(eps_c[:, :], EPS)
            V.memset(m_hid[H:H + 1, :], 1.0)
            after(V.memset(cmean[:, :], 0.0))
            V.memset(fill[:, 0:EF], 0).then_inc(pads_ready, 1)
            for lo in (0, H):
                V.memset(bd_c[lo:lo + H, lo:lo + H], -1.0 / H)
            for lo in (0, 32):
                V.memset(pick[lo:lo + 1, :], 1.0)
            after(V.memset(pick[64:65, :], 1.0))
            dve.wait_ge(pairs_in, 64)
            after(V.tensor_tensor(falls[:, :], pair_a[:, :], pair_b[:, :], ALU.is_gt))
            V.tensor_reduce(falls_lane[0:OP, 0:1], falls[:, :], AX_X, ALU.max).then_inc(falls_ready, 1)
            dve.wait_ge(falls_T, 1)
            after(V.tensor_reduce(falls_any[:, :], psE[0][0:1, 0:P], AX_X, ALU.max))
            V.tensor_copy(falls_flag[:, :], falls_any[:, :]).then_inc(flag_ready, 1)
            dve.wait_ge(pool_consts, 3)
            V.tensor_tensor(bd_c[:, :], bd_c[:, :], ident[:, :], ALU.add)

            dve.wait_ge(raw_in, 80)
            rd = lambda n: raw[:, n].rearrange("q a p -> q (a p)")
            rf = lambda n: rowf[:, n].rearrange("q a p -> q (a p)")
            V.tensor_copy(rf(0), rd(0))
            V.tensor_scalar(rf(1), rd(1), 0.0, None, ALU.max)
            V.tensor_tensor(rf(3), rd(1), rd(2), ALU.is_equal)
            nl = notlast[:, :, :].rearrange("q a p -> q (a p)")
            after(V.tensor_tensor(nl, rd(1), rd(3), ALU.is_equal))
            V.scalar_tensor_tensor(rf(2), nl, float(NOWHERE), rd(1), ALU.mult, ALU.add).then_inc(rowf_ready, 1)
            dve.wait_ge(edgesT, 1)
            for kind, ps in ((SRC, psF[0]), (DSTG, psF[1]), (SIDX, psG[0])):
                last = V.tensor_copy(edges[:, kind, 0:NT], ps[:, 0:NT])
            last.then_inc(edges_ready, 1)
            dve.wait_ge(edges_ready, 1)

            def stage1(c):
                if c.k is not None or c.base >= RING:
                    dve.wait_ge(er_in[c.slot(RING)], c.done(RING, 16 * 2 * TC, RING))
                    dve.wait_ge(rows_set[c.slot(RING)], c.done(RING, 16 * TC, RING))
                V.tensor_copy(ix1[:, c.slot(RING)], edges[:, :, bass.ds(c.value(TC, 0), TC)]).then_inc(ix1_ready, 1)

            stage1(Step(dve, None, 0, {}))
            stage1(Step(dve, None, 1, {}))

            after(V.tensor_scalar(last_chunk[:, :], last_dst[:, :], 0.5 / DC, (OVER + 0.25) * 0.5 / DC + 0.5, ALU.mult, ALU.add))
            after(V.tensor_scalar(last_narrow[:, :], last_dst[:, :], 0.5 / DC3, (OVER + 0.25 - T0 * (DC - DC3)) * 0.5 / DC3 + 0.5,
                                  ALU.mult, ALU.add))
            after(V.tensor_tensor(last_chunk[:, :], last_chunk[:, :], last_narrow[:, :], ALU.max))
            after(V.tensor_scalar(pairs_below[:, :], last_chunk[:, :], float((ND - 1) // 2), 1.0, ALU.min, ALU.max))
            V.tensor_scalar(stored_by[:, 0], pairs_below[:, :], 16.0, 16.0, ALU.mult, ALU.add)
            V.tensor_scalar(stored_by[:, 1], pairs_below[:, :], 16.0, None, ALU.mult).then_inc(stored_by_ready, 1)

            dve.wait_ge(pads_in, 64)
            V.memset(fill[:, :], -1).then_inc(fill_ready, 1)

            dve.wait_ge(weights_in, 16 * 31)
            dve.wait_ge(w_m2T_ps, 1)
            V.tensor_copy(w_m2T[:, :], psM[0][0:H, 0:H + 1]).then_inc(w_m2T_sb, 1)
            dve.wait_ge(w_comb_ps, 1)
            V.tensor_copy(w_comb[:, H:P], psM[1][0:H + 1, 0:H]).then_inc(w_comb_sb, 1)
            after(V.tensor_reduce(cmean[:, :], cen[:, :, :], AX_X, ALU.add))
            after(V.scalar_tensor_tensor(cen[:, :, :], cmean[:, :].unsqueeze(2).to_broadcast([P, 6, H]), -1.0 / H,
                                         cen[:, :, :], ALU.mult, ALU.add))
            for lo in (0, H):
                V.tensor_copy(bd_u2[lo:lo + H, lo:lo + H], cen[lo:lo + H, 0])
                V.tensor_copy(bd_s2[lo:lo + H, lo:lo + H], cen[lo:lo + H, 1])
            V.tensor_copy(w_l2[:, :], cen[:, 2])
            V.tensor_copy(brow[:, 0:2], cen[0:96, 3:5])
            after(V.tensor_copy(brow[:, 3], cen[0:96, 5]))
            after(V.tensor_copy(bpart[:, :, :], brow[:, :, :]))
            after(V.tensor_tensor(brest[:, :, :], brow[:, :, :], bpart[:, :, :], ALU.subtract))
            after(V.tensor_copy(bmid[:, :, :], brest[:, :, :]))
            after(V.tensor_copy(bpart[32:64, :, :], bmid[32:64, :, :]))
            after(V.tensor_tensor(brest[:, :, :], brest[:, :, :], bmid[:, :, :], ALU.subtract))
            after(V.tensor_copy(bpart[64:96, :, :], brest[64:96, :, :]))
            for t in range(8):
                last = V.tensor_copy(bias3[:, :, t * H:(t + 1) * H], bpart[:, :, :])
            last.then_inc(setup_dve, 1)
            dve.wait_ge(setup_dve, 1)

            def variance(into, sq, n, sq_sem, done, s):
                dve.wait_ge(sq_sem, s.done())
                V.tensor_reduce(into, tiles(sq), AX_X, ALU.add).then_inc(done, 1)

            def reciprocal(into, of, std_sem, done, s):
                dve.wait_ge(std_sem, s.done())
                V.reciprocal(into, of).then_inc(done, 1)

            def scaled(into, of, rstd, n, rstd_sem, done, s):
                dve.wait_ge(rstd_sem, s.done())
                V.tensor_tensor(tiles(into), tiles(of), per_row(rstd, n), ALU.mult).then_inc(done, 1)

            def turned_sum(into, yT, xT, src_sem, done, s):
                dve.wait_ge(src_sem, s.done())
                V.scalar_tensor_tensor(into, yT, gam_c[:, :], xT, ALU.mult, ALU.add).then_inc(done, 1)

            def plus(into, a, b, src_sem, done, s):
                dve.wait_ge(src_sem, s.done())
                V.tensor_tensor(into, a, b, ALU.add).then_inc(done, 1)

            f_variance1 = lambda s: variance(f_var[:, 0, 0:width(s) // H], f_sq_a[:, 0:width(s)], width(s) // H, f_sq1, f_var1, s)
            f_variance2 = lambda s: variance(f_var[:, 1, 0:width(s) // H], f_sq_b[:, 0:width(s)], width(s) // H, f_sq2, f_var2, s)
            f_recip1 = lambda s: reciprocal(f_rstd[:, 0, 0:width(s) // H], f_std[:, 0, 0:width(s) // H], f_std1, f_rstd1, s)
            f_recip2 = lambda s: reciprocal(f_rstd[:, 1, 0:width(s) // H], f_std[:, 1, 0:width(s) // H], f_std2, f_rstd2, s)

            def f_scale(s):
                dve.wait_ge(f_yT_ps, s.done(1))
                scaled(f_y[:, 0:width(s)], psF[s.slot(2)][:, 0:width(s)], f_rstd[:, 0, 0:width(s) // H], width(s) // H, f_rstd1, f_y_sb, s)

            def f_sum(s):
                dve.wait_ge(f_sc_ps, s.done(1))
                turned_sum(f_sT[:, 0:width(s)], psF[s.slot(2)][:, 0:width(s)], f_xT[:, s.slot(2), 0:width(s)], f_yT_ps, f_sT_sb, s)

            def f_x1_rows(s):
                dve.wait_ge(g_xT_ps, s.done(2))
                dve.wait_ge(g_r_sb, s.done(2))
                scaled(f_x1[:, s.slot(2), 0:width(s)], psF[s.slot(2)][:, 0:width(s)], f_rstd[:, 1, 0:width(s) // H], width(s) // H, f_rstd2, f_x1_sb, s)

            def g_sum(s):
                dve.wait_ge(g_out_sb, s.done(1))
                plus(g_r[:, 0:width(s)], psG[s.slot(2)][:, 0:width(s)], f_x1[:, s.slot(2), 0:width(s)], g_o_ps, g_r_sb, s)

            g_variance = lambda s: variance(g_var[:, 0:width(s) // H], g_sq[:, 0:width(s)], width(s) // H, g_sq_sb, g_var_sb, s)
            g_recip = lambda s: reciprocal(g_rstd[:, 0:width(s) // H], g_std[:, 0:width(s) // H], g_std_sb, g_rstd_sb, s)

            def g_scale(s):
                dve.wait_ge(out_stored[s.slot(2)], s.done(2, 16, 2))
                scaled(g_out[:, s.slot(2), 0:width(s)], g_r[:, 0:width(s)], g_rstd[:, 0:width(s) // H], width(s) // H, g_rstd_sb, g_out_sb, s)

            def m_ea(c):
                dve.wait_ge(m_T_ps, c.done())
                dve.wait_ge(m_hid_ps, c.done(1))
                V.tensor_copy(m_eaT[:, :], psE[c.slot(2)][0:TC * EF, 0:P]).then_inc(m_eaT_sb, 1)

            def scan(rows, c, data, done):
                first = c.k is None and c.base == 0
                carry = 0.0 if first else m_agg[0:rows, 1 - c.slot(2), EC - 1:EC]
                dve.wait_ge(done, c.done(1))
                V.tensor_tensor_scan(m_agg[0:rows, c.slot(2)], same[0:rows, c.slot(2)], data, carry, ALU.mult,
                                     ALU.add).then_inc(done, 1)

            def m_scan(c):
                dve.wait_ge(ends_in[c.slot(2)], c.done(0, 32, 2))
                dve.wait_ge(m_u_ps, c.done(2))
                dve.wait_ge(count_stored[c.slot(2)], c.done(2, 16, 2))
                dve.wait_ge(m_hid_sb, c.done())
                scan(H + 1, c, m_hid[:, :], m_agg_sb)

            n_variance1 = lambda c: variance(n_var[:, 0], n_sq_a[:, :], 8, n_sq1, n_var1, c)
            n_variance2 = lambda c: variance(n_var[:, 1], n_sq_b[:, :], 8, n_sq2, n_var2, c)
            n_recip1 = lambda c: reciprocal(n_rstd[:, 0], n_std[:, 0], n_std1, n_rstd1, c)
            n_recip2 = lambda c: reciprocal(n_rstd[:, 1], n_std[:, 1], n_std2, n_rstd2, c)

            def n_scale(c):
                dve.wait_ge(n_yT_ps, c.done(1))
                scaled(n_y[:, :], psM[c.slot(2)][:, :], n_rstd[:, 0], 8, n_rstd1, n_y_sb, c)

            def n_sum(c):
                dve.wait_ge(n_sc_ps, c.done(1))
                turned_sum(n_sT[:, :], psM[c.slot(2)][:, :], m_xT[:, c.slot(2)], n_yT_ps, n_sT_sb, c)

            def n_x1_rows(c):
                dve.wait_ge(x1_stored[c.slot(2)], c.done(2, 32, 2))
                scaled(n_x1[:, c.slot(2)], psM[c.slot(2)][:, :], n_rstd[:, 1], 8, n_rstd2, n_x1_sb, c)

            def phase1(s):
                dense(f_scale, s.back(1))
                edge(n_sum, s.back(2))
                dense(f_sum, s.back(1))
                edge(m_scan, s.back(1))
                dense(g_sum, s.back(3))
                edge(n_variance2, s.back(2))
                edge(n_recip2, s.back(2))
                edge(n_x1_rows, s.back(2))
                dense(g_variance, s.back(3))
                dense(g_recip, s.back(3))
                dense(f_variance1, s)
                edge(m_ea, s)
                edge(stage1, s.back(-2))
                dense(f_variance2, s.back(1))
                dense(f_recip2, s.back(1))
                dense(f_x1_rows, s.back(1))
                edge(n_variance1, s.back(1))
                dense(f_recip1, s)
                edge(n_recip1, s.back(1))
                edge(n_scale, s.back(1))
                dense(g_scale, s.back(3))

            all_steps(dve, 0, NCH, phase1, peel=1 + UNROLL)

            def stage2(c):
                if c.k is not None or c.base >= RING:
                    dve.wait_ge(slots_in[c.slot(RING)], c.done(RING, 16 * TC, RING))
                V.tensor_copy(ix2[:, c.slot(RING)], edges[:, :, bass.ds(c.value(TC, 0), TC)]).then_inc(ix2_ready, 1)

            def look(c):
                dve.wait_ge(slots_in[c.slot(RING)], c.done(0, 16 * TC, RING))
                V.tensor_scalar(absent[:, :], slots[:, c.slot(RING)], 0.0, None, ALU.is_lt).then_inc(absent_sb, 1)
                dve.wait_ge(absent_sb, c.done())
                V.scalar_tensor_tensor(away[:, :], ix2[:, c.slot(RING), ENUM], float(EP + 1), absent[:, :],
                                       ALU.add, ALU.mult).then_inc(away_sb, 1)
                at = c.value(TC, 0)
                dve.wait_ge(away_sb, c.done())
                V.tensor_tensor(rows2[:, bass.ds(at, TC)], away[:, :], slots[:, c.slot(RING)], ALU.add).then_inc(rows_found, 1)

            def stage_x1(c):
                dve.wait_ge(rows_found, c.done())
                if c.k is not None or c.base >= RING:
                    dve.wait_ge(q_er_in[c.slot(RING)], c.done(RING, 16 * TC, RING))
                dve.sem_inc(dve_cleared, 1)
                V.tensor_copy(rowix[:, c.slot(RING)], rows2[:, bass.ds(c.value(TC, 0), TC)]).then_inc(rowix_ready, 1)

            def q_scan(c):
                dve.wait_ge(q_T_sb, c.done())
                dve.wait_ge(q_line_in[c.slot(2)], c.done(0, 32, 2))
                dve.wait_ge(q_mean_sb, c.done(2))
                scan(H, c, q_T[0:H, :], q_agg_sb)

            def mean(into, c, agg_sem, done):
                dve.wait_ge(agg_sem, c.done())
                V.tensor_tensor(into, m_agg[0:H, c.slot(2)], inv[:, c.slot(2)], ALU.mult).then_inc(done, 1)

            def q_average(c):
                dve.wait_ge(q_h_ps, c.done(1))
                mean(q_mean[:, :], c, q_agg_sb, q_mean_sb)

            written_out(dve, 0, 3, stage2)

            def between(s):
                phase1(s)
                c = s.back(Q0)
                edge(look, c.back(-3))
                edge(stage_x1, c.back(-2))
                edge(stage2, c.back(-6))

            written_out(dve, NCH, Q0 - NCH, between)
            dve.wait_ge(counts_in, 16)
            V.reciprocal(counts[:, :], counts[:, :]).then_inc(counts_inv, 1)

            def phase2(s):
                c = s.back(Q0)
                dense(f_scale, s.back(1))
                edge(look, c.back(-3))
                edge(stage_x1, c.back(-2))
                dense(f_sum, s.back(1))
                dense(g_sum, s.back(3))
                edge(q_scan, c.back(1))
                edge(q_average, c.back(1))
                dense(f_variance2, s.back(1))
                dense(f_recip2, s.back(1))
                dense(f_x1_rows, s.back(1))
                edge(stage2, c.back(-6))
                dense(g_variance, s.back(3))
                dense(f_variance1, s)
                dense(g_recip, s.back(3))
                dense(f_recip1, s)
                dense(g_scale, s.back(3))

            def ahead(stage, c):
                if c.k is not None or c.base >= RING:
                    edge(stage, c)

            def stage_h1(c):
                if c.k is not None or c.base >= RING:
                    dve.wait_ge(t_er_in[c.slot(RING)], c.done(RING, 16 * TC, RING))
                V.tensor_copy(ix_h1[:, c.slot(RING)], rows2[:, bass.ds(c.value(TC, 0), TC)]).then_inc(ix_h1_ready, 1)

            def stage_out(c):
                dve.wait_ge(rows_scattered[c.slot(RING)], c.done(RING, 16 * TC, RING))
                V.tensor_copy(ix_out[:, c.slot(RING)], edges[:, SIDX, bass.ds(c.value(TC, 0), TC)])
                V.tensor_copy(t_out[:, c.slot(RING)], held[:, bass.ds(c.value(TC * H, 0), TC * H)]).then_inc(rows_staged, 1)

            def t_scan(c):
                dve.wait_ge(t_T_ps, c.done())
                dve.wait_ge(t_line_in[c.slot(2)], c.done(0, 32, 2))
                dve.wait_ge(t_mean_sb, c.done(2))
                scan(H, c, psM[c.slot(2)][0:H, :], t_agg_sb)

            def t_average(c):
                dve.wait_ge(t_o_ps, c.done(2))
                mean(t_T[0:H, c.slot(2)], c, t_agg_sb, t_mean_sb)

            def t_sum(c):
                dve.wait_ge(t_out_sb, c.done(2))
                dve.wait_ge(t_h1_in[c.slot(RING)], c.done(0, 32, RING))
                plus(t_r[:, c.slot(2)], psE[c.slot(2)][:, 0:TC * H], t_x1[:, c.slot(RING)], t_o_ps, t_r_sb, c)

            t_variance = lambda c: variance(t_var[:, c.slot(2)], t_sq[:, c.slot(2)], TC, t_sq_sb, t_var_sb, c)
            t_recip = lambda c: reciprocal(t_rstd[:, c.slot(2)], t_std[:, c.slot(2)], t_std_sb, t_rstd_sb, c)

            def t_scale(c):
                at = c.value(TC * H, 0)
                scaled(held[:, bass.ds(at, TC * H)], t_r[:, c.slot(2)], t_rstd[:, c.slot(2)], TC, t_rstd_sb, t_out_sb, c)


            def phase3(s):
                A, B = s.back(T0).pair()
                edge(t_scan, A)
                ahead(stage_h1, A.back(-RING))
                dense(f_scale, s.back(1))
                dense(g_sum, s.back(3))
                edge(t_scan, B)
                ahead(stage_h1, B.back(-RING))
                edge(t_average, A)
                dense(f_sum, s.back(1))
                edge(t_average, B)
                dense(f_variance1, s)
                edge(t_sum, A)
                dense(g_variance, s.back(3))
                edge(t_sum, B)
                dense(f_variance2, s.back(1))
                edge(t_variance, A)
                dense(g_recip, s.back(3))
                dense(f_recip2, s.back(1))
                edge(t_variance, B)
                dense(f_x1_rows, s.back(1))
                edge(t_recip, A)
                edge(t_recip, B)
                dense(f_recip1, s)
                edge(t_scale, A)
                edge(t_scale, B)
                dense(g_scale, s.back(3))

            all_steps(dve, Q0, NCH - 2 * UNROLL, phase2, peel=1 + UNROLL)
            written_out(dve, Q0 + NCH - 2 * UNROLL, 2 * UNROLL - 1, phase2)
            for i in range(2, 0, -1):
                written_out(dve, NCH - i, 1, q_scan)
                written_out(dve, NCH - i, 1, q_average)
            written_out(dve, 0, RING, stage_h1)

            written_out(dve, Q0 + NCH - 1, T0 - Q0 - NCH + 1, phase3)
            all_steps(dve, T0, LOOPED3, phase3, peel=1 + UNROLL)
            written_out(dve, T0 + LOOPED3, NPAIR - LOOPED3, phase3)
            written_out(dve, T0 + NPAIR, END - T0 - NPAIR, phase2)
            all_steps(dve, HEAD, NCH - HEAD, stage_out, peel=UNROLL)


_INS = ["x", "src", "dst", "edge_attr_16", "L0_gnn_W_m1", "L0_gnn_b_m1", "L0_gnn_W_m2", "L0_gnn_b_m2", "L0_gnn_W_u1",
        "L0_gnn_b_u1", "L0_gnn_W_u2", "L0_gnn_b_u2", "L0_gnn_gamma", "L0_gnn_beta", "L1_gnn_W_self1",
        "L1_gnn_W_neigh1", "L1_gnn_b1", "L1_gnn_W_self2", "L1_gnn_W_neigh2", "L1_gnn_b2"]


def kernel(**inputs):
    import numpy as np
    import concourse.bacc as bacc
    from concourse import mybir as mb
    from concourse.bass_utils import run_bass_kernel_spmd

    nc = bacc.Bacc("TRN2", target_bir_lowering=False, num_devices=1)
    arrays, args = {}, []
    for name in _INS:
        a = np.ascontiguousarray(inputs[name])
        arrays[f"in_{name}"] = a
        args.append(nc.dram_tensor(f"in_{name}", a.shape, mb.dt.from_np(a.dtype), kind="ExternalInput").ap())
    rows, cols = inputs["x"].shape
    out = nc.dram_tensor("out_rows", (rows, cols), mb.dt.float32, kind="ExternalOutput").ap()
    build_gnn(nc, *args, out)
    r = run_bass_kernel_spmd(nc, [arrays], core_ids=[0])
    return r.results[0]["out_rows"]
```
